# Optimizing a Trainium2 kernel written in Bass

```python
import numpy as np
import jax
import jax.numpy as jnp

def _softmax(x, axis=-1):
    return jax.nn.softmax(x, axis=axis)

def _gelu(x):
    return jax.nn.gelu(x, approximate=True)

def _silu(x):
    return jax.nn.silu(x)

def _sigmoid(x):
    return jax.nn.sigmoid(x)

def _layernorm(x, axis=-1, eps=1e-05):
    m = jnp.mean(x, axis=axis, keepdims=True)
    v = jnp.var(x, axis=axis, keepdims=True)
    return (x - m) / jnp.sqrt(v + eps)

def _scatter_add(tgt, idx, src, axis=0):
    return tgt.at[idx].add(src)

def _segment_sum(src, seg, n):
    return jax.ops.segment_sum(src, seg, n)
kernel_name = 'mk_early_fusion_embed_d2_tok_img768_r4_28ceae'

def setup_inputs(seed: int=0):
    np.random.seed(seed)
    _w = jnp.asarray

    def _rec_inputs():
        import jax
        import jax.numpy as jnp
        _rk = jax.random.key(seed)
        x = -4.65018e-05 + 0.999886 * jax.random.normal(jax.random.fold_in(_rk, 1), (32, 3, 96, 96), jnp.float32)
        x_txt = jax.random.randint(jax.random.fold_in(_rk, 51), (32, 128), 0, 31999, jnp.int32)
        mask_BS_i2_0 = jnp.where(jnp.ones((32, 128), dtype=bool), 2, 0).astype(jnp.int32)
        return (x, x_txt, mask_BS_i2_0)
    x, x_txt, mask_BS_i2_0 = _rec_inputs()

    def _L0_tok_setup():
        import jax, jax.numpy as jnp
        import numpy as np
        PATCH = 16
        key = jax.random.key(seed)
        ks = jax.random.split(key, 5)
        bs, C, H, W = (64, 3, 128, 128)
        R, E, P2 = (5, 192, PATCH * PATCH)
        x = jax.random.normal(ks[0], (bs, C, H, W), dtype=jnp.float32)
        W_repr = jax.random.normal(ks[1], (R, C), dtype=jnp.float32) * (1.0 / np.sqrt(C))
        b_repr = jax.random.normal(ks[2], (R,), dtype=jnp.float32) * 0.02
        W_proj = jax.random.normal(ks[3], (R, E, P2), dtype=jnp.float32) * (1.0 / np.sqrt(P2))
        b_proj = jax.random.normal(ks[4], (R, E), dtype=jnp.float32) * 0.02
        return {'x': x, 'W_repr': W_repr, 'b_repr': b_repr, 'W_proj': W_proj, 'b_proj': b_proj}
    _L0_tok_all = _L0_tok_setup()
    _L0_tok_in = {k: v for k, v in _L0_tok_all.items() if k in ('W_repr', 'b_repr', 'W_proj', 'b_proj')}
    del _L0_tok_all

    def _L0_txt_setup():
        import jax, jax.numpy as jnp
        import numpy as np
        VOCAB = 8000
        DIM = 192
        BATCH = 8
        SEQ = 512

        def _sinusoidal_pos(seq_len, dim):
            pos = jnp.arange(seq_len, dtype=jnp.float32)[:, None]
            ids = jnp.arange(dim, dtype=jnp.float32)[None, :]
            even_exp = jnp.floor(ids / 2.0) * 2.0 / dim
            angle = pos / jnp.power(10000.0, even_exp)
            return jnp.where(jnp.arange(dim) % 2 == 0, jnp.sin(angle), jnp.cos(angle))
        key = jax.random.key(seed)
        k1, k2, k3, k4 = jax.random.split(key, 4)
        input_tensor = jax.random.randint(k1, (BATCH, SEQ), 0, VOCAB)
        segment_label = jax.random.randint(k2, (BATCH, SEQ), 0, 3)
        token_table = jax.random.normal(k3, (VOCAB, DIM), dtype=jnp.float32) * 0.02
        segm_table = jax.random.normal(k4, (3, DIM), dtype=jnp.float32) * 0.02
        token_table = token_table.at[0].set(0.0)
        segm_table = segm_table.at[0].set(0.0)
        return {'input_tensor': input_tensor, 'segment_label': segment_label, 'token_table': token_table, 'segm_table': segm_table}
    _L0_txt_all = _L0_txt_setup()
    _L0_txt_in = {k: v for k, v in _L0_txt_all.items() if k in ('token_table', 'segm_table')}
    del _L0_txt_all

    def _L0_attn_setup():
        import jax, jax.numpy as jnp
        import numpy as np
        NH = 12
        LEVEL = 4

        def _build_sets(T, Lmin):
            l_list, r_list = ([], [])
            L = Lmin
            while L <= T:
                for i in range(T // L):
                    l_list.append(i * L)
                    r_list.append((i + 1) * L - 1)
                L *= 2
            return (np.asarray(l_list, np.int32), np.asarray(r_list, np.int32))

        def _get_slice(x_cum, l_idx, r_idx):
            r = x_cum[:, :, r_idx, :]
            l = x_cum[:, :, np.maximum(np.asarray(l_idx) - 1, 0), :]
            mask = (np.asarray(l_idx) >= 1).astype(x_cum.dtype)[None, None, :, None]
            return r - l * mask

        def _get_slice_dyn(x_cum, l_idx, r_idx):
            r = x_cum[:, :, r_idx, :]
            l = x_cum[:, :, jnp.maximum(l_idx - 1, 0), :]
            mask = (l_idx >= 1).astype(x_cum.dtype)[None, None, :, None]
            return r - l * mask
        key = jax.random.key(seed)
        k0, k1, k2, k3 = jax.random.split(key, 4)
        B, T, C = (8, 512, 192)
        hs = C // NH
        s = 0.02
        return {'x': jax.random.normal(k0, (B, T, C), jnp.float32), 'Wqkv': jax.random.normal(k1, (3 * C, C), jnp.float32) * s, 'Wproj': jax.random.normal(k2, (C, C), jnp.float32) * s, 'Wv': jax.random.normal(k3, (hs, hs * hs), jnp.float32) * s, 'bv': jnp.zeros((hs,), jnp.float32)}
    _L0_attn_all = _L0_attn_setup()
    _L0_attn_in = {k: v for k, v in _L0_attn_all.items() if k in ('Wqkv', 'Wproj', 'Wv', 'bv')}
    del _L0_attn_all

    def _L0_ffn_setup():
        import jax, jax.numpy as jnp
        import numpy as np
        B, SEQ, D = (2, 256, 192)
        E, H = (8, 768)
        CAPACITY = 2
        key = jax.random.key(seed)
        ks = jax.random.split(key, 6)
        x = jax.random.normal(ks[0], (B, SEQ, D), dtype=jnp.float32)
        gate_weight = jax.random.normal(ks[1], (E, D), dtype=jnp.float32) * 0.006
        w1 = jax.random.normal(ks[2], (E, D, H), dtype=jnp.float32) * (1.0 / np.sqrt(D))
        b1 = jnp.zeros((E, H), dtype=jnp.float32)
        w2 = jax.random.normal(ks[3], (E, H, D), dtype=jnp.float32) * (1.0 / np.sqrt(H))
        b2 = jnp.zeros((E, D), dtype=jnp.float32)
        return {'x': x, 'gate_weight': gate_weight, 'w1': w1, 'b1': b1, 'w2': w2, 'b2': b2}
    _L0_ffn_all = _L0_ffn_setup()
    _L0_ffn_in = {k: v for k, v in _L0_ffn_all.items() if k in ('gate_weight', 'w1', 'b1', 'w2', 'b2')}
    del _L0_ffn_all

    def _L1_attn_setup():
        import jax, jax.numpy as jnp
        import numpy as np
        import math
        MAX_REL = 32
        key = jax.random.key(seed)
        ks = jax.random.split(key, 6)
        B, S, D = (2, 512, 192)
        H = 12
        dk = D // H
        s = 1.0 / math.sqrt(D)
        return {'x': jax.random.normal(ks[0], (B, S, D), jnp.float32), 'Wq': jax.random.normal(ks[1], (D, D), jnp.float32) * s, 'bq': jnp.zeros((D,), jnp.float32), 'Wk': jax.random.normal(ks[2], (D, D), jnp.float32) * s, 'bk': jnp.zeros((D,), jnp.float32), 'Wv': jax.random.normal(ks[3], (D, D), jnp.float32) * s, 'bv': jnp.zeros((D,), jnp.float32), 'Wo': jax.random.normal(ks[4], (D, D), jnp.float32) * s, 'bo': jnp.zeros((D,), jnp.float32), 'rel_emb': jax.random.normal(ks[5], (2 * MAX_REL + 1, dk), jnp.float32)}
    _L1_attn_all = _L1_attn_setup()
    _L1_attn_in = {k: v for k, v in _L1_attn_all.items() if k in ('Wq', 'bq', 'Wk', 'bk', 'Wv', 'bv', 'Wo', 'bo', 'rel_emb')}
    del _L1_attn_all

    def _L1_ffn_setup():
        import jax, jax.numpy as jnp
        import numpy as np
        B, S, D = (2, 256, 192)
        I = 96
        E = 8
        G = 4
        TOPK_GROUPS = 2
        K = 2
        ROUTE_SCALE = 1.0
        ALPHA, LIMIT = (1.702, 7.0)

        def swiglu(h):
            xg = jnp.minimum(h[..., ::2], LIMIT)
            xl = jnp.clip(h[..., 1::2], -LIMIT, LIMIT)
            return xg * jax.nn.sigmoid(ALPHA * xg) * (xl + 1.0)

        def gate(x, gate_w, gate_b):
            scores = jax.nn.softmax(jnp.einsum('td,ed->te', x, gate_w).astype(jnp.float32), axis=-1)
            original_scores = scores
            s = scores + gate_b
            T = x.shape[0]
            sg = s.reshape(T, G, E // G)
            group_scores = jnp.sum(jax.lax.top_k(sg, 2)[0], axis=-1)
            _, gidx = jax.lax.top_k(group_scores, TOPK_GROUPS)
            keep = jnp.any(jax.nn.one_hot(gidx, G, dtype=jnp.bool_), axis=1)
            sg = jnp.where(keep[:, :, None], sg, -jnp.inf)
            s = sg.reshape(T, E)
            _, idx = jax.lax.top_k(s, K)
            w = jnp.take_along_axis(original_scores, idx, axis=1) * ROUTE_SCALE
            return (w.astype(x.dtype), idx)

        def expert_ffn(x, W1, B1, W3, B3, W2, B2):
            h1 = jnp.einsum('td,edh->teh', x, W1) + B1
            h3 = jnp.einsum('td,edh->teh', x, W3) + B3
            g = swiglu(h1 * h3)
            return jnp.einsum('tei,eid->ted', g, W2) + B2

        def shared_ffn(x, Ws1, Bs1, Ws3, Bs3, Ws2, Bs2):
            h = (x @ Ws1 + Bs1) * (x @ Ws3 + Bs3)
            return swiglu(h) @ Ws2 + Bs2
        key = jax.random.key(seed)
        ks = jax.random.split(key, 16)
        sc = 0.02
        inp = {'x': jax.random.normal(ks[0], (B, S, D), jnp.float32), 'gate_w': jax.random.normal(ks[1], (E, D), jnp.float32) * sc, 'gate_b': jax.random.normal(ks[2], (E,), jnp.float32) * sc, 'W1': jax.random.normal(ks[3], (E, D, 2 * I), jnp.float32) * sc, 'B1': jax.random.normal(ks[4], (E, 2 * I), jnp.float32) * sc, 'W3': jax.random.normal(ks[5], (E, D, 2 * I), jnp.float32) * sc, 'B3': jax.random.normal(ks[6], (E, 2 * I), jnp.float32) * sc, 'W2': jax.random.normal(ks[7], (E, I, D), jnp.float32) * sc, 'B2': jax.random.normal(ks[8], (E, D), jnp.float32) * sc, 'Ws1': jax.random.normal(ks[9], (D, 2 * I), jnp.float32) * sc, 'Bs1': jax.random.normal(ks[10], (2 * I,), jnp.float32) * sc, 'Ws3': jax.random.normal(ks[11], (D, 2 * I), jnp.float32) * sc, 'Bs3': jax.random.normal(ks[12], (2 * I,), jnp.float32) * sc, 'Ws2': jax.random.normal(ks[13], (I, D), jnp.float32) * sc, 'Bs2': jax.random.normal(ks[14], (D,), jnp.float32) * sc}
        return inp
    _L1_ffn_all = _L1_ffn_setup()
    _L1_ffn_in = {k: v for k, v in _L1_ffn_all.items() if k in ('gate_w', 'gate_b', 'W1', 'B1', 'W3', 'B3', 'W2', 'B2', 'Ws1', 'Bs1', 'Ws3', 'Bs3', 'Ws2', 'Bs2')}
    del _L1_ffn_all
    return {'x': x, 'x_txt': x_txt, 'mask_BS_i2_0': mask_BS_i2_0, 'L0_tok_W_repr': _L0_tok_in['W_repr'], 'L0_tok_b_repr': _L0_tok_in['b_repr'], 'L0_tok_W_proj': _L0_tok_in['W_proj'], 'L0_tok_b_proj': _L0_tok_in['b_proj'], 'L0_txt_token_table': _L0_txt_in['token_table'], 'L0_txt_segm_table': _L0_txt_in['segm_table'], 'L0_attn_Wqkv': _L0_attn_in['Wqkv'], 'L0_attn_Wproj': _L0_attn_in['Wproj'], 'L0_attn_Wv': _L0_attn_in['Wv'], 'L0_attn_bv': _L0_attn_in['bv'], 'L0_ffn_gate_weight': _L0_ffn_in['gate_weight'], 'L0_ffn_w1': _L0_ffn_in['w1'], 'L0_ffn_b1': _L0_ffn_in['b1'], 'L0_ffn_w2': _L0_ffn_in['w2'], 'L0_ffn_b2': _L0_ffn_in['b2'], 'L1_attn_Wq': _L1_attn_in['Wq'], 'L1_attn_bq': _L1_attn_in['bq'], 'L1_attn_Wk': _L1_attn_in['Wk'], 'L1_attn_bk': _L1_attn_in['bk'], 'L1_attn_Wv': _L1_attn_in['Wv'], 'L1_attn_bv': _L1_attn_in['bv'], 'L1_attn_Wo': _L1_attn_in['Wo'], 'L1_attn_bo': _L1_attn_in['bo'], 'L1_attn_rel_emb': _L1_attn_in['rel_emb'], 'L1_ffn_gate_w': _L1_ffn_in['gate_w'], 'L1_ffn_gate_b': _L1_ffn_in['gate_b'], 'L1_ffn_W1': _L1_ffn_in['W1'], 'L1_ffn_B1': _L1_ffn_in['B1'], 'L1_ffn_W3': _L1_ffn_in['W3'], 'L1_ffn_B3': _L1_ffn_in['B3'], 'L1_ffn_W2': _L1_ffn_in['W2'], 'L1_ffn_B2': _L1_ffn_in['B2'], 'L1_ffn_Ws1': _L1_ffn_in['Ws1'], 'L1_ffn_Bs1': _L1_ffn_in['Bs1'], 'L1_ffn_Ws3': _L1_ffn_in['Ws3'], 'L1_ffn_Bs3': _L1_ffn_in['Bs3'], 'L1_ffn_Ws2': _L1_ffn_in['Ws2'], 'L1_ffn_Bs2': _L1_ffn_in['Bs2']}

def reference(x, x_txt, mask_BS_i2_0, L0_tok_W_repr, L0_tok_b_repr, L0_tok_W_proj, L0_tok_b_proj, L0_txt_token_table, L0_txt_segm_table, L0_attn_Wqkv, L0_attn_Wproj, L0_attn_Wv, L0_attn_bv, L0_ffn_gate_weight, L0_ffn_w1, L0_ffn_b1, L0_ffn_w2, L0_ffn_b2, L1_attn_Wq, L1_attn_bq, L1_attn_Wk, L1_attn_bk, L1_attn_Wv, L1_attn_bv, L1_attn_Wo, L1_attn_bo, L1_attn_rel_emb, L1_ffn_gate_w, L1_ffn_gate_b, L1_ffn_W1, L1_ffn_B1, L1_ffn_W3, L1_ffn_B3, L1_ffn_W2, L1_ffn_B2, L1_ffn_Ws1, L1_ffn_Bs1, L1_ffn_Ws3, L1_ffn_Bs3, L1_ffn_Ws2, L1_ffn_Bs2):
    import jax
    import jax.numpy as jnp

    def _L0_tok_ref(x, W_repr, b_repr, W_proj, b_proj):
        import jax, jax.numpy as jnp
        import numpy as np
        PATCH = 16
        bs, C, H, W = x.shape
        R = W_repr.shape[0]
        ph = pw = PATCH
        h, w = (H // ph, W // pw)
        y = jnp.einsum('bchw,rc->bhwr', x, W_repr) + b_repr
        y = y.reshape(bs, h, ph, w, pw, R)
        y = y.transpose(5, 0, 1, 3, 2, 4).reshape(R, bs, h * w, ph * pw)
        out = jnp.einsum('rbnp,rep->bne', y, W_proj) + b_proj.sum(axis=0)
        return out

    def _L0_txt_ref(input_tensor, segment_label, token_table, segm_table):
        import jax, jax.numpy as jnp
        import numpy as np
        VOCAB = 8000
        DIM = 192
        BATCH = 8
        SEQ = 512

        def _sinusoidal_pos(seq_len, dim):
            pos = jnp.arange(seq_len, dtype=jnp.float32)[:, None]
            ids = jnp.arange(dim, dtype=jnp.float32)[None, :]
            even_exp = jnp.floor(ids / 2.0) * 2.0 / dim
            angle = pos / jnp.power(10000.0, even_exp)
            return jnp.where(jnp.arange(dim) % 2 == 0, jnp.sin(angle), jnp.cos(angle))
        batch, seq = input_tensor.shape
        pos = _sinusoidal_pos(seq, token_table.shape[1])
        tokens_embed = token_table[input_tensor]
        segments_embed = segm_table[segment_label]
        return segments_embed + pos[None, :, :] + tokens_embed

    def _L0_attn_ref(x, Wqkv, Wproj, Wv, bv):
        import jax, jax.numpy as jnp
        import numpy as np
        NH = 12
        LEVEL = 4

        def _build_sets(T, Lmin):
            l_list, r_list = ([], [])
            L = Lmin
            while L <= T:
                for i in range(T // L):
                    l_list.append(i * L)
                    r_list.append((i + 1) * L - 1)
                L *= 2
            return (np.asarray(l_list, np.int32), np.asarray(r_list, np.int32))

        def _get_slice(x_cum, l_idx, r_idx):
            r = x_cum[:, :, r_idx, :]
            l = x_cum[:, :, np.maximum(np.asarray(l_idx) - 1, 0), :]
            mask = (np.asarray(l_idx) >= 1).astype(x_cum.dtype)[None, None, :, None]
            return r - l * mask

        def _get_slice_dyn(x_cum, l_idx, r_idx):
            r = x_cum[:, :, r_idx, :]
            l = x_cum[:, :, jnp.maximum(l_idx - 1, 0), :]
            mask = (l_idx >= 1).astype(x_cum.dtype)[None, None, :, None]
            return r - l * mask
        B, T, C = x.shape
        nh = NH
        hs = C // nh
        Lmin = 2 ** LEVEL
        scale = 1.0 / jnp.sqrt(jnp.asarray(hs, x.dtype))
        qkv = x @ Wqkv.T
        q, k, v0 = jnp.split(qkv, 3, axis=-1)
        q = q.reshape(B, T, nh, hs).transpose(0, 2, 1, 3)
        k = k.reshape(B, T, nh, hs).transpose(0, 2, 1, 3)
        v0 = v0.reshape(B, T, nh, hs).transpose(0, 2, 1, 3)
        Wv3 = Wv.reshape(hs, hs, hs)
        v = jnp.einsum('bhti,bhtj,eij->bhte', k, v0, Wv3) + bv
        k_cum = jnp.cumsum(k, axis=2)
        v_cum = jnp.cumsum(v, axis=2)
        l_idx, r_idx = _build_sets(T, Lmin)
        K = _get_slice(k_cum, l_idx, r_idx)
        V = _get_slice(v_cum, l_idx, r_idx)
        t_idx = jnp.arange(T)
        mask = t_idx[:, None] >= jnp.asarray(r_idx)[None, :]
        logits = jnp.einsum('bhtd,bhsd->bhts', q, K) * scale
        logits = jnp.where(mask[None, None], logits, -jnp.inf)
        l_tail = t_idx // Lmin * Lmin
        K_tail = _get_slice_dyn(k_cum, l_tail, t_idx)
        V_tail = _get_slice_dyn(v_cum, l_tail, t_idx)
        tail_logits = jnp.sum(q * K_tail, axis=-1) * scale
        att = jax.nn.softmax(jnp.concatenate([logits, tail_logits[..., None]], axis=-1), axis=-1)
        out = jnp.einsum('bhts,bhsd->bhtd', att[..., :-1], V) + att[..., -1:] * V_tail
        out = out.transpose(0, 2, 1, 3).reshape(B, T, C)
        return out @ Wproj.T

    def _L0_ffn_ref(x, gate_weight, w1, b1, w2, b2):
        import jax, jax.numpy as jnp
        import numpy as np
        B, SEQ, D = (2, 256, 192)
        E, H = (8, 768)
        CAPACITY = 2
        Bb, s, d = x.shape
        xf = x.reshape(-1, d)
        S = xf.shape[0]
        k = S * CAPACITY
        logits = xf @ gate_weight.T
        scores = jax.nn.softmax(logits, axis=-1).T
        vals, idx = jax.lax.top_k(scores.reshape(-1), k)
        gate = jnp.zeros((E * S,), dtype=x.dtype).at[idx].add(vals).reshape(E, S)
        h = jax.nn.gelu(jnp.einsum('sd,edh->esh', xf, w1) + b1[:, None, :], approximate=True)
        out = jnp.einsum('esh,ehd->esd', h, w2) + b2[:, None, :]
        y = jnp.einsum('es,esd->sd', gate, out)
        return y.reshape(Bb, s, d)

    def _L1_attn_ref(x, Wq, bq, Wk, bk, Wv, bv, Wo, bo, rel_emb):
        import jax, jax.numpy as jnp
        import numpy as np
        import math
        MAX_REL = 32
        B, S, D = x.shape
        dk = rel_emb.shape[-1]
        H = D // dk
        scale = 1.0 / math.sqrt(dk)

        def proj(W, b):
            return (x @ W + b).reshape(B, S, H, dk).transpose(0, 2, 1, 3)
        Q = proj(Wq, bq)
        K = proj(Wk, bk)
        V = proj(Wv, bv)
        pos = jnp.arange(S)
        rel_idx = jnp.clip(pos[:, None] - pos[None, :], -MAX_REL, MAX_REL) + MAX_REL
        rel = rel_emb[rel_idx]
        scores = jnp.einsum('bhqd,bhkd->bhqk', Q, K)
        scores = scores + jnp.einsum('bhqd,qkd->bhqk', Q, rel)
        scores = scores * scale
        attn = jax.nn.softmax(scores, axis=-1)
        ctx = jnp.einsum('bhqk,bhkd->bhqd', attn, V)
        ctx = ctx.transpose(0, 2, 1, 3).reshape(B, S, D)
        return ctx @ Wo + bo

    def _L1_ffn_ref(x, gate_w, gate_b, W1, B1, W3, B3, W2, B2, Ws1, Bs1, Ws3, Bs3, Ws2, Bs2):
        import jax, jax.numpy as jnp
        import numpy as np
        B, S, D = (2, 256, 192)
        I = 96
        E = 8
        G = 4
        TOPK_GROUPS = 2
        K = 2
        ROUTE_SCALE = 1.0
        ALPHA, LIMIT = (1.702, 7.0)

        def swiglu(h):
            xg = jnp.minimum(h[..., ::2], LIMIT)
            xl = jnp.clip(h[..., 1::2], -LIMIT, LIMIT)
            return xg * jax.nn.sigmoid(ALPHA * xg) * (xl + 1.0)

        def gate(x, gate_w, gate_b):
            scores = jax.nn.softmax(jnp.einsum('td,ed->te', x, gate_w).astype(jnp.float32), axis=-1)
            original_scores = scores
            s = scores + gate_b
            T = x.shape[0]
            sg = s.reshape(T, G, E // G)
            group_scores = jnp.sum(jax.lax.top_k(sg, 2)[0], axis=-1)
            _, gidx = jax.lax.top_k(group_scores, TOPK_GROUPS)
            keep = jnp.any(jax.nn.one_hot(gidx, G, dtype=jnp.bool_), axis=1)
            sg = jnp.where(keep[:, :, None], sg, -jnp.inf)
            s = sg.reshape(T, E)
            _, idx = jax.lax.top_k(s, K)
            w = jnp.take_along_axis(original_scores, idx, axis=1) * ROUTE_SCALE
            return (w.astype(x.dtype), idx)

        def expert_ffn(x, W1, B1, W3, B3, W2, B2):
            h1 = jnp.einsum('td,edh->teh', x, W1) + B1
            h3 = jnp.einsum('td,edh->teh', x, W3) + B3
            g = swiglu(h1 * h3)
            return jnp.einsum('tei,eid->ted', g, W2) + B2

        def shared_ffn(x, Ws1, Bs1, Ws3, Bs3, Ws2, Bs2):
            h = (x @ Ws1 + Bs1) * (x @ Ws3 + Bs3)
            return swiglu(h) @ Ws2 + Bs2
        inp_shape = x.shape
        xt = x.reshape(-1, D)
        w, idx = gate(xt, gate_w, gate_b)
        combine = jnp.einsum('tk,tke->te', w, jax.nn.one_hot(idx, E, dtype=w.dtype))
        per_expert = expert_ffn(xt, W1, B1, W3, B3, W2, B2)
        routed = jnp.einsum('ted,te->td', per_expert, combine)
        out = routed + shared_ffn(xt, Ws1, Bs1, Ws3, Bs3, Ws2, Bs2)
        return out.reshape(inp_shape)
    h = _L0_tok_ref(x, L0_tok_W_repr, L0_tok_b_repr, L0_tok_W_proj, L0_tok_b_proj)
    h = jnp.concatenate([h, _L0_txt_ref(x_txt, mask_BS_i2_0, L0_txt_token_table, L0_txt_segm_table)], axis=1)
    h = h + _L0_attn_ref(_layernorm(h, axis=-1), L0_attn_Wqkv, L0_attn_Wproj, L0_attn_Wv, L0_attn_bv)
    h = h + _L0_ffn_ref(_layernorm(h, axis=-1), L0_ffn_gate_weight, L0_ffn_w1, L0_ffn_b1, L0_ffn_w2, L0_ffn_b2)
    h = h + _L1_attn_ref(_layernorm(h, axis=-1), L1_attn_Wq, L1_attn_bq, L1_attn_Wk, L1_attn_bk, L1_attn_Wv, L1_attn_bv, L1_attn_Wo, L1_attn_bo, L1_attn_rel_emb)
    h = h + _L1_ffn_ref(_layernorm(h, axis=-1), L1_ffn_gate_w, L1_ffn_gate_b, L1_ffn_W1, L1_ffn_B1, L1_ffn_W3, L1_ffn_B3, L1_ffn_W2, L1_ffn_B2, L1_ffn_Ws1, L1_ffn_Bs1, L1_ffn_Ws3, L1_ffn_Bs3, L1_ffn_Ws2, L1_ffn_Bs2)
    return h

_drawn_inputs = setup_inputs


def setup_inputs(seed=0):
    import zlib

    import numpy as np

    out = dict(_drawn_inputs(seed))
    spreads = {'L0_attn_bv': (0.0, 0.1),
     'L0_ffn_b1': (0.0, 0.8),
     'L0_ffn_b2': (0.0, 0.651),
     'L1_attn_bq': (0.0, 0.547),
     'L1_attn_bk': (0.0, 2.0),
     'L1_attn_bv': (0.0, 0.1),
     'L1_attn_bo': (0.0, 0.1)}
    factors = {'L0_tok_b_repr': 3.692,
     'L0_tok_b_proj': 3.828,
     'L1_ffn_gate_w': 8.0,
     'L1_ffn_gate_b': 8.0,
     'L1_ffn_W1': 8.0,
     'L1_ffn_B1': 8.0,
     'L1_ffn_W3': 8.0,
     'L1_ffn_B3': 8.0,
     'L1_ffn_W2': 8.0,
     'L1_ffn_B2': 64.0,
     'L1_ffn_Ws1': 8.0,
     'L1_ffn_Bs1': 8.0,
     'L1_ffn_Ws3': 8.0,
     'L1_ffn_Bs3': 8.0,
     'L1_ffn_Ws2': 8.0,
     'L1_ffn_Bs2': 44.6}
    for name, (base, spread) in spreads.items():
        noise = np.random.default_rng([zlib.crc32(name.encode()), seed]).standard_normal(out[name].shape)
        drawn = base * np.exp(spread * noise) if base else spread * noise
        out[name] = jnp.asarray(drawn.astype(out[name].dtype))
    for name, factor in factors.items():
        out[name] = (out[name] * factor).astype(out[name].dtype)
    return out
```

```python
from contextlib import ExitStack

import numpy as np

import concourse.bass as bass
from concourse import mybir

F32 = mybir.dt.float32
I32 = mybir.dt.int32
ALU = mybir.AluOpType
ACT = mybir.ActivationFunctionType
AX = mybir.AxisListType.X

B = 32
NI = 36
NT = 128
T = NI + NT
S = B * T
D = 192
G = 2
GF = D // G
NH = 12
HG = NH // G
HS = D // NH
EPS = 1e-5
SCALE = 0.25

TR = 84
T0 = (0, 80)
TOWN = (80, 84)

LMIN = 16
SETS = [(i * L, (i + 1) * L - 1) for L in (16, 32, 64, 128) for i in range(T // L)]
NS = len(SETS)
NC = NS + 1
NG = HG * NC


def pipelined(eng, first, second, third, beside):
    def around(b, p, with_third, with_first):
        def place(at):
            for kind, part in beside.get(at, ()):
                if kind == "third" and with_third:
                    third[part](b, p)
                if kind == "first" and with_first:
                    first[part](b + 2, p)
        second(b + 1, 1 - p, place)

    for part in first:
        part(0, 0)
    around(-1, 1, False, True)
    for p in range(2):
        around(p, p, True, True)
    with eng.Fori(1, B // 2 - 1) as pair:
        for p in range(2):
            around(pair * 2 + p, p, True, True)
    around(B - 2, 0, True, False)
    for part in third:
        part(B - 1, 1)


def stage(build):
    def run(nc, *args):
        with nc.cleanup_on_exit():
            build(nc, *args)
    return run


def wait_reuse(eng, sem, value):
    if not (isinstance(value, int) and value <= 0):
        eng.wait_ge(sem, value)


def rows_of(h, b, j, n):
    return h[bass.ds(b * T + T0[j], n), :]


@stage
def build_attention0(nc, h_in, h_out, c):
    with ExitStack() as ctx:
        def sb(name, shape):
            return ctx.enter_context(nc.sbuf_tensor("a0_" + name, shape, F32))

        def ps(name, shape):
            return ctx.enter_context(nc.psum_tensor("a0_" + name, shape, F32))

        def sem(name):
            return nc.alloc_semaphore(name="a0_" + name)

        ident = sb("ident", [128, 128])
        wqkv = sb("wqkv", [GF, G, 3 * D])
        wproj = sb("wproj", [GF, G, D])
        spread = sb("spread", [GF, HG, 3, 128])
        wv_pad = sb("wv_pad", [128, 2, 5 * HS + HS + 5 * HS])
        bv = sb("bv", [GF, 1])
        reset = sb("reset", [GF, T])
        head_mask = sb("head_mask", [GF, HG])
        tail_rows = sb("tail_rows", [NG, GF])
        set_mask = sb("set_mask", [TR, 2, NC])
        half = sb("half", [TR, 2])
        eps = sb("eps", [TR, 2])
        carrier = sb("carrier", [TR, 1])

        hb = sb("hb", [TR, 2, D])
        stats = sb("stats", [TR, 2, 6])
        mean_var = sb("mean_var", [TR, 2, 2])
        var_eps = sb("var_eps", [TR, 2])
        rstd = sb("rstd", [TR, 2])
        xn = sb("xn", [TR, 2, D])
        xt = sb("xt", [GF, G, T])
        qkv = [sb(f"qkv{p}", [GF, 3 * G, T]) for p in range(2)]
        v0x = [sb(f"v0x{i}", [128, T]) for i in range(3)]
        outer = [sb(f"outer{i}", [128, 2, T]) for i in range(3)]
        vt = sb("vt", [GF, G, T])
        ktail = sb("ktail", [GF, G, T])
        vtail = [sb(f"vtail{p}", [GF, G, T]) for p in range(2)]
        ksets = sb("ksets", [GF, G, NS])
        vsets = sb("vsets", [GF, G, NS])
        kdiag = sb("kdiag", [GF, G, HG, NC])
        vdiag = [sb(f"vdiag{p}", [GF, G, HG, NC]) for p in range(2)]
        qk_tail = sb("qk_tail", [GF, G, T])
        lg = sb("lg", [TR, 2 * NH, NC])
        lmax = sb("lmax", [TR, 2 * NH])
        lsum = sb("lsum", [TR, 2 * NH])
        rsum = sb("rsum", [TR, 2 * NH])
        ex = sb("ex", [TR, 2 * NH, NC])
        att = [sb(f"att{p}", [TR, 2 * NH, NC]) for p in range(2)]
        att_t = sb("att_t", [NG, G, T])
        vd_t = sb("vd_t", [NG, G, GF])
        tail_part = sb("tail_part", [GF, G, T])
        ct = sb("ct", [GF, G, T])
        hres = sb("hres", [TR, 2, D])
        hnew = sb("hnew", [TR, 2, D])

        p_x = ps("p_x", [128, 512])
        p_q = ps("p_q", [128, 2, 512])
        p_e = ps("p_e", [128, 3, 512])
        p_v = ps("p_v", [128, 512])
        p_a = ps("p_a", [128, 512])
        p_xt = p_x[0:GF, 0:G * T].rearrange("p (g t) -> p g t", g=G)
        p_vd = p_x[0:NG, 0:G * GF].rearrange("p (g f) -> p g f", g=G)
        p_vt = p_v[0:GF, 0:G * T].rearrange("p (g t) -> p g t", g=G)
        p_at = p_a[0:NG, 0:G * T].rearrange("p (g t) -> p g t", g=G)
        p_o = p_a[0:TR, 0:2 * D].rearrange("p (j f) -> p j f", j=2)
        p_c = p_q[0:GF, 0, 0:G * T].rearrange("p (g t) -> p g t", g=G)
        p_w = p_q[0:GF, 1, 0:G * T].rearrange("p (g t) -> p g t", g=G)

        const_in = sem("const_in")
        cleared = sem("cleared")
        h_in_sem = sem("h_in")
        hres_in = sem("hres_in")
        h_stored = sem("h_stored")
        aggr_in = sem("aggr_in")
        aggr = sem("aggr")
        rstd_ready = sem("rstd_ready")
        pool0 = sem("pool0")
        xn_ready = sem("xn_ready")
        xt_done = sem("xt_done")
        xt_copied = sem("xt_copied")
        qkv_done = sem("qkv_done")
        qkv_copied = sem("qkv_copied")
        spread_done = sem("spread_done")
        v0_copied = sem("v0_copied")
        outer_ready = sem("outer_ready")
        bilin_done = sem("bilin_done")
        vt_copied = sem("vt_copied")
        vec1 = sem("vec1")
        ktail_ready = sem("ktail_ready")
        vtail_ready = sem("vtail_ready")
        kdiag_ready = sem("kdiag_ready")
        qk_ready = sem("qk_ready")
        logits_done = sem("logits_done")
        lg_shifted = sem("lg_shifted")
        exp_done = sem("exp_done")
        att_ready = sem("att_ready")
        vdiag_ready = sem("vdiag_ready")
        turned = sem("turned")
        turned_copied = sem("turned_copied")
        ctx_done = sem("ctx_done")
        vec2 = sem("vec2")
        ct_ready = sem("ct_ready")
        proj_done = sem("proj_done")
        hnew_ready = sem("hnew_ready")

        consts = [(ident[:], c["ident"]), (wqkv[:], c["wqkv"]), (wproj[:], c["wproj"]),
                  (spread[:], c["spread"]), (bv[:], c["bv"]), (reset[:], c["reset"]),
                  (head_mask[:], c["head_mask"]), (tail_rows[:], c["tail_rows"]), (set_mask[:], c["set_mask"]),
                  (wv_pad[:, :, 5 * HS:6 * HS], c["wv"])]
        VEC1 = 13
        block = ctx.enter_context(nc.Block())

        @block.sync
        def _(sp):
            sp.wait_ge(cleared, 4)
            for dst, src in consts:
                sp.dma_start(dst, src).then_inc(const_in, 16)

            def first(b, p):
                wait_reuse(sp, xn_ready, b)
                for j in range(2):
                    sp.dma_start(hb[:, j, :], rows_of(h_in, b, j, TR)).then_inc(h_in_sem, 16)

            def second(b, p, place):
                place(0)

            def residual(b, p):
                wait_reuse(sp, hnew_ready, b)
                for j in range(2):
                    sp.dma_start(hres[:, j, :], rows_of(h_in, b, j, TR)).then_inc(hres_in, 16)

            def store(b, p):
                sp.wait_ge(hnew_ready, b + 1)
                for j in range(2):
                    sp.dma_start(rows_of(h_out, b, j, TOWN[j]), hnew[0:TOWN[j], j, :]).then_inc(h_stored, 16)

            pipelined(sp, [first], second, [residual, store],
                      {0: [("third", 0), ("first", 0), ("third", 1)]})
            sp.wait_ge(h_stored, 32 * B)

        @block.gpsimd
        def _(pool):
            nc.gpsimd.memset(wv_pad[:], 0.0).then_inc(cleared, 1)
            nc.gpsimd.memset(kdiag[:], 0.0).then_inc(cleared, 1)
            nc.gpsimd.memset(vdiag[0][:], 0.0).then_inc(cleared, 1)
            nc.gpsimd.memset(vdiag[1][:], 0.0).then_inc(cleared, 1)
            nc.gpsimd.memset(half[:], -0.5).then_inc(cleared, 1)
            nc.gpsimd.memset(eps[:], EPS).then_inc(cleared, 1)
            pool.wait_ge(cleared, 6)

            def first(b, p):
                pool.wait_ge(aggr, 2 * b + 2)
                nc.gpsimd.tensor_tensor(var_eps[:], mean_var[:, :, 1], eps[:], ALU.add).then_inc(pool0, 1)
                pool.wait_ge(pool0, b + 1)
                nc.gpsimd.tensor_tensor(rstd[:], var_eps[:], half[:], ALU.pow).then_inc(rstd_ready, 1)

            def second(b, p, place):
                pool.wait_ge(ktail_ready, 2 * b + 2)
                wait_reuse(pool, logits_done, b)
                nc.gpsimd.tensor_tensor(qk_tail[:], qkv[p][:, 0:2, :], ktail[:], ALU.mult).then_inc(qk_ready, 1)
                place(0)

            pipelined(pool, [first], second, [], {0: [("first", 0)]})

        @block.vector
        def _(dve):
            dve.wait_ge(const_in, 16 * len(consts))
            dve.wait_ge(cleared, 6)

            def first(b, p):
                dve.wait_ge(h_in_sem, 32 * b + 32)
                for j in range(2):
                    nc.vector.bn_stats(stats[:, j, :], hb[:, j, :]).then_inc(aggr_in, 1)
                dve.wait_ge(aggr_in, 2 * b + 2)
                nc.vector.tensor_copy(carrier[:], half[:, 0:1])
                for j in range(2):
                    nc.vector.bn_aggr(mean_var[:, j, :], stats[:, j, :]).then_inc(aggr, 1)

            def normalise(b, p):
                dve.wait_ge(rstd_ready, b + 1)
                wait_reuse(dve, xt_done, b)
                for j in range(2):
                    i = nc.vector.tensor_scalar(xn[:, j, :], hb[:, j, :], mean_var[:, j, 0:1], rstd[:, j:j + 1],
                                                ALU.subtract, ALU.mult)
                i.then_inc(xn_ready, 1)

            def sums(b, k, src, tail, scanned, sets, diag):
                for g in range(G):
                    nc.vector.tensor_tensor_scan(tail[:, g, :], reset[:], src[:, g, :], 0.0, ALU.mult, ALU.add
                                                 ).then_inc(scanned, 1)
                dve.wait_ge(scanned, 2 * b + 2)
                nc.vector.tensor_copy(sets[:, :, 0:10], tail[:, :, 15:160:16]).then_inc(vec1, 1)
                dve.wait_ge(vec1, VEC1 * b + k + 1)
                nc.vector.tensor_tensor(sets[:, :, 10:15], sets[:, :, 0:10:2], sets[:, :, 1:10:2], ALU.add
                                        ).then_inc(vec1, 1)
                dve.wait_ge(vec1, VEC1 * b + k + 2)
                nc.vector.tensor_tensor(sets[:, :, 15:17], sets[:, :, 10:14:2], sets[:, :, 11:14:2], ALU.add
                                        ).then_inc(vec1, 1)
                dve.wait_ge(vec1, VEC1 * b + k + 3)
                nc.vector.tensor_tensor(sets[:, :, 17:18], sets[:, :, 15:16], sets[:, :, 16:17], ALU.add
                                        ).then_inc(vec1, 1)
                dve.wait_ge(vec1, VEC1 * b + k + 4)
                return [nc.vector.tensor_tensor(diag[:, g, :, 0:NS],
                                                sets[:, g:g + 1, :].broadcast_to([GF, HG, NS]),
                                                head_mask[:].unsqueeze(2).broadcast_to([GF, HG, NS]), ALU.mult)
                        for g in range(G)][-1]

            def products(b, h):
                dve.wait_ge(v0_copied, NH * b + h + 1)
                wait_reuse(dve, bilin_done, NH * b + h - 2)
                nc.vector.tensor_tensor(outer[h % 3][:], p_e[:, h % 3, 0:2 * T].rearrange("p (a t) -> p a t", a=2),
                                        v0x[h % 3][:].unsqueeze(1).broadcast_to([128, 2, T]), ALU.mult
                                        ).then_inc(outer_ready, 1)

            def second(b, p, place):
                dve.wait_ge(qkv_copied, 2 * b + 2)
                wait_reuse(dve, logits_done, b)
                wait_reuse(dve, qk_ready, b)
                sums(b, 0, qkv[p][:, 2:4, :], ktail, ktail_ready, ksets, kdiag).then_inc(kdiag_ready, 1)
                for h in range(4):
                    products(b, h)
                    place(h)
                dve.wait_ge(logits_done, b + 1)
                for j in range(2):
                    nc.vector.scalar_tensor_tensor(
                        lg[:, j * NH:(j + 1) * NH, :],
                        p_a[0:TR, j * 228:(j + 1) * 228].rearrange("p (h s) -> p h s", h=NH), SCALE,
                        set_mask[:, j:j + 1, :].broadcast_to([TR, NH, NC]), ALU.mult, ALU.add).then_inc(vec1, 1)
                dve.wait_ge(vec1, VEC1 * b + 6)
                nc.vector.tensor_reduce(lmax[:], lg[:], AX, ALU.max).then_inc(vec1, 1)
                dve.wait_ge(vec1, VEC1 * b + 7)
                nc.vector.tensor_tensor(lg[:], lg[:], lmax[:].unsqueeze(2).broadcast_to([TR, 2 * NH, NC]),
                                        ALU.subtract).then_inc(lg_shifted, 1)
                for h in range(4, 7):
                    products(b, h)
                    place(h)
                dve.wait_ge(exp_done, b + 1)
                nc.vector.reduce_sum(lsum[:], ex[:], AX).then_inc(vec1, 1)
                products(b, 7)
                dve.wait_ge(vec1, VEC1 * b + 8)
                nc.vector.reciprocal(rsum[:], lsum[:]).then_inc(vec1, 1)
                products(b, 8)
                place(8)
                dve.wait_ge(vec1, VEC1 * b + 9)
                nc.vector.tensor_tensor(att[p][:], ex[:], rsum[:].unsqueeze(2).broadcast_to([TR, 2 * NH, NC]),
                                        ALU.mult).then_inc(att_ready, 1)
                for h in range(9, NH):
                    products(b, h)
                dve.wait_ge(vt_copied, b + 1)
                sums(b, 9, vt, vtail[p], vtail_ready, vsets, vdiag[p]).then_inc(vdiag_ready, 1)

            def context(b, p):
                dve.wait_ge(ctx_done, b + 1)
                nc.vector.tensor_tensor(tail_part[:], p_w, vtail[p][:], ALU.mult).then_inc(vec2, 1)
                dve.wait_ge(vec2, b + 1)
                nc.vector.tensor_tensor(ct[:], tail_part[:], p_c, ALU.add).then_inc(ct_ready, 1)

            def residual(b, p):
                dve.wait_ge(proj_done, b + 1)
                dve.wait_ge(hres_in, 32 * b + 32)
                wait_reuse(dve, h_stored, 32 * b)
                nc.vector.tensor_tensor(hnew[:], p_o, hres[:], ALU.add).then_inc(hnew_ready, 1)

            pipelined(dve, [first, normalise], second, [context, residual],
                      {0: [("first", 0)], 4: [("third", 0)], 6: [("first", 1)], 8: [("third", 1)]})

        @block.scalar
        def _(act):
            act.wait_ge(const_in, 16 * len(consts))

            def copy_xt(b, p):
                act.wait_ge(xt_done, b + 1)
                nc.scalar.copy(xt[:], p_xt).then_inc(xt_copied, 1)

            def copy_qkv(i):
                def part(b, p):
                    act.wait_ge(qkv_done, 2 * b + i + 1)
                    nc.scalar.copy(qkv[p][:, 3 * i:3 * i + 3, :],
                                   p_q[0:GF, i, 0:3 * T].rearrange("p (o t) -> p o t", o=3)).then_inc(qkv_copied, 1)
                return part

            def spread_v(b, h):
                act.wait_ge(spread_done, NH * b + h + 1)
                wait_reuse(act, outer_ready, NH * b + h - 2)
                nc.scalar.copy(v0x[h % 3][:], p_e[:, h % 3, 2 * T:3 * T]).then_inc(v0_copied, 1)

            def second(b, p, place):
                for h in range(6):
                    spread_v(b, h)
                    place(h)
                act.wait_ge(lg_shifted, b + 1)
                wait_reuse(act, att_ready, b)
                nc.scalar.activation(ex[:], lg[:], ACT.Exp).then_inc(exp_done, 1)
                for h in range(6, NH):
                    spread_v(b, h)
                    place(h)
                act.wait_ge(bilin_done, NH * b + NH)
                wait_reuse(act, vdiag_ready, b)
                nc.scalar.activation(vt[:], p_vt, ACT.Identity, bias=bv[:]).then_inc(vt_copied, 1)

            def copy_turned(b, p):
                act.wait_ge(turned, b + 1)
                nc.scalar.copy(vd_t[:], p_vd).then_inc(turned_copied, 1)
                nc.scalar.copy(att_t[:], p_at).then_inc(turned_copied, 1)

            pipelined(act, [copy_xt, copy_qkv(0), copy_qkv(1)], second, [copy_turned],
                      {2: [("third", 0)], 10: [("first", 0)], 11: [("first", 1), ("first", 2)]})

        @block.tensor
        def _(pe):
            pe.wait_ge(const_in, 16 * len(consts))
            pe.wait_ge(cleared, 6)

            def first(b, p):
                pe.wait_ge(xn_ready, b + 1)
                wait_reuse(pe, turned_copied, 2 * b - 2)
                wait_reuse(pe, xt_copied, b)
                for g in range(G):
                    for j in range(2):
                        mm = nc.tensor.transpose(p_xt[:, g, T0[j]:T0[j] + TR], xn[:, j, g * GF:(g + 1) * GF],
                                                 ident[0:TR, 0:TR])
                mm.then_inc(xt_done, 1)

            def project_in(b, p):
                pe.wait_ge(xt_copied, b + 1)
                wait_reuse(pe, ct_ready, b - 1)
                wait_reuse(pe, qkv_copied, 2 * b)
                for i in range(2):
                    for o in range(3):
                        for k in range(G):
                            mm = nc.tensor.matmul(p_q[0:GF, i, o * T:(o + 1) * T],
                                                  wqkv[:, k, (3 * i + o) * GF:(3 * i + o + 1) * GF], xt[:, k, :],
                                                  start=(k == 0), stop=(k == G - 1))
                    mm.then_inc(qkv_done, 1)

            def heads_out(b, p, h):
                g, hh = h // HG, h % HG
                wait_reuse(pe, outer_ready, NH * b + h - 2)
                for a in range(3):
                    src = qkv[p][:, 2 + g, :] if a < 2 else qkv[p][:, 4 + g, :]
                    mm = nc.tensor.matmul(p_e[:, h % 3, a * T:(a + 1) * T], spread[:, hh, a, :], src,
                                          start=True, stop=True)
                mm.then_inc(spread_done, 1)

            def contract(b, h):
                g, hh = h // HG, h % HG
                pe.wait_ge(outer_ready, NH * b + h + 1)
                if h == 0:
                    wait_reuse(pe, vt_copied, b)
                for a in range(2):
                    mm = nc.tensor.matmul(p_vt[:, g, :], wv_pad[:, a, (5 - hh) * HS:(11 - hh) * HS],
                                          outer[h % 3][:, a, :], start=(hh == 0 and a == 0),
                                          stop=(hh == HG - 1 and a == 1))
                mm.then_inc(bilin_done, 1)

            def logits(b, p):
                pe.wait_ge(kdiag_ready, b + 1)
                pe.wait_ge(qk_ready, b + 1)
                wait_reuse(pe, turned_copied, 2 * b)
                wait_reuse(pe, hnew_ready, b - 1)
                for j in range(2):
                    for g in range(G):
                        at = j * 228 + g * NG
                        nc.tensor.matmul(p_a[0:TR, at:at + NG], qkv[p][:, g, T0[j]:T0[j] + TR],
                                         kdiag[:, g, :, :].rearrange("p h s -> p (h s)"), start=True, stop=False)
                        mm = nc.tensor.matmul(p_a[0:TR, at + NS:at + NG:NC], qk_tail[:, g, T0[j]:T0[j] + TR],
                                              head_mask[:], start=False, stop=True)
                mm.then_inc(logits_done, 1)

            def second(b, p, place):
                pe.wait_ge(qkv_copied, 2 * b + 2)
                heads_out(b, p, 0)
                heads_out(b, p, 1)
                place(0)
                for h in range(2, NH):
                    heads_out(b, p, h)
                    if h == 3:
                        logits(b, p)
                    contract(b, h - 2)
                    place(h)
                contract(b, NH - 2)
                contract(b, NH - 1)

            def turn(b, p):
                pe.wait_ge(att_ready, b + 1)
                pe.wait_ge(vdiag_ready, b + 1)
                pe.wait_ge(xt_copied, b + 2 if not isinstance(b, int) else min(b + 2, B))
                wait_reuse(pe, hnew_ready, b)
                for g in range(G):
                    nc.tensor.transpose(p_vd[:, g, :], vdiag[p][:, g, :, :].rearrange("p h s -> p (h s)"),
                                        ident[0:GF, 0:GF])
                    for j in range(2):
                        mm = nc.tensor.transpose(
                            p_at[:, g, T0[j]:T0[j] + TR],
                            att[p][:, j * NH + g * HG:j * NH + (g + 1) * HG, :].rearrange("p h s -> p (h s)"),
                            ident[0:TR, 0:TR])
                mm.then_inc(turned, 1)

            def context(b, p):
                pe.wait_ge(turned_copied, 2 * b + 2)
                pe.wait_ge(qkv_copied, 2 * b + 4 if not isinstance(b, int) else min(2 * b + 4, 2 * B))
                for g in range(G):
                    nc.tensor.matmul(p_c[:, g, :], vd_t[:, g, :], att_t[:, g, :], start=True, stop=True)
                    mm = nc.tensor.matmul(p_w[:, g, :], tail_rows[:], att_t[:, g, :], start=True, stop=True)
                mm.then_inc(ctx_done, 1)

            def project_out(b, p):
                pe.wait_ge(ct_ready, b + 1)
                pe.wait_ge(lg_shifted, b + 2 if not isinstance(b, int) else min(b + 2, B))
                for j in range(2):
                    for g in range(G):
                        mm = nc.tensor.matmul(p_o[:, j, :], ct[:, g, T0[j]:T0[j] + TR], wproj[:, g, :],
                                              start=(g == 0), stop=(g == G - 1))
                mm.then_inc(proj_done, 1)

            pipelined(pe, [first, project_in], second, [turn, context, project_out],
                      {0: [("third", 0)], 3: [("third", 1)], 7: [("third", 2)], 8: [("first", 0)],
                       10: [("first", 1)]})


QB = 8
NQ = -(-T // QB)
TP = NQ * QB
QR = NH * QB
QG = 3
REL_W = T + (NQ - 1) * QB
V0 = (HG - 1) * HS
VW = V0 + HS + V0


@stage
def build_attention1(nc, h_in, h_out, c):
    with ExitStack() as ctx:
        def sb(name, shape):
            return ctx.enter_context(nc.sbuf_tensor("a1_" + name, shape, F32))

        def ps(name, shape):
            return ctx.enter_context(nc.psum_tensor("a1_" + name, shape, F32))

        def sem(name):
            return nc.alloc_semaphore(name="a1_" + name)

        ident = sb("ident", [128, 128])
        wqk = sb("wqk", [GF, G, 2 * D])
        wv = sb("wv", [GF, G, D])
        wo = sb("wo", [GF, G, D])
        bqk = sb("bqk", [GF, 2 * G])
        bv = sb("bv", [TR, D])
        bo = sb("bo", [TR, D])
        spread = sb("spread", [GF, HG, 128])
        query_mask = sb("query_mask", [128, TP])
        head_mask = sb("head_mask", [GF, HG])
        rel = sb("rel", [128, REL_W])
        half = sb("half", [TR, 2])
        eps = sb("eps", [TR, 2])
        carrier = sb("carrier", [TR, 1])

        hb = sb("hb", [TR, 2, D])
        stats = sb("stats", [TR, 2, 6])
        mean_var = sb("mean_var", [TR, 2, 2])
        var_eps = sb("var_eps", [TR, 2])
        rstd = sb("rstd", [TR, 2])
        xn = sb("xn", [TR, 2, D])
        xt = [sb(f"xt{p}", [GF, G, T]) for p in range(2)]
        qk = [sb(f"qk{p}", [GF, 2 * G, TP]) for p in range(2)]
        q_heads = [sb(f"q_heads{p}", [GF, G, NQ, NH, QB]) for p in range(2)]
        q_block = [sb(f"q_block{p}", [128, NQ, NH, QB]) for p in range(2)]
        v_pad = [sb(f"v_pad{p}", [TR, 2, NH, VW]) for p in range(2)]
        ntop = sb("ntop", [QR, NQ])
        ex = [sb(f"ex{i}", [QR, QG, T]) for i in range(3)]
        esum = sb("esum", [QR, NQ])
        rsum = sb("rsum", [QR, NQ])
        ex_t = [sb(f"ex_t{p}", [TR, 2, NH, TP]) for p in range(2)]
        ct = sb("ct", [GF, G, T])
        hres = sb("hres", [TR, 2, D])
        hbias = sb("hbias", [TR, 2, D])
        hnew = sb("hnew", [TR, 2, D])

        p_x = ps("p_x", [128, 512])
        p_q = ps("p_q", [128, 2, 512])
        p_s = ps("p_s", [128, 2, 512])
        p_t = ps("p_t", [128, 2, 512])
        p_c = ps("p_c", [128, 512])
        p_xt = p_x[0:GF, 0:G * T].rearrange("p (g t) -> p g t", g=G)
        p_o = p_x[0:TR, 0:2 * D].rearrange("p (j f) -> p j f", j=2)
        p_ct = p_c[0:GF, 0:G * TP].rearrange("p (g t) -> p g t", g=G)

        const_in = sem("const_in")
        cleared = sem("cleared")
        h_in_sem = sem("h_in")
        hres_in = sem("hres_in")
        h_stored = sem("h_stored")
        stats_ready = sem("stats_ready")
        aggr = sem("aggr")
        pool0 = sem("pool0")
        rstd_ready = sem("rstd_ready")
        xn_ready = sem("xn_ready")
        xt_done = sem("xt_done")
        xt_copied = sem("xt_copied")
        qk_done = sem("qk_done")
        qk_copied = sem("qk_copied")
        q_heads_ready = sem("q_heads_ready")
        spread_done = sem("spread_done")
        q_block_ready = sem("q_block_ready")
        v_done = sem("v_done")
        v_ready = sem("v_ready")
        scores_done = sem("scores_done")
        ntop_ready = sem("ntop_ready")
        exp_done = sem("exp_done")
        turned = sem("turned")
        turned_copied0 = sem("turned_copied0")
        turned_copied1 = sem("turned_copied1")
        context_done = sem("context_done")
        scaled = sem("scaled")
        rsum_ready = sem("rsum_ready")
        weights_ready = sem("weights_ready")
        ct_copied = sem("ct_copied")
        hbias_ready = sem("hbias_ready")
        proj_done = sem("proj_done")
        hnew_ready = sem("hnew_ready")

        consts = [(ident[:], c["ident"]), (wqk[:], c["wqk"]), (wv[:], c["wv"]), (wo[:], c["wo"]),
                  (bqk[:], c["bqk"]), (bv[:], c["bv"].broadcast_to([TR, D])), (bo[:], c["bo"].broadcast_to([TR, D])),
                  (spread[:], c["spread"]), (query_mask[:], c["query_mask"]), (head_mask[:], c["head_mask"]),
                  (rel[:], c["rel"])]
        NG3 = NQ // QG
        block = ctx.enter_context(nc.Block())

        @block.sync
        def _(sp):
            for dst, src in consts:
                sp.dma_start(dst, src).then_inc(const_in, 16)

            def first(b, p):
                wait_reuse(sp, xn_ready, b)
                for j in range(2):
                    sp.dma_start(hb[:, j, :], rows_of(h_in, b, j, TR)).then_inc(h_in_sem, 16)

            def second(b, p, place):
                place(0)

            def residual(b, p):
                wait_reuse(sp, hbias_ready, b)
                for j in range(2):
                    sp.dma_start(hres[:, j, :], rows_of(h_in, b, j, TR)).then_inc(hres_in, 16)

            def store(b, p):
                sp.wait_ge(hnew_ready, b + 1)
                for j in range(2):
                    sp.dma_start(rows_of(h_out, b, j, TOWN[j]), hnew[0:TOWN[j], j, :]).then_inc(h_stored, 16)

            pipelined(sp, [first], second, [residual, store],
                      {0: [("third", 0), ("first", 0), ("third", 1)]})
            sp.wait_ge(h_stored, 32 * B)

        @block.gpsimd
        def _(pool):
            nc.gpsimd.memset(half[:], -0.5).then_inc(cleared, 1)
            nc.gpsimd.memset(eps[:], EPS).then_inc(cleared, 1)
            for p in range(2):
                nc.gpsimd.memset(q_heads[p][:], 0.0).then_inc(cleared, 1)
                nc.gpsimd.memset(qk[p][:, :, T:TP], 0.0).then_inc(cleared, 1)
                nc.gpsimd.memset(v_pad[p][:], 0.0).then_inc(cleared, 1)
            pool.wait_ge(cleared, 8)
            pool.wait_ge(const_in, 16 * len(consts))

            def first(b, p):
                pool.wait_ge(aggr, 2 * b + 2)
                nc.gpsimd.tensor_tensor(var_eps[:], mean_var[:, :, 1], eps[:], ALU.add).then_inc(pool0, 1)
                pool.wait_ge(pool0, b + 1)
                nc.gpsimd.tensor_tensor(rstd[:], var_eps[:], half[:], ALU.pow).then_inc(rstd_ready, 1)

            def split_heads(b, p):
                pool.wait_ge(qk_copied, 4 * b + 2)
                wait_reuse(pool, scores_done, NG3 * (b - 1))
                for g in range(G):
                    for h in range(HG):
                        dst = q_heads[p][:, g, :, g * HG + h, :]
                        src = qk[p][:, g, :].rearrange("p (n q) -> p n q", q=QB)
                        if g == h == 0:
                            i = nc.gpsimd.tensor_tensor(dst, src, head_mask[:, 0:1].unsqueeze(2).broadcast_to(
                                [GF, NQ, QB]), ALU.mult)
                        else:
                            i = nc.gpsimd.tensor_scalar(dst, src, head_mask[:, h:h + 1], None, ALU.mult)
                i.then_inc(q_heads_ready, 1)

            def second(b, p, place):
                place(0)

            def add_bias(b, p):
                pool.wait_ge(hres_in, 32 * b + 32)
                wait_reuse(pool, hnew_ready, b)
                nc.gpsimd.tensor_tensor(hbias[:], hres[:], bo[:].unsqueeze(1).broadcast_to([TR, 2, D]), ALU.add
                                        ).then_inc(hbias_ready, 1)

            pipelined(pool, [first, split_heads], second, [add_bias],
                      {0: [("third", 0), ("first", 0), ("first", 1)]})

        @block.vector
        def _(dve):
            dve.wait_ge(const_in, 16 * len(consts))
            dve.wait_ge(cleared, 8)
            nc.vector.tensor_scalar(bqk[:, 0:G], bqk[:, 0:G], SCALE, None, ALU.mult).then_inc(scaled, 1)

            def first(b, p):
                dve.wait_ge(h_in_sem, 32 * b + 32)
                for j in range(2):
                    nc.vector.bn_stats(stats[:, j, :], hb[:, j, :]).then_inc(stats_ready, 1)
                dve.wait_ge(stats_ready, 2 * b + 2)
                nc.vector.tensor_copy(carrier[:], half[:, 0:1])
                for j in range(2):
                    nc.vector.bn_aggr(mean_var[:, j, :], stats[:, j, :]).then_inc(aggr, 1)

            def normalise(b, p):
                dve.wait_ge(rstd_ready, b + 1)
                wait_reuse(dve, xt_done, b)
                for j in range(2):
                    i = nc.vector.tensor_scalar(xn[:, j, :], hb[:, j, :], mean_var[:, j, 0:1], rstd[:, j:j + 1],
                                                ALU.subtract, ALU.mult)
                i.then_inc(xn_ready, 1)

            def block_queries(i):
                def part(b, p):
                    dve.wait_ge(spread_done, 4 * b + i + 1)
                    if i == 0:
                        wait_reuse(dve, scores_done, NG3 * (b - 1))
                    nc.vector.tensor_tensor(q_block[p][:, :, 3 * i:3 * i + 3, :].rearrange("p n h q -> p h n q"),
                                            p_q[:, i % 2, 0:3 * TP].rearrange("p (h n q) -> p h n q", h=3, q=QB),
                                            query_mask[:].rearrange("p (n q) -> p n q", q=QB).unsqueeze(1)
                                            .broadcast_to([128, 3, NQ, QB]), ALU.mult).then_inc(q_block_ready, 1)
                return part

            def second(b, p, place):
                dve.wait_ge(v_done, b + 1)
                wait_reuse(dve, context_done, b - 1)
                for j in range(2):
                    i = nc.vector.tensor_tensor(v_pad[p][:, j, :, V0:V0 + HS],
                                                p_o[:, j, :].rearrange("p (h e) -> p h e", h=NH),
                                                bv[:].rearrange("p (h e) -> p h e", h=NH), ALU.add)
                i.then_inc(v_ready, 1)

                def divide(k):
                    dve.wait_ge(exp_done, NG3 * b + k + 1)
                    cols = slice(QG * k, QG * k + QG)
                    nc.vector.reciprocal(rsum[:, cols], esum[:, cols]).then_inc(rsum_ready, 1)
                    dve.wait_ge(rsum_ready, NG3 * b + k + 1)
                    for i in range(QG):
                        a = nc.vector.tensor_scalar(ex[k % 3][:, i, :], ex[k % 3][:, i, :],
                                                    rsum[:, QG * k + i:QG * k + i + 1], None, ALU.mult)
                    a.then_inc(weights_ready, 1)

                def copy_turned(k):
                    dve.wait_ge(turned, NG3 * b + k + 1)
                    nc.vector.tensor_copy(ex_t[p][:, 1, :, QB * QG * k:QB * QG * (k + 1)]
                                          .rearrange("p h (i q) -> p i h q", q=QB),
                                          p_t[0:TR, 1, 0:QG * QR].rearrange("p (i h q) -> p i h q", i=QG, q=QB)
                                          ).then_inc(turned_copied1, 1)

                for k in range(NG3 + 2):
                    if k < NG3:
                        dve.wait_ge(scores_done, NG3 * b + k + 1)
                        if k == 0:
                            wait_reuse(dve, exp_done, NG3 * b)
                        nc.vector.tensor_reduce(ntop[:, QG * k:QG * k + QG],
                                                p_s[0:QR, k % 2, 0:QG * T].rearrange("p (i t) -> p i t", i=QG),
                                                AX, ALU.max, negate=True).then_inc(ntop_ready, 1)
                    if 1 <= k <= NG3:
                        divide(k - 1)
                    if k >= 2:
                        copy_turned(k - 2)
                    place(k)

            def residual(b, p):
                dve.wait_ge(proj_done, b + 1)
                dve.wait_ge(hbias_ready, b + 1)
                wait_reuse(dve, h_stored, 32 * b)
                nc.vector.tensor_tensor(hnew[:], p_o, hbias[:], ALU.add).then_inc(hnew_ready, 1)

            pipelined(dve, [first, normalise] + [block_queries(i) for i in range(4)], second, [residual],
                      {0: [("first", 0)], 2: [("first", 1)], 3: [("third", 0)], 6: [("first", 2), ("first", 3)],
                       7: [("first", 4), ("first", 5)]})

        @block.scalar
        def _(act):
            act.wait_ge(const_in, 16 * len(consts))
            act.wait_ge(cleared, 8)
            act.wait_ge(scaled, 1)

            def copy_xt(b, p):
                act.wait_ge(xt_done, b + 1)
                nc.scalar.copy(xt[p][:], p_xt).then_inc(xt_copied, 1)

            def copy_qk(b, p):
                act.wait_ge(qk_done, b + 1)
                for o in range(2 * G):
                    nc.scalar.activation(qk[p][:, o, 0:T], p_q[0:GF, o // 3, (o % 3) * T:(o % 3 + 1) * T], ACT.Identity,
                                         bias=bqk[:, o:o + 1], scale=SCALE if o < G else 1.0).then_inc(qk_copied, 1)

            def second(b, p, place):
                def copy_turned(k):
                    act.wait_ge(turned, NG3 * b + k + 1)
                    nc.scalar.copy(ex_t[p][:, 0, :, QB * QG * k:QB * QG * (k + 1)]
                                   .rearrange("p h (i q) -> p i h q", q=QB),
                                   p_t[0:TR, 0, 0:QG * QR].rearrange("p (i h q) -> p i h q", i=QG, q=QB)
                                   ).then_inc(turned_copied0, 1)

                wait_reuse(act, context_done, b - 1)
                for k in range(NG3 + 2):
                    if k < NG3:
                        act.wait_ge(ntop_ready, NG3 * b + k + 1)
                        wait_reuse(act, turned, NG3 * b + max(k - 2, 0))
                        for i in range(QG):
                            at = QG * k + i
                            a = nc.scalar.activation(ex[k % 3][:, i, :], p_s[0:QR, k % 2, i * T:(i + 1) * T],
                                                     ACT.Exp, bias=ntop[:, at:at + 1], accum_out=esum[:, at:at + 1])
                        a.then_inc(exp_done, 1)
                    if k >= 2:
                        copy_turned(k - 2)
                    place(k)

            def copy_ct(b, p):
                act.wait_ge(context_done, b + 1)
                wait_reuse(act, proj_done, b)
                nc.scalar.copy(ct[:], p_ct[:, :, 0:T]).then_inc(ct_copied, 1)

            pipelined(act, [copy_xt, copy_qk], second, [copy_ct],
                      {1: [("third", 0)], 4: [("first", 0)], 5: [("first", 1)]})

        @block.tensor
        def _(pe):
            pe.wait_ge(const_in, 16 * len(consts))
            pe.wait_ge(cleared, 8)

            def first(b, p):
                pe.wait_ge(xn_ready, b + 1)
                wait_reuse(pe, hnew_ready, b - 1)
                wait_reuse(pe, v_ready, b)
                for g in range(G):
                    for j in range(2):
                        mm = nc.tensor.transpose(p_xt[:, g, T0[j]:T0[j] + TR], xn[:, j, g * GF:(g + 1) * GF],
                                                 ident[0:TR, 0:TR])
                mm.then_inc(xt_done, 1)

            def project_in(b, p):
                pe.wait_ge(xt_copied, b + 1)
                wait_reuse(pe, q_block_ready, 4 * b)
                for o in range(2 * G):
                    for k in range(G):
                        mm = nc.tensor.matmul(p_q[0:GF, o // 3, (o % 3) * T:(o % 3 + 1) * T],
                                              wqk[:, k, o * GF:(o + 1) * GF], xt[p][:, k, :],
                                              start=(k == 0), stop=(k == G - 1))
                mm.then_inc(qk_done, 1)

            def spread_queries(i):
                def part(b, p):
                    pe.wait_ge(qk_copied, 4 * b + 4)
                    if i >= 2:
                        wait_reuse(pe, q_block_ready, 4 * b + i - 1)
                    for h in range(3 * i, 3 * i + 3):
                        mm = nc.tensor.matmul(p_q[:, i % 2, (h - 3 * i) * TP:(h - 3 * i + 1) * TP],
                                              spread[:, h % HG, :], qk[p][:, h // HG, :], start=True, stop=True)
                    mm.then_inc(spread_done, 1)
                return part

            def second(b, p, place):
                wait_reuse(pe, hnew_ready, b - 1)
                pe.wait_ge(xt_copied, b + 1)
                for j in range(2):
                    for g in range(G):
                        mm = nc.tensor.matmul(p_o[:, j, :], xt[p][:, g, T0[j]:T0[j] + TR], wv[:, g, :],
                                              start=(g == 0), stop=(g == G - 1))
                mm.then_inc(v_done, 1)
                pe.wait_ge(q_heads_ready, b + 1)
                pe.wait_ge(q_block_ready, 4 * b + 4)

                def scores(k):
                    wait_reuse(pe, exp_done, NG3 * b + max(k - 1, 0))
                    for i in range(QG):
                        n = QG * k + i
                        out = p_s[0:QR, k % 2, i * T:(i + 1) * T]
                        nc.tensor.matmul(out, q_block[p][:, n, :, :].rearrange("p h q -> p (h q)"),
                                         rel[:, REL_W - T - QB * n:REL_W - QB * n], start=True, stop=False)
                        for g in range(G):
                            mm = nc.tensor.matmul(out, q_heads[p][:, g, n, :, :].rearrange("p h q -> p (h q)"),
                                                  qk[p][:, G + g, 0:T], start=False, stop=(g == G - 1))
                    mm.then_inc(scores_done, 1)

                def turn(k):
                    pe.wait_ge(weights_ready, NG3 * b + k + 1)
                    wait_reuse(pe, turned_copied0, NG3 * b + k)
                    wait_reuse(pe, turned_copied1, NG3 * b + k)
                    for j in range(2):
                        for i in range(QG):
                            mm = nc.tensor.transpose(p_t[0:TR, j, i * QR:(i + 1) * QR],
                                                     ex[k % 3][:, i, T0[j]:T0[j] + TR], ident[0:QR, 0:QR])
                    mm.then_inc(turned, 1)

                for k in range(NG3 + 2):
                    if k < NG3:
                        scores(k)
                    if k >= 2:
                        turn(k - 2)
                    place(k)

            def context(g):
                def part(b, p):
                    pe.wait_ge(v_ready, b + 1)
                    pe.wait_ge(turned_copied0, NG3 * b + NG3)
                    pe.wait_ge(turned_copied1, NG3 * b + NG3)
                    wait_reuse(pe, ct_copied, b)
                    for h in range(HG):
                        for j in range(2):
                            mm = nc.tensor.matmul(
                                p_ct[:, g, :], v_pad[p][0:TOWN[j], j, g * HG + h, V0 - h * HS:V0 - h * HS + GF],
                                ex_t[p][0:TOWN[j], j, g * HG + h, :], start=(h == 0 and j == 0),
                                stop=(h == HG - 1 and j == 1))
                    if g == G - 1:
                        mm.then_inc(context_done, 1)
                return part

            def project_out(b, p):
                pe.wait_ge(ct_copied, b + 1)
                pe.wait_ge(v_ready, b + 2 if not isinstance(b, int) else min(b + 2, B))
                for j in range(2):
                    for g in range(G):
                        mm = nc.tensor.matmul(p_o[:, j, :], ct[:, g, T0[j]:T0[j] + TR], wo[:, g, :],
                                              start=(g == 0), stop=(g == G - 1))
                mm.then_inc(proj_done, 1)

            pipelined(pe, [first, project_in] + [spread_queries(i) for i in range(4)], second,
                      [context(0), context(1), project_out],
                      {0: [("third", 0)], 1: [("third", 1)], 3: [("third", 2)], 4: [("first", 0)],
                       5: [("first", 1)], 6: [("first", 2), ("first", 3)], 7: [("first", 4), ("first", 5)]})



NTILE = S // 128
CH = 4
NCH = NTILE // CH
E0 = 8
H0 = 768
M0 = H0 // 128
KEPT = 2 * S
E1 = 9
I1 = 96


def in_pairs(eng, step):
    for p in range(2):
        step(p, p)
    with eng.Fori(1, NTILE // 2) as pair:
        for p in range(2):
            step(pair * 2 + p, p)
    step(NTILE - 1, 0)


def over_chunks(eng, step):
    step(0, CH)
    with eng.Fori(1, NCH) as i:
        step(i, CH)
    step(NCH, NTILE - NCH * CH)


@stage
def build_norm(nc, pre, h_in, ident_in, gate_in, t, n_gate):
    with ExitStack() as ctx:
        def sb(name, shape):
            return ctx.enter_context(nc.sbuf_tensor(pre + name, shape, F32))

        def sem(name):
            return nc.alloc_semaphore(name=pre + name)

        h, xt, logits, ident = t["h"], t["xt"], t["logits"], t["ident"]
        wg = sb("wg", [GF, G, n_gate])
        stats = sb("stats", [128, NTILE, 6])
        mean = sb("mean", [128, NTILE])
        gap = sb("gap", [128, NTILE])
        sq = sb("sq", [128, NTILE])
        var = sb("var", [128, NTILE])
        half = sb("half", [128, NTILE])
        rstd = sb("rstd", [128, NTILE])
        xn = [sb(f"xn{p}", [128, D]) for p in range(2)]
        xs = [sb(f"xs{p}", [GF, G, 128]) for p in range(2)]
        p_x = ctx.enter_context(nc.psum_tensor(pre + "p_x", [128, 2, 512], F32))
        p_l = ctx.enter_context(nc.psum_tensor(pre + "p_l", [128, 512], F32))

        loaded = sem("loaded")
        half_ready = sem("half_ready")
        stats_ready = sem("stats_ready")
        vec = sem("vec")
        var_ready = sem("var_ready")
        rstd_ready = sem("rstd_ready")
        xn_ready = sem("xn_ready")
        xt_done = sem("xt_done")
        xs_copied = sem("xs_copied")
        xt_copied = sem("xt_copied")
        logits_done = sem("logits_done")
        block = ctx.enter_context(nc.Block())

        @block.sync
        def _(sp):
            sp.dma_start(h[:], h_in.rearrange("(t p) f -> p t f", p=128)).then_inc(loaded, 16)
            sp.dma_start(wg[:], gate_in).then_inc(loaded, 16)
            sp.dma_start(ident[:], ident_in).then_inc(loaded, 16)

        @block.gpsimd
        def _(pool):
            nc.gpsimd.memset(half[:], -0.5).then_inc(half_ready, 1)
            pool.wait_ge(half_ready, 1)
            pool.wait_ge(var_ready, 1)
            nc.gpsimd.tensor_tensor(rstd[:], var[:], half[:], ALU.pow).then_inc(rstd_ready, 1)

        @block.vector
        def _(dve):
            dve.wait_ge(loaded, 48)
            with dve.Fori(0, NTILE) as i:
                nc.vector.bn_stats(stats[:, bass.ds(i, 1), :].rearrange("p a s -> p (a s)"),
                                   h[:, bass.ds(i, 1), :].rearrange("p a f -> p (a f)")).then_inc(stats_ready, 1)
            dve.wait_ge(stats_ready, NTILE)
            nc.vector.tensor_tensor(mean[:], stats[:, :, 1], stats[:, :, 4], ALU.add).then_inc(vec, 1)
            nc.vector.tensor_tensor(gap[:], stats[:, :, 1], stats[:, :, 4], ALU.subtract).then_inc(vec, 1)
            nc.vector.tensor_tensor(var[:], stats[:, :, 2], stats[:, :, 5], ALU.add).then_inc(vec, 1)
            dve.wait_ge(vec, 3)
            nc.vector.tensor_scalar(mean[:], mean[:], 0.5, None, ALU.mult).then_inc(vec, 1)
            nc.vector.scalar_tensor_tensor(sq[:], gap[:], 0.25, gap[:], ALU.mult, ALU.mult).then_inc(vec, 1)
            nc.vector.tensor_scalar(var[:], var[:], 1.0 / D, EPS, ALU.mult, ALU.add).then_inc(vec, 1)
            dve.wait_ge(vec, 6)
            nc.vector.tensor_tensor(var[:], var[:], sq[:], ALU.add).then_inc(var_ready, 1)
            dve.wait_ge(rstd_ready, 1)

            def step(i, p):
                wait_reuse(dve, xt_done, i)
                nc.vector.tensor_scalar(xn[p][:], h[:, bass.ds(i, 1), :].rearrange("p a f -> p (a f)"),
                                        mean[:, bass.ds(i, 1)], rstd[:, bass.ds(i, 1)], ALU.subtract, ALU.mult
                                        ).then_inc(xn_ready, 1)
                dve.wait_ge(xs_copied, i + 1)
                nc.vector.tensor_copy(xt[:, :, bass.ds(i * 128, 128)], xs[p][:]).then_inc(xt_copied, 1)

            in_pairs(dve, step)
            dve.wait_ge(logits_done, NTILE)
            nc.vector.tensor_copy(logits[:], p_l[:, 0:NTILE * n_gate].rearrange("p (t e) -> p t e", e=n_gate)
                                  ).then_inc(vec, 1)

        @block.scalar
        def _(act):
            def step(i, p):
                act.wait_ge(xt_done, i + 1)
                wait_reuse(act, logits_done, i)
                wait_reuse(act, xt_copied, i)
                nc.scalar.copy(xs[p][:], p_x[0:GF, p, 0:G * 128].rearrange("p (g t) -> p g t", g=G)
                               ).then_inc(xs_copied, 1)

            in_pairs(act, step)

        @block.tensor
        def _(pe):
            def step(i, p):
                pe.wait_ge(xn_ready, i + 1)
                wait_reuse(pe, xs_copied, i)
                for g in range(G):
                    mm = nc.tensor.transpose(p_x[0:GF, p, g * 128:(g + 1) * 128], xn[p][:, g * GF:(g + 1) * GF],
                                             ident[:])
                mm.then_inc(xt_done, 1)
                pe.wait_ge(xs_copied, i + 1)
                for g in range(G):
                    mm = nc.tensor.matmul(p_l[:, bass.ds(i * n_gate, n_gate)], xs[p][:, g, :], wg[:, g, :],
                                          start=(g == 0), stop=(g == G - 1))
                mm.then_inc(logits_done, 1)

            in_pairs(pe, step)


def expert_softmax(nc, dve, vec, at, exp_done, logits, shifted, stat, n):
    wide = [128, NTILE, n]
    nc.vector.tensor_reduce(stat[:], logits[:], AX, ALU.max).then_inc(vec, 1)
    dve.wait_ge(vec, at + 1)
    nc.vector.tensor_tensor(shifted[:], logits[:], stat[:].unsqueeze(2).broadcast_to(wide), ALU.subtract
                            ).then_inc(vec, 1)
    dve.wait_ge(exp_done, 1)
    nc.vector.reduce_sum(stat[:], shifted[:], AX).then_inc(vec, 1)
    dve.wait_ge(vec, at + 3)
    nc.vector.reciprocal(stat[:], stat[:]).then_inc(vec, 1)
    dve.wait_ge(vec, at + 4)
    nc.vector.tensor_tensor(logits[:], shifted[:], stat[:].unsqueeze(2).broadcast_to(wide), ALU.mult
                            ).then_inc(vec, 1)
    dve.wait_ge(vec, at + 5)
    return at + 5


@stage
def build_gate0(nc, c, t):
    with ExitStack() as ctx:
        def sb(name, shape, dt=F32):
            return ctx.enter_context(nc.sbuf_tensor("g0_" + name, shape, dt))

        def sem(name):
            return nc.alloc_semaphore(name="g0_" + name)

        NB = 30
        logits, gate = t["logits"], t["gate"]
        shifted = sb("shifted", [128, NTILE, E0])
        stat = sb("stat", [128, NTILE])
        score = sb("score", [128, E0, NTILE])
        above = sb("above", [128, E0, NTILE])
        ties = sb("ties", [128, E0, NTILE])
        tie_rank = sb("tie_rank", [128, E0 * NTILE])
        before = sb("before", [128, E0 * NTILE])
        room = sb("room", [128, 1])
        count = sb("count", [128, 1])
        bits = sb("bits", [128, NB], I32)
        bits_f = sb("bits_f", [128, NB])
        found = sb("found", [128, 1], I32)
        tried = sb("tried", [128, 1], I32)
        kept = sb("kept", [128, 1], I32)
        ones = sb("ones", [128, 128])
        lower = sb("lower", [128, 128])
        p_c = ctx.enter_context(nc.psum_tensor("g0_p_c", [128, 512], F32))
        p_r = ctx.enter_context(nc.psum_tensor("g0_p_r", [128, 512], F32))
        p_t = ctx.enter_context(nc.psum_tensor("g0_p_t", [128, 512], F32))

        loaded = sem("loaded")
        cleared = sem("cleared")
        vec = sem("vec")
        shift_done = sem("shift_done")
        exp_done = sem("exp_done")
        tried_ready = sem("tried_ready")
        counted = sem("counted")
        summed = sem("summed")
        kept_ready = sem("kept_ready")
        found_ready = sem("found_ready")
        masks_ready = sem("masks_ready")
        ranks_done = sem("ranks_done")
        block = ctx.enter_context(nc.Block())

        @block.sync
        def _(sp):
            for dst, src in ((bits[:], c["bits"]), (bits_f[:], c["bits_f"]), (ones[:], c["ones"]),
                             (lower[:], c["lower"])):
                sp.dma_start(dst, src).then_inc(loaded, 16)

        @block.scalar
        def _(act):
            act.wait_ge(vec, 2)
            nc.scalar.activation(shifted[:], shifted[:], ACT.Exp).then_inc(exp_done, 1)

        @block.vector
        def _(dve):
            dve.wait_ge(loaded, 64)
            at = expert_softmax(nc, dve, vec, 0, exp_done, logits, shifted, stat, E0)
            nc.vector.tensor_copy(score[:], logits[:].rearrange("p t e -> p e t")).then_inc(vec, 1)
            nc.vector.memset(found[:], 0).then_inc(vec, 1)
            dve.wait_ge(vec, at + 2)
            with dve.Fori(0, NB) as i:
                nc.vector.tensor_tensor(tried[:], found[:], bits[:, bass.ds(i, 1)], ALU.bitwise_or
                                        ).then_inc(tried_ready, 1)
                dve.wait_ge(tried_ready, i + 1)
                nc.vector.tensor_scalar(above[:], score[:], tried[:].bitcast(F32), 0.0, ALU.is_ge, ALU.add,
                                        accum_out=count[:]).then_inc(counted, 1)
                dve.wait_ge(summed, i + 1)
                nc.vector.tensor_scalar(kept[:], p_c[:, 0:1], float(KEPT), bits_f[:, bass.ds(i, 1)],
                                        ALU.is_ge, ALU.mult).then_inc(kept_ready, 1)
                dve.wait_ge(kept_ready, i + 1)
                nc.vector.tensor_tensor(found[:], found[:], kept[:], ALU.bitwise_or).then_inc(found_ready, 1)
                dve.wait_ge(found_ready, i + 1)
            nc.vector.tensor_scalar(above[:], score[:], found[:].bitcast(F32), 0.0, ALU.is_gt, ALU.add,
                                    accum_out=count[:]).then_inc(masks_ready, 1)
            nc.vector.tensor_scalar(ties[:], score[:], found[:].bitcast(F32), None, ALU.is_equal
                                    ).then_inc(masks_ready, 1)
            dve.wait_ge(ranks_done, 1)
            nc.vector.tensor_scalar(room[:], p_c[:, 1:2], -1.0, float(KEPT), ALU.mult, ALU.add).then_inc(vec, 1)
            nc.vector.tensor_copy(tie_rank[:], p_t[:, 0:E0 * NTILE]).then_inc(vec, 1)
            dve.wait_ge(vec, at + 4)
            nc.vector.tensor_tensor_scan(before[:], ones[:, 0:1].broadcast_to([128, E0 * NTILE]), tie_rank[:], 0.0,
                                         ALU.mult, ALU.add).then_inc(vec, 1)
            dve.wait_ge(vec, at + 5)
            nc.vector.tensor_tensor(before[:], before[:], tie_rank[:], ALU.subtract).then_inc(vec, 1)
            dve.wait_ge(vec, at + 6)
            nc.vector.tensor_tensor(tie_rank[:], p_r[:, 0:E0 * NTILE], before[:], ALU.add).then_inc(vec, 1)
            dve.wait_ge(vec, at + 7)
            nc.vector.scalar_tensor_tensor(before[:], tie_rank[:], room[:], ties[:].rearrange("p e t -> p (e t)"),
                                           ALU.is_lt, ALU.mult).then_inc(vec, 1)
            dve.wait_ge(vec, at + 8)
            nc.vector.tensor_tensor(above[:], above[:], before[:].rearrange("p (e t) -> p e t", e=E0), ALU.add
                                    ).then_inc(vec, 1)
            dve.wait_ge(vec, at + 9)
            nc.vector.tensor_tensor(gate[:], score[:].rearrange("p e t -> p t e"),
                                    above[:].rearrange("p e t -> p t e"), ALU.mult).then_inc(vec, 1)

        @block.tensor
        def _(pe):
            pe.wait_ge(loaded, 64)
            with pe.Fori(0, NB) as i:
                pe.wait_ge(counted, i + 1)
                nc.tensor.matmul(p_c[:, 0:1], ones[:], count[:], start=True, stop=True).then_inc(summed, 1)
            pe.wait_ge(masks_ready, 2)
            nc.tensor.matmul(p_c[:, 1:2], ones[:], count[:], start=True, stop=True)
            flat = ties[:].rearrange("p e t -> p (e t)")
            nc.tensor.matmul(p_r[:, 0:E0 * NTILE], lower[:], flat, start=True, stop=True)
            nc.tensor.matmul(p_t[:, 0:E0 * NTILE], ones[:], flat, start=True, stop=True).then_inc(ranks_done, 1)


@stage
def build_gate1(nc, c, t):
    with ExitStack() as ctx:
        def sb(name, shape, dt=F32):
            return ctx.enter_context(nc.sbuf_tensor("g1_" + name, shape, dt))

        def sem(name):
            return nc.alloc_semaphore(name="g1_" + name)

        E, GR = E1 - 1, (E1 - 1) // 2
        logits, gate = t["logits"], t["gate"]
        shifted = sb("shifted", [128, NTILE, E])
        stat = sb("stat", [128, NTILE])
        bias = sb("bias", [128, E])
        biased = sb("biased", [128, NTILE, E])
        group = sb("group", [128, NTILE, GR])
        out_of_group = sb("out_of_group", [128, NTILE, GR])
        earlier = sb("earlier", [128, E, E])
        better = sb("better", [128, NTILE, E, E])
        equal = sb("equal", [128, NTILE, E, E])
        rank = sb("rank", [128, NTILE, E])
        loaded = sem("loaded")
        vec = sem("vec")
        exp_done = sem("exp_done")
        block = ctx.enter_context(nc.Block())

        @block.sync
        def _(sp):
            sp.dma_start(bias[:], c["gate_b"].broadcast_to([128, E])).then_inc(loaded, 16)
            sp.dma_start(earlier[:], c["earlier"]).then_inc(loaded, 16)

        @block.scalar
        def _(act):
            act.wait_ge(vec, 2)
            nc.scalar.activation(shifted[:], shifted[:], ACT.Exp).then_inc(exp_done, 1)

        @block.vector
        def _(dve):
            steps = [0]

            def link(ins):
                steps[0] += 1
                ins.then_inc(vec, 1)
                dve.wait_ge(vec, steps[0])

            def ranks(x, n, out):
                a = better[:].rearrange("p t i j -> p t (i j)")[:, :, 0:n * n].rearrange("p t (i j) -> p t i j", i=n)
                q = equal[:].rearrange("p t i j -> p t (i j)")[:, :, 0:n * n].rearrange("p t (i j) -> p t i j", i=n)
                for i in range(n):
                    mine = x[:, :, i:i + 1].broadcast_to([128, NTILE, n])
                    nc.vector.tensor_tensor(a[:, :, i, :], x, mine, ALU.is_gt).then_inc(vec, 1)
                    nc.vector.tensor_tensor(q[:, :, i, :], x, mine, ALU.is_equal).then_inc(vec, 1)
                steps[0] += 2 * n
                dve.wait_ge(vec, steps[0])
                for i in range(n):
                    nc.vector.tensor_tensor(q[:, :, i, :], q[:, :, i, :],
                                            earlier[:, i:i + 1, 0:n].broadcast_to([128, NTILE, n]), ALU.mult
                                            ).then_inc(vec, 1)
                steps[0] += n
                dve.wait_ge(vec, steps[0])
                link(nc.vector.tensor_tensor(a, a, q, ALU.add))
                link(nc.vector.reduce_sum(out, a, AX))

            dve.wait_ge(loaded, 32)
            steps[0] = expert_softmax(nc, dve, vec, 0, exp_done, logits, shifted, stat, E)
            link(nc.vector.tensor_tensor(biased[:], logits[:], bias[:].unsqueeze(1).broadcast_to([128, NTILE, E]),
                                         ALU.add))
            link(nc.vector.tensor_tensor(group[:], biased[:, :, 0:E:2], biased[:, :, 1:E:2], ALU.add))
            ranks(group[:], GR, out_of_group[:])
            link(nc.vector.tensor_scalar(out_of_group[:], out_of_group[:], 2.0, -1e30, ALU.is_ge, ALU.mult))
            for i in range(2):
                link(nc.vector.tensor_tensor(biased[:, :, i:E:2], biased[:, :, i:E:2], out_of_group[:], ALU.add))
            ranks(biased[:], E, rank[:])
            link(nc.vector.tensor_scalar(rank[:], rank[:], 2.0, None, ALU.is_lt))
            link(nc.vector.tensor_tensor(gate[:, :, 0:E], logits[:], rank[:], ALU.mult))
            link(nc.vector.memset(gate[:, :, E:E1], 1.0))


@stage
def build_bias2(nc, pre, ne, b2_in, t):
    with ExitStack() as ctx:
        def sem(name):
            return nc.alloc_semaphore(name=pre + name)

        h, gate, ident = t["h"], t["gate"], t["ident"]
        b2 = ctx.enter_context(nc.sbuf_tensor(pre + "b2", [ne, D], F32))
        gate_s = [ctx.enter_context(nc.sbuf_tensor(f"{pre}gate_s{p}", [128, ne], F32)) for p in range(2)]
        gate_t = [ctx.enter_context(nc.sbuf_tensor(f"{pre}gate_t{p}", [ne, 128], F32)) for p in range(2)]
        p_g = ctx.enter_context(nc.psum_tensor(pre + "p_g", [128, 2, 512], F32))
        p_b = ctx.enter_context(nc.psum_tensor(pre + "p_b", [128, 2, 512], F32))
        loaded = sem("loaded")
        picked = sem("picked")
        turned = sem("turned")
        turned_copied = sem("turned_copied")
        bias_done = sem("bias_done")
        added = sem("added")
        block = ctx.enter_context(nc.Block())

        @block.sync
        def _(sp):
            sp.dma_start(b2[:], b2_in).then_inc(loaded, 16)

        @block.scalar
        def _(act):
            def step(i, p):
                wait_reuse(act, turned, i)
                nc.scalar.copy(gate_s[p][:], gate[:, bass.ds(i, 1), :].rearrange("p a e -> p (a e)")
                               ).then_inc(picked, 1)
                act.wait_ge(turned, i + 1)
                wait_reuse(act, bias_done, i)
                nc.scalar.copy(gate_t[p][:], p_g[0:ne, p, 0:128]).then_inc(turned_copied, 1)

            in_pairs(act, step)

        @block.tensor
        def _(pe):
            pe.wait_ge(loaded, 16)

            def step(i, p):
                pe.wait_ge(picked, i + 1)
                wait_reuse(pe, turned_copied, i)
                nc.tensor.transpose(p_g[0:ne, p, 0:128], gate_s[p][:], ident[:]).then_inc(turned, 1)
                pe.wait_ge(turned_copied, i + 1)
                wait_reuse(pe, added, i)
                nc.tensor.matmul(p_b[:, p, 0:D], gate_t[p][:], b2[:], start=True, stop=True).then_inc(bias_done, 1)

            in_pairs(pe, step)

        @block.vector
        def _(dve):
            def step(i, p):
                dve.wait_ge(bias_done, i + 1)
                at = h[:, bass.ds(i, 1), :].rearrange("p a f -> p (a f)")
                nc.vector.tensor_tensor(at, at, p_b[:, p, 0:D], ALU.add).then_inc(added, 1)

            in_pairs(dve, step)


@stage
def build_experts0(nc, h_out, c, t):
    with ExitStack() as ctx:
        def sb(name, shape):
            return ctx.enter_context(nc.sbuf_tensor("e0_" + name, shape, F32))

        def sem(name):
            return nc.alloc_semaphore(name="e0_" + name)

        NR = 3
        h, xt, gate = t["h"], t["xt"], t["gate"]
        w1 = sb("w1", [GF, E0, G, H0])
        w2 = sb("w2", [128, E0, M0, D])
        b1 = sb("b1", [128, E0, M0])
        hid = [sb(f"hid{i}", [128, CH * 128]) for i in range(NR)]
        p_h = ctx.enter_context(nc.psum_tensor("e0_p_h", [128, 2, 512], F32))
        p_y = ctx.enter_context(nc.psum_tensor("e0_p_y", [128, 2, 2, 512], F32))

        w1_in = [sem(f"w1_in{e}") for e in range(E0)]
        w2_in = [sem(f"w2_in{e}") for e in range(E0)]
        b1_in = sem("b1_in")
        first_done = sem("first_done")
        gelu_done = sem("gelu_done")
        second_done = sem("second_done")
        expert_done = sem("expert_done")
        added = sem("added")
        stored = sem("stored")
        block = ctx.enter_context(nc.Block())

        @block.sync
        def _(sp):
            sp.dma_start(b1[:], c["b1"]).then_inc(b1_in, 16)
            for e in range(E0):
                sp.dma_start(w1[:, e, :, :], c["w1"][e]).then_inc(w1_in[e], 16)
                sp.dma_start(w2[:, e, :, :], c["w2"][e]).then_inc(w2_in[e], 16)

            def step(i, n):
                sp.wait_ge(added, E0 * i + E0)
                sp.dma_start(h_out.rearrange("(t p) f -> p t f", p=128)[:, bass.ds(i * CH, n), :],
                             h[:, bass.ds(i * CH, n), :]).then_inc(stored, 16)

            over_chunks(sp, step)
            sp.wait_ge(stored, 16 * (NCH + 1))

        @block.scalar
        def _(act):
            act.wait_ge(b1_in, 16)

            def step(i, n):
                for e in range(E0):
                    for m in range(M0):
                        k = e * M0 + m
                        act.wait_ge(first_done, E0 * M0 * i + k + 1)
                        if k >= NR:
                            act.wait_ge(second_done, E0 * M0 * i + k - NR + 1)
                        else:
                            wait_reuse(act, second_done, E0 * M0 * i)
                        nc.scalar.activation(hid[k % NR][:, 0:n * 128], p_h[:, k % 2, 0:n * 128],
                                             ACT.Gelu_apprx_tanh, bias=b1[:, e, m:m + 1]).then_inc(gelu_done, 1)

            over_chunks(act, step)

        @block.tensor
        def _(pe):
            def step(i, n):
                def first(k):
                    e, m = k // M0, k % M0
                    if m == 0:
                        pe.wait_ge(w1_in[e], 16)
                    if k >= 2:
                        wait_reuse(pe, gelu_done, E0 * M0 * i + k - 1)
                    else:
                        wait_reuse(pe, gelu_done, E0 * M0 * i)
                    for g in range(G):
                        mm = nc.tensor.matmul(p_h[:, k % 2, 0:n * 128], w1[:, e, g, m * 128:(m + 1) * 128],
                                              xt[:, g, bass.ds(i * CH * 128, n * 128)],
                                              start=(g == 0), stop=(g == G - 1))
                    mm.then_inc(first_done, 1)

                def second(k):
                    e, m = k // M0, k % M0
                    if m == 0:
                        pe.wait_ge(w2_in[e], 16)
                        if e >= 2:
                            wait_reuse(pe, added, E0 * i + e - 1)
                        else:
                            wait_reuse(pe, added, E0 * i)
                    pe.wait_ge(gelu_done, E0 * M0 * i + k + 1)
                    for a in range(n):
                        mm = nc.tensor.matmul(p_y[:, e % 2, a // 2, (a % 2) * D:(a % 2 + 1) * D],
                                              hid[k % NR][:, a * 128:(a + 1) * 128], w2[:, e, m, :],
                                              start=(m == 0 and a % 2 == 0), stop=(m == M0 - 1),
                                              skip_group_check=True)
                    mm.then_inc(second_done, 1)

                first(0)
                for k in range(E0 * M0):
                    if k + 1 < E0 * M0:
                        first(k + 1)
                    second(k)

            over_chunks(pe, step)

        @block.vector
        def _(dve):
            def step(i, n):
                for e in range(E0):
                    dve.wait_ge(second_done, E0 * M0 * i + (e + 1) * M0)
                    if e > 0:
                        dve.wait_ge(added, E0 * i + e)
                    for a in range(n):
                        at = h[:, bass.ds(i * CH + a, 1), :].rearrange("p a f -> p (a f)")
                        v = nc.vector.scalar_tensor_tensor(
                            at, p_y[:, e % 2, a // 2, (a % 2) * D:(a % 2 + 1) * D],
                            gate[:, bass.ds(i * CH + a, 1), e:e + 1].rearrange("p a e -> p (a e)"), at,
                            ALU.mult, ALU.add)
                    v.then_inc(added, 1)

            over_chunks(dve, step)


@stage
def build_experts1(nc, h_out, c, t):
    with ExitStack() as ctx:
        def sb(name, shape):
            return ctx.enter_context(nc.sbuf_tensor("e1_" + name, shape, F32))

        def sem(name):
            return nc.alloc_semaphore(name="e1_" + name)

        ALPHA, LIMIT = 1.702, 7.0
        N = CH * 128
        h, xt, gate = t["h"], t["xt"], t["gate"]
        w13 = sb("w13", [GF, E1, G, 4, I1])
        w2 = sb("w2", [I1, E1, D])
        b13 = sb("b13", [I1, E1, 4])
        h3 = sb("h3", [I1, 2, N])
        prod = sb("prod", [I1, 2, N])
        lin = sb("lin", [I1, N])
        xg = sb("xg", [I1, N])
        sg = sb("sg", [I1, N])
        xl = sb("xl", [I1, N])
        act_t = [sb(f"act_t{i}", [I1, N]) for i in range(2)]
        p_h = ctx.enter_context(nc.psum_tensor("e1_p_h", [128, 4, 512], F32))
        p_y = ctx.enter_context(nc.psum_tensor("e1_p_y", [128, 2, 2, 512], F32))

        loaded = sem("loaded")
        h3_done = sem("h3_done")
        h1_done = sem("h1_done")
        h3_copied = sem("h3_copied")
        prod_ready = sem("prod_ready")
        xg_ready = sem("xg_ready")
        sg_ready = sem("sg_ready")
        xl_ready = sem("xl_ready")
        lin_ready = sem("lin_ready")
        act_ready = sem("act_ready")
        second_done = sem("second_done")
        added = sem("added")
        stored = sem("stored")
        block = ctx.enter_context(nc.Block())

        @block.sync
        def _(sp):
            for dst, src in ((w13[:], c["w13"]), (w2[:], c["w2"]), (b13[:], c["b13"])):
                sp.dma_start(dst, src).then_inc(loaded, 16)

            def step(i, n):
                sp.wait_ge(added, E1 * i + E1)
                sp.dma_start(h_out.rearrange("(t p) f -> p t f", p=128)[:, bass.ds(i * CH, n), :],
                             h[:, bass.ds(i * CH, n), :]).then_inc(stored, 16)

            over_chunks(sp, step)
            sp.wait_ge(stored, 16 * (NCH + 1))

        @block.scalar
        def _(act):
            act.wait_ge(loaded, 48)

            def step(i, n):
                w = n * 128
                for e in range(E1):
                    u = E1 * i + e
                    act.wait_ge(h3_done, u + 1)
                    wait_reuse(act, prod_ready, 2 * u)
                    for o in range(2):
                        nc.scalar.activation(h3[:, o, 0:w], p_h[0:I1, 2 + o, 0:w], ACT.Identity,
                                             bias=b13[:, e, 2 + o:3 + o]).then_inc(h3_copied, 1)
                    act.wait_ge(xg_ready, u + 1)
                    wait_reuse(act, act_ready, u)
                    nc.scalar.activation(sg[:, 0:w], xg[:, 0:w], ACT.Sigmoid, scale=ALPHA).then_inc(sg_ready, 1)

            over_chunks(act, step)

        @block.vector
        def _(dve):
            dve.wait_ge(loaded, 48)

            def step(i, n):
                w = n * 128

                def add(e):
                    dve.wait_ge(second_done, E1 * i + e + 1)
                    if e > 0:
                        dve.wait_ge(added, E1 * i + e)
                    for a in range(n):
                        at = h[:, bass.ds(i * CH + a, 1), :].rearrange("p a f -> p (a f)")
                        v = nc.vector.scalar_tensor_tensor(
                            at, p_y[:, e % 2, a // 2, (a % 2) * D:(a % 2 + 1) * D],
                            gate[:, bass.ds(i * CH + a, 1), e:e + 1].rearrange("p a e -> p (a e)"), at,
                            ALU.mult, ALU.add)
                    v.then_inc(added, 1)

                for e in range(E1):
                    u = E1 * i + e
                    dve.wait_ge(h1_done, u + 1)
                    dve.wait_ge(h3_copied, 2 * u + 2)
                    for o in range(2):
                        nc.vector.scalar_tensor_tensor(prod[:, o, 0:w], p_h[0:I1, o, 0:w], b13[:, e, o:o + 1],
                                                       h3[:, o, 0:w], ALU.add, ALU.mult).then_inc(prod_ready, 1)
                    dve.wait_ge(prod_ready, 2 * u + 2)
                    wait_reuse(dve, sg_ready, u)
                    nc.vector.tensor_scalar(xg[:, 0:w], prod[:, 0, 0:w], LIMIT, None, ALU.min).then_inc(xg_ready, 1)
                    nc.vector.tensor_scalar(xl[:, 0:w], prod[:, 1, 0:w], -LIMIT, LIMIT, ALU.max, ALU.min
                                            ).then_inc(xl_ready, 1)
                    if e > 0:
                        add(e - 1)
                    dve.wait_ge(xl_ready, u + 1)
                    dve.wait_ge(xg_ready, u + 1)
                    nc.vector.scalar_tensor_tensor(lin[:, 0:w], xl[:, 0:w], 1.0, xg[:, 0:w], ALU.add, ALU.mult
                                                   ).then_inc(lin_ready, 1)
                    dve.wait_ge(lin_ready, u + 1)
                    dve.wait_ge(sg_ready, u + 1)
                    if e >= 2:
                        wait_reuse(dve, second_done, u - 1)
                    nc.vector.tensor_tensor(act_t[e % 2][:, 0:w], lin[:, 0:w], sg[:, 0:w], ALU.mult
                                            ).then_inc(act_ready, 1)
                add(E1 - 1)

            over_chunks(dve, step)

        @block.tensor
        def _(pe):
            pe.wait_ge(loaded, 48)

            def step(i, n):
                w = n * 128

                def first(e):
                    u = E1 * i + e
                    for half, done in ((2, h3_done), (0, h1_done)):
                        if half == 2:
                            wait_reuse(pe, h3_copied, 2 * u)
                        else:
                            wait_reuse(pe, prod_ready, 2 * u)
                        for o in range(half, half + 2):
                            for g in range(G):
                                mm = nc.tensor.matmul(p_h[0:I1, o, 0:w], w13[:, e, g, o, :],
                                                      xt[:, g, bass.ds(i * N, w)], start=(g == 0), stop=(g == G - 1))
                        mm.then_inc(done, 1)

                def second(e):
                    u = E1 * i + e
                    pe.wait_ge(act_ready, u + 1)
                    if e >= 2:
                        wait_reuse(pe, added, u - 1)
                    else:
                        wait_reuse(pe, added, E1 * i)
                    for a in range(n):
                        mm = nc.tensor.matmul(p_y[:, e % 2, a // 2, (a % 2) * D:(a % 2 + 1) * D],
                                              act_t[e % 2][:, a * 128:(a + 1) * 128], w2[:, e, :],
                                              start=True, stop=True)
                    mm.then_inc(second_done, 1)

                first(0)
                for e in range(E1):
                    if e + 1 < E1:
                        first(e + 1)
                    second(e)

            over_chunks(pe, step)


def build_moe(nc, layer, h_in, h_out, c):
    ne = (E0, E1)[layer]
    n_gate = 8
    with ExitStack() as ctx:
        def sb(name, shape):
            return ctx.enter_context(nc.sbuf_tensor(f"f{layer}_{name}", shape, F32))

        t = {"h": sb("h", [128, NTILE, D]), "xt": sb("xt", [GF, G, S]), "logits": sb("logits", [128, NTILE, n_gate]),
             "gate": sb("gate", [128, NTILE, ne]), "ident": sb("ident", [128, 128])}
        build_norm(nc, f"n{layer}_", h_in, c["ident"], c["gate_w"], t, n_gate)
        (build_gate0, build_gate1)[layer](nc, c, t)
        build_bias2(nc, f"b{layer}_", ne, c["b2"], t)
        (build_experts0, build_experts1)[layer](nc, h_out, c, t)



CIN = 3
PP = 256
R = 5
VOCAB = 8000
NSEG = 3
KI = CIN * PP // 128
BI = 3
IT = [(3 * i, min(BI, B - 3 * i)) for i in range(-(-B // BI))]
TB = 4


@stage
def build_embed(nc, h_out, c, token_table, segm_table):
    with ExitStack() as ctx:
        def sb(name, shape, dt=F32):
            return ctx.enter_context(nc.sbuf_tensor("em_" + name, shape, dt))

        def sem(name):
            return nc.alloc_semaphore(name="em_" + name)

        pix = sb("pix", [128, KI, B * NI])
        wp = sb("wp", [128, 2, R, D])
        w_repr = sb("w_repr", [128, CIN * R])
        b_repr = sb("b_repr", [128, R])
        b_proj = sb("b_proj", [R, D])
        ones = sb("ones", [128, 128])
        mixed = sb("mixed", [128, CIN + 1, 2, D])
        pos = sb("pos", [NT, D])
        ids = [sb(f"ids{k}", [NT, B], I32) for k in range(2)]
        below = [sb(f"below{k}", [NT, B]) for k in range(2)]
        row = [sb(f"row{k}", [NT, B], I32) for k in range(2)]
        tok = sb("tok", [NT, B, D])
        seg = sb("seg", [NT, B, D])
        img = [sb(f"img{i}", [128, D]) for i in range(2)]
        p_i = ctx.enter_context(nc.psum_tensor("em_p_i", [128, 2, 512], F32))

        pix_in = [sem(f"pix_in{k}") for k in range(KI)]
        w_in = sem("w_in")
        ids_in = sem("ids_in")
        pos_in = sem("pos_in")
        ones_ready = sem("ones_ready")
        mixing = sem("mixing")
        below_ready = sem("below_ready")
        wrapped = sem("wrapped")
        rows_ready = sem("rows_ready")
        gathered = [sem(f"gathered{i}") for i in range(B // TB)]
        with_pos = sem("with_pos")
        text_ready = sem("text_ready")
        image_done = sem("image_done")
        image_copied = sem("image_copied")
        image_stored = [sem(f"image_stored{i}") for i in range(2)]
        text_stored = sem("text_stored")
        h3 = h_out.rearrange("(b t) f -> b t f", t=T)
        block = ctx.enter_context(nc.Block())

        @block.sync
        def _(sp):
            for k in range(2):
                sp.dma_start(ids[k][:], c["ids"][k]).then_inc(ids_in, 16)
            for dst, src in ((wp[:], c["wp"]), (w_repr[:], c["w_repr"].broadcast_to([128, CIN * R])),
                             (b_repr[:], c["b_repr"].broadcast_to([128, R])), (b_proj[:], c["b_proj"])):
                sp.dma_start(dst, src).then_inc(w_in, 16)
            for k in range(KI):
                sp.dma_start(pix[:, k, :], c["pix"][k]).then_inc(pix_in[k], 16)
            sp.dma_start(pos[:], c["pos"]).then_inc(pos_in, 16)
            for i, (b0, nb) in enumerate(IT):
                sp.wait_ge(image_copied, i + 1)
                for b in range(nb):
                    sp.dma_start(h3[b0 + b, 0:NI, :], img[i % 2][b * NI:(b + 1) * NI, :]
                                 ).then_inc(image_stored[i % 2], 16)
            for i in range(B // TB):
                sp.wait_ge(text_ready, i + 1)
                sp.dma_start(h3[i * TB:(i + 1) * TB, NI:T, :].rearrange("b t f -> t b f"),
                             tok[:, i * TB:(i + 1) * TB, :]).then_inc(text_stored, 16)
            for i in range(2):
                sp.wait_ge(image_stored[i], 16 * sum(n for _, n in IT[i::2]))
            sp.wait_ge(text_stored, 16 * (B // TB))

        @block.gpsimd
        def _(pool):
            nc.gpsimd.memset(ones[:], 1.0).then_inc(ones_ready, 1)
            pool.wait_ge(rows_ready, 2)
            for b in range(B):
                for dst, at, table in ((tok, row[0], token_table), (seg, row[1], segm_table)):
                    nc.gpsimd.indirect_dma_start(
                        dst[:, b, :], None, table[:, :], bass.IndirectOffsetOnAxis(ap=at[:, b:b + 1], axis=0)
                    ).then_inc(gathered[b // TB], 16)

        @block.vector
        def _(dve):
            dve.wait_ge(ids_in, 32)
            for k, n in enumerate((VOCAB, NSEG)):
                nc.vector.tensor_scalar(below[k][:], ids[k][:], 0.0, float(n), ALU.is_lt, ALU.mult
                                        ).then_inc(below_ready, 1)
            dve.wait_ge(below_ready, 2)
            for k in range(2):
                nc.vector.tensor_tensor(below[k][:], below[k][:], ids[k][:], ALU.add).then_inc(wrapped, 1)
            dve.wait_ge(wrapped, 2)
            for k, n in enumerate((VOCAB, NSEG)):
                nc.vector.tensor_scalar(row[k][:], below[k][:], 0.0, float(n - 1), ALU.max, ALU.min
                                        ).then_inc(rows_ready, 1)
            dve.wait_ge(w_in, 64)
            for r in range(R):
                if r > 0:
                    dve.wait_ge(mixing, (CIN + 1) * r)
                for ch in range(CIN + 1):
                    by = w_repr[:, ch * R + r:ch * R + r + 1] if ch < CIN else b_repr[:, r:r + 1]
                    if r == 0:
                        nc.vector.tensor_scalar(mixed[:, ch, :, :], wp[:, :, r, :], by, None, ALU.mult
                                                ).then_inc(mixing, 1)
                    else:
                        nc.vector.scalar_tensor_tensor(mixed[:, ch, :, :], wp[:, :, r, :], by, mixed[:, ch, :, :],
                                                       ALU.mult, ALU.add).then_inc(mixing, 1)
            dve.wait_ge(pos_in, 16)
            for i in range(B // TB):
                dve.wait_ge(gathered[i], 32 * TB)
                part = slice(i * TB, (i + 1) * TB)
                nc.vector.tensor_tensor(seg[:, part, :], seg[:, part, :],
                                        pos[:].unsqueeze(1).broadcast_to([NT, TB, D]), ALU.add).then_inc(with_pos, 1)
                dve.wait_ge(with_pos, i + 1)
                nc.vector.tensor_tensor(tok[:, part, :], seg[:, part, :], tok[:, part, :], ALU.add
                                        ).then_inc(text_ready, 1)

        @block.tensor
        def _(pe):
            pe.wait_ge(mixing, (CIN + 1) * R)
            pe.wait_ge(ones_ready, 1)
            for k in range(KI):
                pe.wait_ge(pix_in[k], 16)
            for i, (b0, nb) in enumerate(IT):
                if i >= 2:
                    wait_reuse(pe, image_copied, i - 1)
                out = p_i[0:nb * NI, i % 2, 0:D]
                for k in range(KI):
                    nc.tensor.matmul(out, pix[:, k, b0 * NI:(b0 + nb) * NI], mixed[:, k // 2, k % 2, :],
                                     start=(k == 0), stop=False)
                for k in range(2):
                    nc.tensor.matmul(out, ones[:, 0:nb * NI], mixed[:, CIN, k, :], start=False, stop=False)
                nc.tensor.matmul(out, ones[0:R, 0:nb * NI], b_proj[:], start=False, stop=True
                                 ).then_inc(image_done, 1)

        @block.scalar
        def _(act):
            for i, (b0, nb) in enumerate(IT):
                act.wait_ge(image_done, i + 1)
                if i >= 2:
                    act.wait_ge(image_stored[i % 2], 16 * sum(n for _, n in IT[i % 2:i:2]))
                nc.scalar.copy(img[i % 2][0:nb * NI, :], p_i[0:nb * NI, i % 2, 0:D]).then_inc(image_copied, 1)


def build(nc, a, out):
    def of(stage):
        return {k[3:]: v for k, v in a.items() if k[:3] == stage}

    h = [nc.dram_tensor(f"h{i}", (S, D), F32, kind="Internal").ap() for i in range(4)]
    build_embed(nc, h[0], of("em_"), a["em_token_table"], a["em_segm_table"])
    build_attention0(nc, h[0], h[1], of("a0_"))
    build_moe(nc, 0, h[1], h[2], of("f0_"))
    build_attention1(nc, h[2], h[3], of("a1_"))
    build_moe(nc, 1, h[3], out, of("f1_"))



def by_groups(w):
    return np.ascontiguousarray(w.reshape(G, GF, -1).transpose(1, 0, 2))


def layout(x):
    c = {}
    f32 = np.float32
    ident = np.eye(128, dtype=f32)
    f = np.arange(GF)
    head_mask = (f[:, None] // HS == np.arange(HG)).astype(f32)

    side = x["x"].shape[-1] // 16
    pix = x["x"].reshape(B, CIN, side, 16, side, 16).transpose(1, 3, 5, 0, 2, 4)
    c["em_pix"] = pix.reshape(KI, 128, B * NI)
    c["em_wp"] = x["L0_tok_W_proj"].reshape(R, D, 2, 128).transpose(3, 2, 0, 1)
    c["em_w_repr"] = x["L0_tok_W_repr"].T.reshape(1, CIN * R)
    c["em_b_repr"] = x["L0_tok_b_repr"][None]
    c["em_b_proj"] = x["L0_tok_b_proj"]
    c["em_ids"] = np.stack([x["x_txt"].T, x["mask_BS_i2_0"].T])
    c["em_token_table"] = x["L0_txt_token_table"]
    c["em_segm_table"] = x["L0_txt_segm_table"]
    even = (np.arange(D) // 2 * 2).astype(f32) / f32(D)
    angle = np.arange(NT, dtype=f32)[:, None] / np.power(f32(10000.0), even)[None, :]
    c["em_pos"] = np.where(np.arange(D) % 2 == 0, np.sin(angle), np.cos(angle)).astype(f32)

    c["a0_ident"] = ident
    c["a0_wqkv"] = by_groups(x["L0_attn_Wqkv"].T)
    c["a0_wproj"] = by_groups(x["L0_attn_Wproj"].T)
    c["a0_wv"] = np.ascontiguousarray(x["L0_attn_Wv"].T.reshape(2, 128, HS).transpose(1, 0, 2))
    c["a0_bv"] = np.tile(x["L0_attn_bv"], HG)[:, None]
    col = np.arange(128)
    spread = np.zeros((GF, HG, 3, 128), f32)
    for h in range(HG):
        for a in range(2):
            spread[h * HS + a * 8 + col // HS, h, a, col] = 1
        spread[h * HS + col % HS, h, 2, col] = 1
    c["a0_spread"] = spread
    c["a0_reset"] = np.broadcast_to((np.arange(T) % LMIN != 0).astype(f32), (GF, T))
    c["a0_head_mask"] = head_mask
    tail_rows = np.zeros((HG, NC, GF), f32)
    tail_rows[:, NS, :] = head_mask.T
    c["a0_tail_rows"] = tail_rows.reshape(NG, GF)
    tok = np.arange(TR)[:, None, None] + np.array(T0)[None, :, None]
    last = np.array([r for _, r in SETS] + [-1])
    c["a0_set_mask"] = np.where(tok >= last, 0, -1e30).astype(f32)

    c["a1_ident"] = ident
    c["a1_wqk"] = by_groups(np.concatenate([x["L1_attn_Wq"], x["L1_attn_Wk"]], axis=1))
    c["a1_wv"] = by_groups(x["L1_attn_Wv"])
    c["a1_wo"] = by_groups(x["L1_attn_Wo"])
    c["a1_bqk"] = np.concatenate([x["L1_attn_bq"].reshape(G, GF), x["L1_attn_bk"].reshape(G, GF)]).T
    c["a1_bv"] = x["L1_attn_bv"][None]
    c["a1_bo"] = x["L1_attn_bo"][None]
    c["a1_spread"] = spread[:, :, 2, :]
    c["a1_query_mask"] = (col[:, None] // HS == np.arange(TP) % QB).astype(f32)
    c["a1_head_mask"] = head_mask
    far = x["L1_attn_rel_emb"].shape[0] // 2
    offset = np.arange(QB)[:, None] - (np.arange(REL_W) - (REL_W - T))
    c["a1_rel"] = x["L1_attn_rel_emb"][np.clip(offset, -far, far) + far].transpose(0, 2, 1).reshape(128, REL_W)

    c["f0_ident"] = ident
    c["f0_gate_w"] = by_groups(x["L0_ffn_gate_weight"].T)
    power = 2 ** np.arange(29, -1, -1)
    c["f0_bits"] = np.broadcast_to(power.astype(np.int32), (128, 30))
    c["f0_bits_f"] = np.broadcast_to(power.astype(f32), (128, 30))
    c["f0_ones"] = np.ones((128, 128), f32)
    c["f0_lower"] = np.triu(np.ones((128, 128), f32), 1)
    c["f0_w1"] = x["L0_ffn_w1"].reshape(E0, G, GF, H0).transpose(0, 2, 1, 3)
    c["f0_w2"] = x["L0_ffn_w2"].reshape(E0, M0, 128, D).transpose(0, 2, 1, 3)
    c["f0_b1"] = x["L0_ffn_b1"].reshape(E0, M0, 128).transpose(2, 0, 1)
    c["f0_b2"] = x["L0_ffn_b2"]

    w1, w3, w2, b1, b3, b2 = (np.concatenate([x["L1_ffn_" + a], x["L1_ffn_" + s][None]])
                              for a, s in (("W1", "Ws1"), ("W3", "Ws3"), ("W2", "Ws2"),
                                           ("B1", "Bs1"), ("B3", "Bs3"), ("B2", "Bs2")))
    c["f1_ident"] = ident
    c["f1_gate_w"] = by_groups(x["L1_ffn_gate_w"].T)
    c["f1_gate_b"] = x["L1_ffn_gate_b"][None]
    n = E1 - 1
    c["f1_earlier"] = np.broadcast_to(np.tril(np.ones((n, n), f32), -1), (128, n, n))
    w = np.stack([w1, w3]).reshape(2, E1, G, GF, I1, 2)
    c["f1_w13"] = w.transpose(3, 1, 2, 0, 5, 4).reshape(GF, E1, G, 4, I1)
    c["f1_b13"] = np.stack([b1, b3]).reshape(2, E1, I1, 2).transpose(2, 1, 0, 3).reshape(I1, E1, 4)
    c["f1_w2"] = w2.transpose(1, 0, 2)
    c["f1_b2"] = b2
    return c


def kernel(**inputs):
    from concourse import bacc
    from concourse.bass_utils import run_bass_kernel_spmd

    nc = bacc.Bacc("TRN2", target_bir_lowering=False, num_devices=1)
    arrays, a = {}, {}
    for name, array in layout({k: np.asarray(v) for k, v in inputs.items()}).items():
        arrays["in_" + name] = np.ascontiguousarray(array)
        a[name] = nc.dram_tensor("in_" + name, array.shape, mybir.dt.from_np(array.dtype), kind="ExternalInput").ap()
    out = nc.dram_tensor("out", (S, D), F32, kind="ExternalOutput").ap()
    build(nc, a, out)
    r = run_bass_kernel_spmd(nc, [arrays], core_ids=[0])
    return r.results[0]["out"].reshape(B, T, D)
```

```python
from contextlib import ExitStack

import numpy as np

import concourse.bass as bass
from concourse import mybir

F32 = mybir.dt.float32
I32 = mybir.dt.int32
BF16 = mybir.dt.bfloat16
ALU = mybir.AluOpType
ACT = mybir.ActivationFunctionType
AX = mybir.AxisListType.X

B = 32
NI = 36
NT = 128
T = NI + NT
S = B * T
D = 192
G = 2
GF = D // G
NH = 12
HG = NH // G
HS = D // NH
EPS = 1e-5
SCALE = 0.25

TR = 84
T0 = (0, 80)
TOWN = (80, 84)

LMIN = 16
SETS = [(i * L, (i + 1) * L - 1) for L in (16, 32, 64, 128) for i in range(T // L)]
NS = len(SETS)
NC = NS + 1
NG = HG * NC


def pipelined(eng, first, second, third, beside):
    def around(b, p, with_third, with_first):
        def place(at):
            for kind, part in beside.get(at, ()):
                if kind == "third" and with_third:
                    third[part](b, p)
                if kind == "first" and with_first:
                    first[part](b + 2, p)
        second(b + 1, 1 - p, place)

    for part in first:
        part(0, 0)
    around(-1, 1, False, True)
    for p in range(2):
        around(p, p, True, True)
    with eng.Fori(1, B // 2 - 1) as pair:
        for p in range(2):
            around(pair * 2 + p, p, True, True)
    around(B - 2, 0, True, False)
    for part in third:
        part(B - 1, 1)


def stage(build):
    def run(nc, *args):
        with nc.cleanup_on_exit():
            build(nc, *args)
    return run


def wait_reuse(eng, sem, value):
    if not (isinstance(value, int) and value <= 0):
        eng.wait_ge(sem, value)


def rows_of(h, b, j, n):
    return h[bass.ds(b * T + T0[j], n), :]


@stage
def build_attention0(nc, h_in, h_out, c):
    with ExitStack() as ctx:
        def sb(name, shape):
            return ctx.enter_context(nc.sbuf_tensor("a0_" + name, shape, F32))

        def ps(name, shape):
            return ctx.enter_context(nc.psum_tensor("a0_" + name, shape, F32))

        def sem(name):
            return nc.alloc_semaphore(name="a0_" + name)

        ident = sb("ident", [128, 128])
        wqkv = sb("wqkv", [GF, G, 3 * D])
        wproj = sb("wproj", [GF, G, D])
        spread = sb("spread", [GF, HG, 3, 128])
        wv_pad = sb("wv_pad", [128, 2, 5 * HS + HS + 5 * HS])
        bv = sb("bv", [GF, 1])
        reset = sb("reset", [GF, T])
        head_mask = sb("head_mask", [GF, HG])
        tail_rows = sb("tail_rows", [NG, GF])
        set_mask = sb("set_mask", [TR, 2, NC])
        half = sb("half", [TR, 2])
        eps = sb("eps", [TR, 2])
        carrier = sb("carrier", [TR, 1])

        hb = sb("hb", [TR, 2, D])
        stats = sb("stats", [TR, 2, 6])
        mean_var = sb("mean_var", [TR, 2, 2])
        var_eps = sb("var_eps", [TR, 2])
        rstd = sb("rstd", [TR, 2])
        xn = sb("xn", [TR, 2, D])
        xt = sb("xt", [GF, G, T])
        qkv = [sb(f"qkv{p}", [GF, 3 * G, T]) for p in range(2)]
        v0x = [sb(f"v0x{i}", [128, T]) for i in range(3)]
        outer = [sb(f"outer{i}", [128, 2, T]) for i in range(3)]
        vt = sb("vt", [GF, G, T])
        ktail = sb("ktail", [GF, G, T])
        vtail = [sb(f"vtail{p}", [GF, G, T]) for p in range(2)]
        ksets = sb("ksets", [GF, G, NS])
        vsets = sb("vsets", [GF, G, NS])
        kdiag = sb("kdiag", [GF, G, HG, NC])
        vdiag = [sb(f"vdiag{p}", [GF, G, HG, NC]) for p in range(2)]
        qk_tail = sb("qk_tail", [GF, G, T])
        lg = sb("lg", [TR, 2 * NH, NC])
        lmax = sb("lmax", [TR, 2 * NH])
        lsum = sb("lsum", [TR, 2 * NH])
        rsum = sb("rsum", [TR, 2 * NH])
        ex = sb("ex", [TR, 2 * NH, NC])
        att = [sb(f"att{p}", [TR, 2 * NH, NC]) for p in range(2)]
        att_t = sb("att_t", [NG, G, T])
        vd_t = sb("vd_t", [NG, G, GF])
        tail_part = sb("tail_part", [GF, G, T])
        ct = sb("ct", [GF, G, T])
        hres = sb("hres", [TR, 2, D])
        hnew = sb("hnew", [TR, 2, D])

        p_x = ps("p_x", [128, 512])
        p_q = ps("p_q", [128, 2, 512])
        p_e = ps("p_e", [128, 3, 512])
        p_v = ps("p_v", [128, 512])
        p_a = ps("p_a", [128, 512])
        p_xt = p_x[0:GF, 0:G * T].rearrange("p (g t) -> p g t", g=G)
        p_vd = p_x[0:NG, 0:G * GF].rearrange("p (g f) -> p g f", g=G)
        p_vt = p_v[0:GF, 0:G * T].rearrange("p (g t) -> p g t", g=G)
        p_at = p_a[0:NG, 0:G * T].rearrange("p (g t) -> p g t", g=G)
        p_o = p_a[0:TR, 0:2 * D].rearrange("p (j f) -> p j f", j=2)
        p_c = p_q[0:GF, 0, 0:G * T].rearrange("p (g t) -> p g t", g=G)
        p_w = p_q[0:GF, 1, 0:G * T].rearrange("p (g t) -> p g t", g=G)

        const_in = sem("const_in")
        cleared = sem("cleared")
        h_in_sem = sem("h_in")
        hres_in = sem("hres_in")
        h_stored = sem("h_stored")
        aggr_in = sem("aggr_in")
        aggr = sem("aggr")
        rstd_ready = sem("rstd_ready")
        pool0 = sem("pool0")
        xn_ready = sem("xn_ready")
        xt_done = sem("xt_done")
        xt_copied = sem("xt_copied")
        qkv_done = sem("qkv_done")
        qkv_copied = sem("qkv_copied")
        spread_done = sem("spread_done")
        v0_copied = sem("v0_copied")
        outer_ready = sem("outer_ready")
        bilin_done = sem("bilin_done")
        vt_copied = sem("vt_copied")
        vec1 = sem("vec1")
        ktail_ready = sem("ktail_ready")
        vtail_ready = sem("vtail_ready")
        kdiag_ready = sem("kdiag_ready")
        qk_ready = sem("qk_ready")
        logits_done = sem("logits_done")
        lg_shifted = sem("lg_shifted")
        exp_done = sem("exp_done")
        att_ready = sem("att_ready")
        vdiag_ready = sem("vdiag_ready")
        turned = sem("turned")
        turned_copied = sem("turned_copied")
        ctx_done = sem("ctx_done")
        vec2 = sem("vec2")
        ct_ready = sem("ct_ready")
        proj_done = sem("proj_done")
        hnew_ready = sem("hnew_ready")

        consts = [(ident[:], c["ident"]), (wqkv[:], c["wqkv"]), (wproj[:], c["wproj"]),
                  (spread[:], c["spread"]), (bv[:], c["bv"]), (reset[:], c["reset"]),
                  (head_mask[:], c["head_mask"]), (tail_rows[:], c["tail_rows"]), (set_mask[:], c["set_mask"]),
                  (wv_pad[:, :, 5 * HS:6 * HS], c["wv"])]
        VEC1 = 13
        block = ctx.enter_context(nc.Block())

        @block.sync
        def _(sp):
            sp.wait_ge(cleared, 4)
            for dst, src in consts:
                sp.dma_start(dst, src).then_inc(const_in, 16)

            def first(b, p):
                wait_reuse(sp, xn_ready, b)
                for j in range(2):
                    sp.dma_start(hb[:, j, :], rows_of(h_in, b, j, TR)).then_inc(h_in_sem, 16)

            def second(b, p, place):
                place(0)

            def residual(b, p):
                wait_reuse(sp, hnew_ready, b)
                for j in range(2):
                    sp.dma_start(hres[:, j, :], rows_of(h_in, b, j, TR)).then_inc(hres_in, 16)

            def store(b, p):
                sp.wait_ge(hnew_ready, b + 1)
                for j in range(2):
                    sp.dma_start(rows_of(h_out, b, j, TOWN[j]), hnew[0:TOWN[j], j, :]).then_inc(h_stored, 16)

            pipelined(sp, [first], second, [residual, store],
                      {0: [("third", 0), ("first", 0), ("third", 1)]})
            sp.wait_ge(h_stored, 32 * B)

        @block.gpsimd
        def _(pool):
            nc.gpsimd.memset(wv_pad[:], 0.0).then_inc(cleared, 1)
            nc.gpsimd.memset(kdiag[:], 0.0).then_inc(cleared, 1)
            nc.gpsimd.memset(vdiag[0][:], 0.0).then_inc(cleared, 1)
            nc.gpsimd.memset(vdiag[1][:], 0.0).then_inc(cleared, 1)
            nc.gpsimd.memset(half[:], -0.5).then_inc(cleared, 1)
            nc.gpsimd.memset(eps[:], EPS).then_inc(cleared, 1)
            pool.wait_ge(cleared, 6)

            def first(b, p):
                pool.wait_ge(aggr, 2 * b + 2)
                nc.gpsimd.tensor_tensor(var_eps[:], mean_var[:, :, 1], eps[:], ALU.add).then_inc(pool0, 1)
                pool.wait_ge(pool0, b + 1)
                nc.gpsimd.tensor_tensor(rstd[:], var_eps[:], half[:], ALU.pow).then_inc(rstd_ready, 1)

            def second(b, p, place):
                pool.wait_ge(ktail_ready, 2 * b + 2)
                wait_reuse(pool, logits_done, b)
                nc.gpsimd.tensor_tensor(qk_tail[:], qkv[p][:, 0:2, :], ktail[:], ALU.mult).then_inc(qk_ready, 1)
                place(0)

            pipelined(pool, [first], second, [], {0: [("first", 0)]})

        @block.vector
        def _(dve):
            dve.wait_ge(const_in, 16 * len(consts))
            dve.wait_ge(cleared, 6)

            def first(b, p):
                dve.wait_ge(h_in_sem, 32 * b + 32)
                for j in range(2):
                    nc.vector.bn_stats(stats[:, j, :], hb[:, j, :]).then_inc(aggr_in, 1)
                dve.wait_ge(aggr_in, 2 * b + 2)
                nc.vector.tensor_copy(carrier[:], half[:, 0:1])
                for j in range(2):
                    nc.vector.bn_aggr(mean_var[:, j, :], stats[:, j, :]).then_inc(aggr, 1)

            def normalise(b, p):
                dve.wait_ge(rstd_ready, b + 1)
                wait_reuse(dve, xt_done, b)
                for j in range(2):
                    i = nc.vector.tensor_scalar(xn[:, j, :], hb[:, j, :], mean_var[:, j, 0:1], rstd[:, j:j + 1],
                                                ALU.subtract, ALU.mult)
                i.then_inc(xn_ready, 1)

            def sums(b, k, src, tail, scanned, sets, diag):
                for g in range(G):
                    nc.vector.tensor_tensor_scan(tail[:, g, :], reset[:], src[:, g, :], 0.0, ALU.mult, ALU.add
                                                 ).then_inc(scanned, 1)
                dve.wait_ge(scanned, 2 * b + 2)
                nc.vector.tensor_copy(sets[:, :, 0:10], tail[:, :, 15:160:16]).then_inc(vec1, 1)
                dve.wait_ge(vec1, VEC1 * b + k + 1)
                nc.vector.tensor_tensor(sets[:, :, 10:15], sets[:, :, 0:10:2], sets[:, :, 1:10:2], ALU.add
                                        ).then_inc(vec1, 1)
                dve.wait_ge(vec1, VEC1 * b + k + 2)
                nc.vector.tensor_tensor(sets[:, :, 15:17], sets[:, :, 10:14:2], sets[:, :, 11:14:2], ALU.add
                                        ).then_inc(vec1, 1)
                dve.wait_ge(vec1, VEC1 * b + k + 3)
                nc.vector.tensor_tensor(sets[:, :, 17:18], sets[:, :, 15:16], sets[:, :, 16:17], ALU.add
                                        ).then_inc(vec1, 1)
                dve.wait_ge(vec1, VEC1 * b + k + 4)
                return [nc.vector.tensor_tensor(diag[:, g, :, 0:NS],
                                                sets[:, g:g + 1, :].broadcast_to([GF, HG, NS]),
                                                head_mask[:].unsqueeze(2).broadcast_to([GF, HG, NS]), ALU.mult)
                        for g in range(G)][-1]

            def products(b, h):
                dve.wait_ge(v0_copied, NH * b + h + 1)
                wait_reuse(dve, bilin_done, NH * b + h - 2)
                nc.vector.tensor_tensor(outer[h % 3][:], p_e[:, h % 3, 0:2 * T].rearrange("p (a t) -> p a t", a=2),
                                        v0x[h % 3][:].unsqueeze(1).broadcast_to([128, 2, T]), ALU.mult
                                        ).then_inc(outer_ready, 1)

            def second(b, p, place):
                dve.wait_ge(qkv_copied, 2 * b + 2)
                wait_reuse(dve, logits_done, b)
                wait_reuse(dve, qk_ready, b)
                sums(b, 0, qkv[p][:, 2:4, :], ktail, ktail_ready, ksets, kdiag).then_inc(kdiag_ready, 1)
                for h in range(4):
                    products(b, h)
                    place(h)
                dve.wait_ge(logits_done, b + 1)
                for j in range(2):
                    nc.vector.scalar_tensor_tensor(
                        lg[:, j * NH:(j + 1) * NH, :],
                        p_a[0:TR, j * 228:(j + 1) * 228].rearrange("p (h s) -> p h s", h=NH), SCALE,
                        set_mask[:, j:j + 1, :].broadcast_to([TR, NH, NC]), ALU.mult, ALU.add).then_inc(vec1, 1)
                dve.wait_ge(vec1, VEC1 * b + 6)
                nc.vector.tensor_reduce(lmax[:], lg[:], AX, ALU.max).then_inc(vec1, 1)
                dve.wait_ge(vec1, VEC1 * b + 7)
                nc.vector.tensor_tensor(lg[:], lg[:], lmax[:].unsqueeze(2).broadcast_to([TR, 2 * NH, NC]),
                                        ALU.subtract).then_inc(lg_shifted, 1)
                for h in range(4, 7):
                    products(b, h)
                    place(h)
                dve.wait_ge(exp_done, b + 1)
                nc.vector.reduce_sum(lsum[:], ex[:], AX).then_inc(vec1, 1)
                products(b, 7)
                dve.wait_ge(vec1, VEC1 * b + 8)
                nc.vector.reciprocal(rsum[:], lsum[:]).then_inc(vec1, 1)
                products(b, 8)
                place(8)
                dve.wait_ge(vec1, VEC1 * b + 9)
                nc.vector.tensor_tensor(att[p][:], ex[:], rsum[:].unsqueeze(2).broadcast_to([TR, 2 * NH, NC]),
                                        ALU.mult).then_inc(att_ready, 1)
                for h in range(9, NH):
                    products(b, h)
                dve.wait_ge(vt_copied, b + 1)
                sums(b, 9, vt, vtail[p], vtail_ready, vsets, vdiag[p]).then_inc(vdiag_ready, 1)

            def context(b, p):
                dve.wait_ge(ctx_done, b + 1)
                nc.vector.tensor_tensor(tail_part[:], p_w, vtail[p][:], ALU.mult).then_inc(vec2, 1)
                dve.wait_ge(vec2, b + 1)
                nc.vector.tensor_tensor(ct[:], tail_part[:], p_c, ALU.add).then_inc(ct_ready, 1)

            def residual(b, p):
                dve.wait_ge(proj_done, b + 1)
                dve.wait_ge(hres_in, 32 * b + 32)
                wait_reuse(dve, h_stored, 32 * b)
                nc.vector.tensor_tensor(hnew[:], p_o, hres[:], ALU.add).then_inc(hnew_ready, 1)

            pipelined(dve, [first, normalise], second, [context, residual],
                      {0: [("first", 0)], 4: [("third", 0)], 6: [("first", 1)], 8: [("third", 1)]})

        @block.scalar
        def _(act):
            act.wait_ge(const_in, 16 * len(consts))

            def copy_xt(b, p):
                act.wait_ge(xt_done, b + 1)
                nc.scalar.copy(xt[:], p_xt).then_inc(xt_copied, 1)

            def copy_qkv(i):
                def part(b, p):
                    act.wait_ge(qkv_done, 2 * b + i + 1)
                    nc.scalar.copy(qkv[p][:, 3 * i:3 * i + 3, :],
                                   p_q[0:GF, i, 0:3 * T].rearrange("p (o t) -> p o t", o=3)).then_inc(qkv_copied, 1)
                return part

            def spread_v(b, h):
                act.wait_ge(spread_done, NH * b + h + 1)
                wait_reuse(act, outer_ready, NH * b + h - 2)
                nc.scalar.copy(v0x[h % 3][:], p_e[:, h % 3, 2 * T:3 * T]).then_inc(v0_copied, 1)

            def second(b, p, place):
                for h in range(6):
                    spread_v(b, h)
                    place(h)
                act.wait_ge(lg_shifted, b + 1)
                wait_reuse(act, att_ready, b)
                nc.scalar.activation(ex[:], lg[:], ACT.Exp).then_inc(exp_done, 1)
                for h in range(6, NH):
                    spread_v(b, h)
                    place(h)
                act.wait_ge(bilin_done, NH * b + NH)
                wait_reuse(act, vdiag_ready, b)
                nc.scalar.activation(vt[:], p_vt, ACT.Identity, bias=bv[:]).then_inc(vt_copied, 1)

            def copy_turned(b, p):
                act.wait_ge(turned, b + 1)
                nc.scalar.copy(vd_t[:], p_vd).then_inc(turned_copied, 1)
                nc.scalar.copy(att_t[:], p_at).then_inc(turned_copied, 1)

            pipelined(act, [copy_xt, copy_qkv(0), copy_qkv(1)], second, [copy_turned],
                      {2: [("third", 0)], 10: [("first", 0)], 11: [("first", 1), ("first", 2)]})

        @block.tensor
        def _(pe):
            pe.wait_ge(const_in, 16 * len(consts))
            pe.wait_ge(cleared, 6)

            def first(b, p):
                pe.wait_ge(xn_ready, b + 1)
                wait_reuse(pe, turned_copied, 2 * b - 2)
                wait_reuse(pe, xt_copied, b)
                for g in range(G):
                    for j in range(2):
                        mm = nc.tensor.transpose(p_xt[:, g, T0[j]:T0[j] + TR], xn[:, j, g * GF:(g + 1) * GF],
                                                 ident[0:TR, 0:TR])
                mm.then_inc(xt_done, 1)

            def project_in(b, p):
                pe.wait_ge(xt_copied, b + 1)
                wait_reuse(pe, ct_ready, b - 1)
                wait_reuse(pe, qkv_copied, 2 * b)
                for i in range(2):
                    for o in range(3):
                        for k in range(G):
                            mm = nc.tensor.matmul(p_q[0:GF, i, o * T:(o + 1) * T],
                                                  wqkv[:, k, (3 * i + o) * GF:(3 * i + o + 1) * GF], xt[:, k, :],
                                                  start=(k == 0), stop=(k == G - 1))
                    mm.then_inc(qkv_done, 1)

            def heads_out(b, p, h):
                g, hh = h // HG, h % HG
                wait_reuse(pe, outer_ready, NH * b + h - 2)
                for a in range(3):
                    src = qkv[p][:, 2 + g, :] if a < 2 else qkv[p][:, 4 + g, :]
                    mm = nc.tensor.matmul(p_e[:, h % 3, a * T:(a + 1) * T], spread[:, hh, a, :], src,
                                          start=True, stop=True)
                mm.then_inc(spread_done, 1)

            def contract(b, h):
                g, hh = h // HG, h % HG
                pe.wait_ge(outer_ready, NH * b + h + 1)
                if h == 0:
                    wait_reuse(pe, vt_copied, b)
                for a in range(2):
                    mm = nc.tensor.matmul(p_vt[:, g, :], wv_pad[:, a, (5 - hh) * HS:(11 - hh) * HS],
                                          outer[h % 3][:, a, :], start=(hh == 0 and a == 0),
                                          stop=(hh == HG - 1 and a == 1))
                mm.then_inc(bilin_done, 1)

            def logits(b, p):
                pe.wait_ge(kdiag_ready, b + 1)
                pe.wait_ge(qk_ready, b + 1)
                wait_reuse(pe, turned_copied, 2 * b)
                wait_reuse(pe, hnew_ready, b - 1)
                for j in range(2):
                    for g in range(G):
                        at = j * 228 + g * NG
                        nc.tensor.matmul(p_a[0:TR, at:at + NG], qkv[p][:, g, T0[j]:T0[j] + TR],
                                         kdiag[:, g, :, :].rearrange("p h s -> p (h s)"), start=True, stop=False)
                        mm = nc.tensor.matmul(p_a[0:TR, at + NS:at + NG:NC], qk_tail[:, g, T0[j]:T0[j] + TR],
                                              head_mask[:], start=False, stop=True)
                mm.then_inc(logits_done, 1)

            def second(b, p, place):
                pe.wait_ge(qkv_copied, 2 * b + 2)
                heads_out(b, p, 0)
                heads_out(b, p, 1)
                place(0)
                for h in range(2, NH):
                    heads_out(b, p, h)
                    if h == 3:
                        logits(b, p)
                    contract(b, h - 2)
                    place(h)
                contract(b, NH - 2)
                contract(b, NH - 1)

            def turn(b, p):
                pe.wait_ge(att_ready, b + 1)
                pe.wait_ge(vdiag_ready, b + 1)
                pe.wait_ge(xt_copied, b + 2 if not isinstance(b, int) else min(b + 2, B))
                wait_reuse(pe, hnew_ready, b)
                for g in range(G):
                    nc.tensor.transpose(p_vd[:, g, :], vdiag[p][:, g, :, :].rearrange("p h s -> p (h s)"),
                                        ident[0:GF, 0:GF])
                    for j in range(2):
                        mm = nc.tensor.transpose(
                            p_at[:, g, T0[j]:T0[j] + TR],
                            att[p][:, j * NH + g * HG:j * NH + (g + 1) * HG, :].rearrange("p h s -> p (h s)"),
                            ident[0:TR, 0:TR])
                mm.then_inc(turned, 1)

            def context(b, p):
                pe.wait_ge(turned_copied, 2 * b + 2)
                pe.wait_ge(qkv_copied, 2 * b + 4 if not isinstance(b, int) else min(2 * b + 4, 2 * B))
                for g in range(G):
                    nc.tensor.matmul(p_c[:, g, :], vd_t[:, g, :], att_t[:, g, :], start=True, stop=True)
                    mm = nc.tensor.matmul(p_w[:, g, :], tail_rows[:], att_t[:, g, :], start=True, stop=True)
                mm.then_inc(ctx_done, 1)

            def project_out(b, p):
                pe.wait_ge(ct_ready, b + 1)
                pe.wait_ge(lg_shifted, b + 2 if not isinstance(b, int) else min(b + 2, B))
                for j in range(2):
                    for g in range(G):
                        mm = nc.tensor.matmul(p_o[:, j, :], ct[:, g, T0[j]:T0[j] + TR], wproj[:, g, :],
                                              start=(g == 0), stop=(g == G - 1))
                mm.then_inc(proj_done, 1)

            pipelined(pe, [first, project_in], second, [turn, context, project_out],
                      {0: [("third", 0)], 3: [("third", 1)], 7: [("third", 2)], 8: [("first", 0)],
                       10: [("first", 1)]})


QB = 8
NQ = -(-T // QB)
TP = NQ * QB
QR = NH * QB
QG = 3
REL_W = T + (NQ - 1) * QB
V0 = (HG - 1) * HS
VW = V0 + HS + V0


@stage
def build_attention1(nc, h_in, h_out, c):
    with ExitStack() as ctx:
        def sb(name, shape):
            return ctx.enter_context(nc.sbuf_tensor("a1_" + name, shape, F32))

        def ps(name, shape):
            return ctx.enter_context(nc.psum_tensor("a1_" + name, shape, F32))

        def sem(name):
            return nc.alloc_semaphore(name="a1_" + name)

        ident = sb("ident", [128, 128])
        wqk = sb("wqk", [GF, G, 2 * D])
        wv = sb("wv", [GF, G, D])
        wo = sb("wo", [GF, G, D])
        bqk = sb("bqk", [GF, 2 * G])
        bv = sb("bv", [TR, D])
        bo = sb("bo", [TR, D])
        spread = sb("spread", [GF, HG, 128])
        query_mask = sb("query_mask", [128, TP])
        head_mask = sb("head_mask", [GF, HG])
        rel = sb("rel", [128, REL_W])
        half = sb("half", [TR, 2])
        eps = sb("eps", [TR, 2])
        carrier = sb("carrier", [TR, 1])

        hb = sb("hb", [TR, 2, D])
        stats = sb("stats", [TR, 2, 6])
        mean_var = sb("mean_var", [TR, 2, 2])
        var_eps = sb("var_eps", [TR, 2])
        rstd = sb("rstd", [TR, 2])
        xn = sb("xn", [TR, 2, D])
        xt = [sb(f"xt{p}", [GF, G, T]) for p in range(2)]
        qk = [sb(f"qk{p}", [GF, 2 * G, TP]) for p in range(2)]
        q_heads = [sb(f"q_heads{p}", [GF, G, NQ, NH, QB]) for p in range(2)]
        q_block = [sb(f"q_block{p}", [128, NQ, NH, QB]) for p in range(2)]
        v_pad = [sb(f"v_pad{p}", [TR, 2, NH, VW]) for p in range(2)]
        ntop = sb("ntop", [QR, NQ])
        ex = [sb(f"ex{i}", [QR, QG, T]) for i in range(3)]
        esum = sb("esum", [QR, NQ])
        rsum = sb("rsum", [QR, NQ])
        ex_t = [sb(f"ex_t{p}", [TR, 2, NH, TP]) for p in range(2)]
        ct = sb("ct", [GF, G, T])
        hres = sb("hres", [TR, 2, D])
        hbias = sb("hbias", [TR, 2, D])
        hnew = sb("hnew", [TR, 2, D])

        p_x = ps("p_x", [128, 512])
        p_q = ps("p_q", [128, 2, 512])
        p_s = ps("p_s", [128, 2, 512])
        p_t = ps("p_t", [128, 2, 512])
        p_c = ps("p_c", [128, 512])
        p_xt = p_x[0:GF, 0:G * T].rearrange("p (g t) -> p g t", g=G)
        p_o = p_x[0:TR, 0:2 * D].rearrange("p (j f) -> p j f", j=2)
        p_ct = p_c[0:GF, 0:G * TP].rearrange("p (g t) -> p g t", g=G)

        const_in = sem("const_in")
        cleared = sem("cleared")
        h_in_sem = sem("h_in")
        hres_in = sem("hres_in")
        h_stored = sem("h_stored")
        stats_ready = sem("stats_ready")
        aggr = sem("aggr")
        pool0 = sem("pool0")
        rstd_ready = sem("rstd_ready")
        xn_ready = sem("xn_ready")
        xt_done = sem("xt_done")
        xt_copied = sem("xt_copied")
        qk_done = sem("qk_done")
        qk_copied = sem("qk_copied")
        q_heads_ready = sem("q_heads_ready")
        spread_done = sem("spread_done")
        q_block_ready = sem("q_block_ready")
        v_done = sem("v_done")
        v_ready = sem("v_ready")
        scores_done = sem("scores_done")
        ntop_ready = sem("ntop_ready")
        exp_done = sem("exp_done")
        turned = sem("turned")
        turned_copied0 = sem("turned_copied0")
        turned_copied1 = sem("turned_copied1")
        context_done = sem("context_done")
        scaled = sem("scaled")
        rsum_ready = sem("rsum_ready")
        weights_ready = sem("weights_ready")
        ct_copied = sem("ct_copied")
        hbias_ready = sem("hbias_ready")
        proj_done = sem("proj_done")
        hnew_ready = sem("hnew_ready")

        consts = [(ident[:], c["ident"]), (wqk[:], c["wqk"]), (wv[:], c["wv"]), (wo[:], c["wo"]),
                  (bqk[:], c["bqk"]), (bv[:], c["bv"].broadcast_to([TR, D])), (bo[:], c["bo"].broadcast_to([TR, D])),
                  (spread[:], c["spread"]), (query_mask[:], c["query_mask"]), (head_mask[:], c["head_mask"]),
                  (rel[:], c["rel"])]
        NG3 = NQ // QG
        block = ctx.enter_context(nc.Block())

        @block.sync
        def _(sp):
            for dst, src in consts:
                sp.dma_start(dst, src).then_inc(const_in, 16)

            def first(b, p):
                wait_reuse(sp, xn_ready, b)
                for j in range(2):
                    sp.dma_start(hb[:, j, :], rows_of(h_in, b, j, TR)).then_inc(h_in_sem, 16)

            def second(b, p, place):
                place(0)

            def residual(b, p):
                wait_reuse(sp, hbias_ready, b)
                for j in range(2):
                    sp.dma_start(hres[:, j, :], rows_of(h_in, b, j, TR)).then_inc(hres_in, 16)

            def store(b, p):
                sp.wait_ge(hnew_ready, b + 1)
                for j in range(2):
                    sp.dma_start(rows_of(h_out, b, j, TOWN[j]), hnew[0:TOWN[j], j, :]).then_inc(h_stored, 16)

            pipelined(sp, [first], second, [residual, store],
                      {0: [("third", 0), ("first", 0), ("third", 1)]})
            sp.wait_ge(h_stored, 32 * B)

        @block.gpsimd
        def _(pool):
            nc.gpsimd.memset(half[:], -0.5).then_inc(cleared, 1)
            nc.gpsimd.memset(eps[:], EPS).then_inc(cleared, 1)
            for p in range(2):
                nc.gpsimd.memset(q_heads[p][:], 0.0).then_inc(cleared, 1)
                nc.gpsimd.memset(qk[p][:, :, T:TP], 0.0).then_inc(cleared, 1)
                nc.gpsimd.memset(v_pad[p][:], 0.0).then_inc(cleared, 1)
            pool.wait_ge(cleared, 8)
            pool.wait_ge(const_in, 16 * len(consts))

            def first(b, p):
                pool.wait_ge(aggr, 2 * b + 2)
                nc.gpsimd.tensor_tensor(var_eps[:], mean_var[:, :, 1], eps[:], ALU.add).then_inc(pool0, 1)
                pool.wait_ge(pool0, b + 1)
                nc.gpsimd.tensor_tensor(rstd[:], var_eps[:], half[:], ALU.pow).then_inc(rstd_ready, 1)

            def split_heads(b, p):
                pool.wait_ge(qk_copied, 4 * b + 2)
                wait_reuse(pool, scores_done, NG3 * (b - 1))
                for g in range(G):
                    for h in range(HG):
                        dst = q_heads[p][:, g, :, g * HG + h, :]
                        src = qk[p][:, g, :].rearrange("p (n q) -> p n q", q=QB)
                        if g == h == 0:
                            i = nc.gpsimd.tensor_tensor(dst, src, head_mask[:, 0:1].unsqueeze(2).broadcast_to(
                                [GF, NQ, QB]), ALU.mult)
                        else:
                            i = nc.gpsimd.tensor_scalar(dst, src, head_mask[:, h:h + 1], None, ALU.mult)
                i.then_inc(q_heads_ready, 1)

            def second(b, p, place):
                place(0)

            def add_bias(b, p):
                pool.wait_ge(hres_in, 32 * b + 32)
                wait_reuse(pool, hnew_ready, b)
                nc.gpsimd.tensor_tensor(hbias[:], hres[:], bo[:].unsqueeze(1).broadcast_to([TR, 2, D]), ALU.add
                                        ).then_inc(hbias_ready, 1)

            pipelined(pool, [first, split_heads], second, [add_bias],
                      {0: [("third", 0), ("first", 0), ("first", 1)]})

        @block.vector
        def _(dve):
            dve.wait_ge(const_in, 16 * len(consts))
            dve.wait_ge(cleared, 8)
            nc.vector.tensor_scalar(bqk[:, 0:G], bqk[:, 0:G], SCALE, None, ALU.mult).then_inc(scaled, 1)

            def first(b, p):
                dve.wait_ge(h_in_sem, 32 * b + 32)
                for j in range(2):
                    nc.vector.bn_stats(stats[:, j, :], hb[:, j, :]).then_inc(stats_ready, 1)
                dve.wait_ge(stats_ready, 2 * b + 2)
                nc.vector.tensor_copy(carrier[:], half[:, 0:1])
                for j in range(2):
                    nc.vector.bn_aggr(mean_var[:, j, :], stats[:, j, :]).then_inc(aggr, 1)

            def normalise(b, p):
                dve.wait_ge(rstd_ready, b + 1)
                wait_reuse(dve, xt_done, b)
                for j in range(2):
                    i = nc.vector.tensor_scalar(xn[:, j, :], hb[:, j, :], mean_var[:, j, 0:1], rstd[:, j:j + 1],
                                                ALU.subtract, ALU.mult)
                i.then_inc(xn_ready, 1)

            def block_queries(i):
                def part(b, p):
                    dve.wait_ge(spread_done, 4 * b + i + 1)
                    if i == 0:
                        wait_reuse(dve, scores_done, NG3 * (b - 1))
                    nc.vector.tensor_tensor(q_block[p][:, :, 3 * i:3 * i + 3, :].rearrange("p n h q -> p h n q"),
                                            p_q[:, i % 2, 0:3 * TP].rearrange("p (h n q) -> p h n q", h=3, q=QB),
                                            query_mask[:].rearrange("p (n q) -> p n q", q=QB).unsqueeze(1)
                                            .broadcast_to([128, 3, NQ, QB]), ALU.mult).then_inc(q_block_ready, 1)
                return part

            def second(b, p, place):
                dve.wait_ge(v_done, b + 1)
                wait_reuse(dve, context_done, b - 1)
                for j in range(2):
                    i = nc.vector.tensor_tensor(v_pad[p][:, j, :, V0:V0 + HS],
                                                p_o[:, j, :].rearrange("p (h e) -> p h e", h=NH),
                                                bv[:].rearrange("p (h e) -> p h e", h=NH), ALU.add)
                i.then_inc(v_ready, 1)

                def divide(k):
                    dve.wait_ge(exp_done, NG3 * b + k + 1)
                    cols = slice(QG * k, QG * k + QG)
                    nc.vector.reciprocal(rsum[:, cols], esum[:, cols]).then_inc(rsum_ready, 1)
                    dve.wait_ge(rsum_ready, NG3 * b + k + 1)
                    for i in range(QG):
                        a = nc.vector.tensor_scalar(ex[k % 3][:, i, :], ex[k % 3][:, i, :],
                                                    rsum[:, QG * k + i:QG * k + i + 1], None, ALU.mult)
                    a.then_inc(weights_ready, 1)

                def copy_turned(k):
                    dve.wait_ge(turned, NG3 * b + k + 1)
                    nc.vector.tensor_copy(ex_t[p][:, 1, :, QB * QG * k:QB * QG * (k + 1)]
                                          .rearrange("p h (i q) -> p i h q", q=QB),
                                          p_t[0:TR, 1, 0:QG * QR].rearrange("p (i h q) -> p i h q", i=QG, q=QB)
                                          ).then_inc(turned_copied1, 1)

                for k in range(NG3 + 2):
                    if k < NG3:
                        dve.wait_ge(scores_done, NG3 * b + k + 1)
                        if k == 0:
                            wait_reuse(dve, exp_done, NG3 * b)
                        nc.vector.tensor_reduce(ntop[:, QG * k:QG * k + QG],
                                                p_s[0:QR, k % 2, 0:QG * T].rearrange("p (i t) -> p i t", i=QG),
                                                AX, ALU.max, negate=True).then_inc(ntop_ready, 1)
                    if 1 <= k <= NG3:
                        divide(k - 1)
                    if k >= 2:
                        copy_turned(k - 2)
                    place(k)

            def residual(b, p):
                dve.wait_ge(proj_done, b + 1)
                dve.wait_ge(hbias_ready, b + 1)
                wait_reuse(dve, h_stored, 32 * b)
                nc.vector.tensor_tensor(hnew[:], p_o, hbias[:], ALU.add).then_inc(hnew_ready, 1)

            pipelined(dve, [first, normalise] + [block_queries(i) for i in range(4)], second, [residual],
                      {0: [("first", 0)], 2: [("first", 1)], 3: [("third", 0)], 6: [("first", 2), ("first", 3)],
                       7: [("first", 4), ("first", 5)]})

        @block.scalar
        def _(act):
            act.wait_ge(const_in, 16 * len(consts))
            act.wait_ge(cleared, 8)
            act.wait_ge(scaled, 1)

            def copy_xt(b, p):
                act.wait_ge(xt_done, b + 1)
                nc.scalar.copy(xt[p][:], p_xt).then_inc(xt_copied, 1)

            def copy_qk(b, p):
                act.wait_ge(qk_done, b + 1)
                for o in range(2 * G):
                    nc.scalar.activation(qk[p][:, o, 0:T], p_q[0:GF, o // 3, (o % 3) * T:(o % 3 + 1) * T], ACT.Identity,
                                         bias=bqk[:, o:o + 1], scale=SCALE if o < G else 1.0).then_inc(qk_copied, 1)

            def second(b, p, place):
                def copy_turned(k):
                    act.wait_ge(turned, NG3 * b + k + 1)
                    nc.scalar.copy(ex_t[p][:, 0, :, QB * QG * k:QB * QG * (k + 1)]
                                   .rearrange("p h (i q) -> p i h q", q=QB),
                                   p_t[0:TR, 0, 0:QG * QR].rearrange("p (i h q) -> p i h q", i=QG, q=QB)
                                   ).then_inc(turned_copied0, 1)

                wait_reuse(act, context_done, b - 1)
                for k in range(NG3 + 2):
                    if k < NG3:
                        act.wait_ge(ntop_ready, NG3 * b + k + 1)
                        wait_reuse(act, turned, NG3 * b + max(k - 2, 0))
                        for i in range(QG):
                            at = QG * k + i
                            a = nc.scalar.activation(ex[k % 3][:, i, :], p_s[0:QR, k % 2, i * T:(i + 1) * T],
                                                     ACT.Exp, bias=ntop[:, at:at + 1], accum_out=esum[:, at:at + 1])
                        a.then_inc(exp_done, 1)
                    if k >= 2:
                        copy_turned(k - 2)
                    place(k)

            def copy_ct(b, p):
                act.wait_ge(context_done, b + 1)
                wait_reuse(act, proj_done, b)
                nc.scalar.copy(ct[:], p_ct[:, :, 0:T]).then_inc(ct_copied, 1)

            pipelined(act, [copy_xt, copy_qk], second, [copy_ct],
                      {1: [("third", 0)], 4: [("first", 0)], 5: [("first", 1)]})

        @block.tensor
        def _(pe):
            pe.wait_ge(const_in, 16 * len(consts))
            pe.wait_ge(cleared, 8)

            def first(b, p):
                pe.wait_ge(xn_ready, b + 1)
                wait_reuse(pe, hnew_ready, b - 1)
                wait_reuse(pe, v_ready, b)
                for g in range(G):
                    for j in range(2):
                        mm = nc.tensor.transpose(p_xt[:, g, T0[j]:T0[j] + TR], xn[:, j, g * GF:(g + 1) * GF],
                                                 ident[0:TR, 0:TR])
                mm.then_inc(xt_done, 1)

            def project_in(b, p):
                pe.wait_ge(xt_copied, b + 1)
                wait_reuse(pe, q_block_ready, 4 * b)
                for o in range(2 * G):
                    for k in range(G):
                        mm = nc.tensor.matmul(p_q[0:GF, o // 3, (o % 3) * T:(o % 3 + 1) * T],
                                              wqk[:, k, o * GF:(o + 1) * GF], xt[p][:, k, :],
                                              start=(k == 0), stop=(k == G - 1))
                mm.then_inc(qk_done, 1)

            def spread_queries(i):
                def part(b, p):
                    pe.wait_ge(qk_copied, 4 * b + 4)
                    if i >= 2:
                        wait_reuse(pe, q_block_ready, 4 * b + i - 1)
                    for h in range(3 * i, 3 * i + 3):
                        mm = nc.tensor.matmul(p_q[:, i % 2, (h - 3 * i) * TP:(h - 3 * i + 1) * TP],
                                              spread[:, h % HG, :], qk[p][:, h // HG, :], start=True, stop=True)
                    mm.then_inc(spread_done, 1)
                return part

            def second(b, p, place):
                wait_reuse(pe, hnew_ready, b - 1)
                pe.wait_ge(xt_copied, b + 1)
                for j in range(2):
                    for g in range(G):
                        mm = nc.tensor.matmul(p_o[:, j, :], xt[p][:, g, T0[j]:T0[j] + TR], wv[:, g, :],
                                              start=(g == 0), stop=(g == G - 1))
                mm.then_inc(v_done, 1)
                pe.wait_ge(q_heads_ready, b + 1)
                pe.wait_ge(q_block_ready, 4 * b + 4)

                def scores(k):
                    wait_reuse(pe, exp_done, NG3 * b + max(k - 1, 0))
                    for i in range(QG):
                        n = QG * k + i
                        out = p_s[0:QR, k % 2, i * T:(i + 1) * T]
                        nc.tensor.matmul(out, q_block[p][:, n, :, :].rearrange("p h q -> p (h q)"),
                                         rel[:, REL_W - T - QB * n:REL_W - QB * n], start=True, stop=False)
                        for g in range(G):
                            mm = nc.tensor.matmul(out, q_heads[p][:, g, n, :, :].rearrange("p h q -> p (h q)"),
                                                  qk[p][:, G + g, 0:T], start=False, stop=(g == G - 1))
                    mm.then_inc(scores_done, 1)

                def turn(k):
                    pe.wait_ge(weights_ready, NG3 * b + k + 1)
                    wait_reuse(pe, turned_copied0, NG3 * b + k)
                    wait_reuse(pe, turned_copied1, NG3 * b + k)
                    for j in range(2):
                        for i in range(QG):
                            mm = nc.tensor.transpose(p_t[0:TR, j, i * QR:(i + 1) * QR],
                                                     ex[k % 3][:, i, T0[j]:T0[j] + TR], ident[0:QR, 0:QR])
                    mm.then_inc(turned, 1)

                for k in range(NG3 + 2):
                    if k < NG3:
                        scores(k)
                    if k >= 2:
                        turn(k - 2)
                    place(k)

            def context(g):
                def part(b, p):
                    pe.wait_ge(v_ready, b + 1)
                    pe.wait_ge(turned_copied0, NG3 * b + NG3)
                    pe.wait_ge(turned_copied1, NG3 * b + NG3)
                    wait_reuse(pe, ct_copied, b)
                    for h in range(HG):
                        for j in range(2):
                            mm = nc.tensor.matmul(
                                p_ct[:, g, :], v_pad[p][0:TOWN[j], j, g * HG + h, V0 - h * HS:V0 - h * HS + GF],
                                ex_t[p][0:TOWN[j], j, g * HG + h, :], start=(h == 0 and j == 0),
                                stop=(h == HG - 1 and j == 1))
                    if g == G - 1:
                        mm.then_inc(context_done, 1)
                return part

            def project_out(b, p):
                pe.wait_ge(ct_copied, b + 1)
                pe.wait_ge(v_ready, b + 2 if not isinstance(b, int) else min(b + 2, B))
                for j in range(2):
                    for g in range(G):
                        mm = nc.tensor.matmul(p_o[:, j, :], ct[:, g, T0[j]:T0[j] + TR], wo[:, g, :],
                                              start=(g == 0), stop=(g == G - 1))
                mm.then_inc(proj_done, 1)

            pipelined(pe, [first, project_in] + [spread_queries(i) for i in range(4)], second,
                      [context(0), context(1), project_out],
                      {0: [("third", 0)], 1: [("third", 1)], 3: [("third", 2)], 4: [("first", 0)],
                       5: [("first", 1)], 6: [("first", 2), ("first", 3)], 7: [("first", 4), ("first", 5)]})



NTILE = S // 128
CH = 4
NCH = NTILE // CH
E0 = 8
H0 = 768
M0 = H0 // 128
KEPT = 2 * S
E1 = 9
I1 = 96

PC = 256
NCHK = -(-(KEPT + 8 * (PC - 1) - PC + 1) // PC)
MAX_CH = -(-S // PC)
SLOTS = NCHK * PC // 128
ROUND = 1.5 * 2 ** 23


def in_pairs(eng, step):
    for p in range(2):
        step(p, p)
    with eng.Fori(1, NTILE // 2) as pair:
        for p in range(2):
            step(pair * 2 + p, p)
    step(NTILE - 1, 0)


def over_chunks(eng, step):
    step(0, CH)
    with eng.Fori(1, NCH) as i:
        step(i, CH)
    step(NCH, NTILE - NCH * CH)


@stage
def build_norm(nc, pre, h_in, ident_in, gate_in, t, n_gate):
    with ExitStack() as ctx:
        def sb(name, shape):
            return ctx.enter_context(nc.sbuf_tensor(pre + name, shape, F32))

        def sem(name):
            return nc.alloc_semaphore(name=pre + name)

        h, xt, logits, ident = t["h"], t.get("xt"), t["logits"], t["ident"]
        wg = sb("wg", [GF, G, n_gate])
        stats = sb("stats", [128, NTILE, 6])
        mean = sb("mean", [128, NTILE])
        gap = sb("gap", [128, NTILE])
        sq = sb("sq", [128, NTILE])
        var = sb("var", [128, NTILE])
        half = sb("half", [128, NTILE])
        rstd = sb("rstd", [128, NTILE])
        xn = [sb(f"xn{p}", [128, D]) for p in range(2)]
        xs = [sb(f"xs{p}", [GF, G, 128]) for p in range(2)]
        p_x = ctx.enter_context(nc.psum_tensor(pre + "p_x", [128, 2, 512], F32))
        p_l = ctx.enter_context(nc.psum_tensor(pre + "p_l", [128, 512], F32))

        loaded = sem("loaded")
        half_ready = sem("half_ready")
        stats_ready = sem("stats_ready")
        vec = sem("vec")
        var_ready = sem("var_ready")
        rstd_ready = sem("rstd_ready")
        xn_ready = sem("xn_ready")
        xt_done = sem("xt_done")
        xs_copied = sem("xs_copied")
        xt_copied = sem("xt_copied")
        row_copied = sem("row_copied")
        logits_done = sem("logits_done")
        block = ctx.enter_context(nc.Block())

        @block.sync
        def _(sp):
            sp.dma_start(h[:], h_in.rearrange("(t p) f -> p t f", p=128)).then_inc(loaded, 16)
            sp.dma_start(wg[:], gate_in).then_inc(loaded, 16)
            sp.dma_start(ident[:], ident_in).then_inc(loaded, 16)

        @block.gpsimd
        def _(pool):
            nc.gpsimd.memset(half[:], -0.5).then_inc(half_ready, 1)
            pool.wait_ge(half_ready, 1)
            pool.wait_ge(var_ready, 1)
            nc.gpsimd.tensor_tensor(rstd[:], var[:], half[:], ALU.pow).then_inc(rstd_ready, 1)

        @block.vector
        def _(dve):
            dve.wait_ge(loaded, 48)
            with dve.Fori(0, NTILE) as i:
                nc.vector.bn_stats(stats[:, bass.ds(i, 1), :].rearrange("p a s -> p (a s)"),
                                   h[:, bass.ds(i, 1), :].rearrange("p a f -> p (a f)")).then_inc(stats_ready, 1)
            dve.wait_ge(stats_ready, NTILE)
            nc.vector.tensor_tensor(mean[:], stats[:, :, 1], stats[:, :, 4], ALU.add).then_inc(vec, 1)
            nc.vector.tensor_tensor(gap[:], stats[:, :, 1], stats[:, :, 4], ALU.subtract).then_inc(vec, 1)
            nc.vector.tensor_tensor(var[:], stats[:, :, 2], stats[:, :, 5], ALU.add).then_inc(vec, 1)
            dve.wait_ge(vec, 3)
            nc.vector.tensor_scalar(mean[:], mean[:], 0.5, None, ALU.mult).then_inc(vec, 1)
            nc.vector.scalar_tensor_tensor(sq[:], gap[:], 0.25, gap[:], ALU.mult, ALU.mult).then_inc(vec, 1)
            nc.vector.tensor_scalar(var[:], var[:], 1.0 / D, EPS, ALU.mult, ALU.add).then_inc(vec, 1)
            dve.wait_ge(vec, 6)
            nc.vector.tensor_tensor(var[:], var[:], sq[:], ALU.add).then_inc(var_ready, 1)
            dve.wait_ge(rstd_ready, 1)

            def step(i, p):
                wait_reuse(dve, xt_done, i)
                nc.vector.tensor_scalar(xn[p][:], h[:, bass.ds(i, 1), :].rearrange("p a f -> p (a f)"),
                                        mean[:, bass.ds(i, 1)], rstd[:, bass.ds(i, 1)], ALU.subtract, ALU.mult
                                        ).then_inc(xn_ready, 1)
                dve.wait_ge(xn_ready, i + 1)
                nc.vector.tensor_copy(t["rows"][:, bass.ds(i, 1), 0:D].rearrange("p a f -> p (a f)"), xn[p][:]
                                      ).then_inc(row_copied, 1)
                if xt is not None:
                    dve.wait_ge(xs_copied, i + 1)
                    nc.vector.tensor_copy(xt[:, :, bass.ds(i * 128, 128)], xs[p][:]).then_inc(xt_copied, 1)

            in_pairs(dve, step)
            dve.wait_ge(logits_done, NTILE)
            nc.vector.tensor_copy(logits[:], p_l[:, 0:NTILE * n_gate].rearrange("p (t e) -> p t e", e=n_gate)
                                  ).then_inc(vec, 1)

        @block.scalar
        def _(act):
            def step(i, p):
                act.wait_ge(xt_done, i + 1)
                wait_reuse(act, logits_done, i)
                if xt is not None:
                    wait_reuse(act, xt_copied, i)
                nc.scalar.copy(xs[p][:], p_x[0:GF, p, 0:G * 128].rearrange("p (g t) -> p g t", g=G)
                               ).then_inc(xs_copied, 1)

            in_pairs(act, step)

        @block.tensor
        def _(pe):
            def step(i, p):
                pe.wait_ge(xn_ready, i + 1)
                wait_reuse(pe, xs_copied, i)
                for g in range(G):
                    mm = nc.tensor.transpose(p_x[0:GF, p, g * 128:(g + 1) * 128], xn[p][:, g * GF:(g + 1) * GF],
                                             ident[:])
                mm.then_inc(xt_done, 1)
                pe.wait_ge(xs_copied, i + 1)
                for g in range(G):
                    mm = nc.tensor.matmul(p_l[:, bass.ds(i * n_gate, n_gate)], xs[p][:, g, :], wg[:, g, :],
                                          start=(g == 0), stop=(g == G - 1))
                mm.then_inc(logits_done, 1)

            in_pairs(pe, step)


def expert_softmax(nc, dve, vec, at, exp_done, logits, shifted, stat, n):
    wide = [128, NTILE, n]
    nc.vector.tensor_reduce(stat[:], logits[:], AX, ALU.max).then_inc(vec, 1)
    dve.wait_ge(vec, at + 1)
    nc.vector.tensor_tensor(shifted[:], logits[:], stat[:].unsqueeze(2).broadcast_to(wide), ALU.subtract
                            ).then_inc(vec, 1)
    dve.wait_ge(exp_done, 1)
    nc.vector.reduce_sum(stat[:], shifted[:], AX).then_inc(vec, 1)
    dve.wait_ge(vec, at + 3)
    nc.vector.reciprocal(stat[:], stat[:]).then_inc(vec, 1)
    dve.wait_ge(vec, at + 4)
    nc.vector.tensor_tensor(logits[:], shifted[:], stat[:].unsqueeze(2).broadcast_to(wide), ALU.mult
                            ).then_inc(vec, 1)
    dve.wait_ge(vec, at + 5)
    return at + 5


@stage
def build_gate0(nc, c, t):
    with ExitStack() as ctx:
        def sb(name, shape, dt=F32):
            return ctx.enter_context(nc.sbuf_tensor("g0_" + name, shape, dt))

        def sem(name):
            return nc.alloc_semaphore(name="g0_" + name)

        NB = 30
        logits, gate = t["logits"], t["gate"]
        shifted = sb("shifted", [128, NTILE, E0])
        stat = sb("stat", [128, NTILE])
        score = sb("score", [128, E0, NTILE])
        above = sb("above", [128, E0, NTILE])
        ties = sb("ties", [128, E0, NTILE])
        tie_rank = sb("tie_rank", [128, E0 * NTILE])
        before = sb("before", [128, E0 * NTILE])
        room = sb("room", [128, 1])
        count = sb("count", [128, 1])
        bits = sb("bits", [128, NB], I32)
        bits_f = sb("bits_f", [128, NB])
        found = sb("found", [128, 1], I32)
        tried = sb("tried", [128, 1], I32)
        kept = sb("kept", [128, 1], I32)
        ones = sb("ones", [128, 128])
        lower = sb("lower", [128, 128])
        p_c = ctx.enter_context(nc.psum_tensor("g0_p_c", [128, 512], F32))
        p_r = ctx.enter_context(nc.psum_tensor("g0_p_r", [128, 512], F32))
        p_t = ctx.enter_context(nc.psum_tensor("g0_p_t", [128, 512], F32))

        loaded = sem("loaded")
        cleared = sem("cleared")
        vec = sem("vec")
        shift_done = sem("shift_done")
        exp_done = sem("exp_done")
        tried_ready = sem("tried_ready")
        counted = sem("counted")
        summed = sem("summed")
        kept_ready = sem("kept_ready")
        found_ready = sem("found_ready")
        masks_ready = sem("masks_ready")
        ranks_done = sem("ranks_done")
        block = ctx.enter_context(nc.Block())

        @block.sync
        def _(sp):
            for dst, src in ((bits[:], c["bits"]), (bits_f[:], c["bits_f"]), (ones[:], c["ones"]),
                             (lower[:], c["lower"])):
                sp.dma_start(dst, src).then_inc(loaded, 16)

        @block.scalar
        def _(act):
            act.wait_ge(vec, 2)
            nc.scalar.activation(shifted[:], shifted[:], ACT.Exp).then_inc(exp_done, 1)

        @block.vector
        def _(dve):
            dve.wait_ge(loaded, 64)
            at = expert_softmax(nc, dve, vec, 0, exp_done, logits, shifted, stat, E0)
            nc.vector.tensor_copy(score[:], logits[:].rearrange("p t e -> p e t")).then_inc(vec, 1)
            nc.vector.memset(found[:], 0).then_inc(vec, 1)
            dve.wait_ge(vec, at + 2)
            with dve.Fori(0, NB) as i:
                nc.vector.tensor_tensor(tried[:], found[:], bits[:, bass.ds(i, 1)], ALU.bitwise_or
                                        ).then_inc(tried_ready, 1)
                dve.wait_ge(tried_ready, i + 1)
                nc.vector.tensor_scalar(above[:], score[:], tried[:].bitcast(F32), 0.0, ALU.is_ge, ALU.add,
                                        accum_out=count[:]).then_inc(counted, 1)
                dve.wait_ge(summed, i + 1)
                nc.vector.tensor_scalar(kept[:], p_c[:, 0:1], float(KEPT), bits_f[:, bass.ds(i, 1)],
                                        ALU.is_ge, ALU.mult).then_inc(kept_ready, 1)
                dve.wait_ge(kept_ready, i + 1)
                nc.vector.tensor_tensor(found[:], found[:], kept[:], ALU.bitwise_or).then_inc(found_ready, 1)
                dve.wait_ge(found_ready, i + 1)
            nc.vector.tensor_scalar(above[:], score[:], found[:].bitcast(F32), 0.0, ALU.is_gt, ALU.add,
                                    accum_out=count[:]).then_inc(masks_ready, 1)
            nc.vector.tensor_scalar(ties[:], score[:], found[:].bitcast(F32), None, ALU.is_equal
                                    ).then_inc(masks_ready, 1)
            dve.wait_ge(ranks_done, 1)
            nc.vector.tensor_scalar(room[:], p_c[:, 1:2], -1.0, float(KEPT), ALU.mult, ALU.add).then_inc(vec, 1)
            nc.vector.tensor_copy(tie_rank[:], p_t[:, 0:E0 * NTILE]).then_inc(vec, 1)
            dve.wait_ge(vec, at + 4)
            nc.vector.tensor_tensor_scan(before[:], ones[:, 0:1].broadcast_to([128, E0 * NTILE]), tie_rank[:], 0.0,
                                         ALU.mult, ALU.add).then_inc(vec, 1)
            dve.wait_ge(vec, at + 5)
            nc.vector.tensor_tensor(before[:], before[:], tie_rank[:], ALU.subtract).then_inc(vec, 1)
            dve.wait_ge(vec, at + 6)
            nc.vector.tensor_tensor(tie_rank[:], p_r[:, 0:E0 * NTILE], before[:], ALU.add).then_inc(vec, 1)
            dve.wait_ge(vec, at + 7)
            nc.vector.scalar_tensor_tensor(before[:], tie_rank[:], room[:], ties[:].rearrange("p e t -> p (e t)"),
                                           ALU.is_lt, ALU.mult).then_inc(vec, 1)
            dve.wait_ge(vec, at + 8)
            nc.vector.tensor_tensor(above[:], above[:], before[:].rearrange("p (e t) -> p e t", e=E0), ALU.add
                                    ).then_inc(vec, 1)
            dve.wait_ge(vec, at + 9)
            nc.vector.tensor_tensor(gate[:], score[:].rearrange("p e t -> p t e"),
                                    above[:].rearrange("p e t -> p t e"), ALU.mult).then_inc(vec, 1)

        @block.tensor
        def _(pe):
            pe.wait_ge(loaded, 64)
            with pe.Fori(0, NB) as i:
                pe.wait_ge(counted, i + 1)
                nc.tensor.matmul(p_c[:, 0:1], ones[:], count[:], start=True, stop=True).then_inc(summed, 1)
            pe.wait_ge(masks_ready, 2)
            nc.tensor.matmul(p_c[:, 1:2], ones[:], count[:], start=True, stop=True)
            flat = ties[:].rearrange("p e t -> p (e t)")
            nc.tensor.matmul(p_r[:, 0:E0 * NTILE], lower[:], flat, start=True, stop=True)
            nc.tensor.matmul(p_t[:, 0:E0 * NTILE], ones[:], flat, start=True, stop=True).then_inc(ranks_done, 1)


@stage
def build_gate1(nc, c, t):
    with ExitStack() as ctx:
        def sb(name, shape, dt=F32):
            return ctx.enter_context(nc.sbuf_tensor("g1_" + name, shape, dt))

        def sem(name):
            return nc.alloc_semaphore(name="g1_" + name)

        E, GR = E1 - 1, (E1 - 1) // 2
        logits, gate = t["logits"], t["gate"]
        shifted = sb("shifted", [128, NTILE, E])
        stat = sb("stat", [128, NTILE])
        bias = sb("bias", [128, E])
        biased = sb("biased", [128, NTILE, E])
        group = sb("group", [128, NTILE, GR])
        out_of_group = sb("out_of_group", [128, NTILE, GR])
        earlier = sb("earlier", [128, E, E])
        better = sb("better", [128, NTILE, E, E])
        equal = sb("equal", [128, NTILE, E, E])
        rank = sb("rank", [128, NTILE, E])
        loaded = sem("loaded")
        vec = sem("vec")
        exp_done = sem("exp_done")
        block = ctx.enter_context(nc.Block())

        @block.sync
        def _(sp):
            sp.dma_start(bias[:], c["gate_b"].broadcast_to([128, E])).then_inc(loaded, 16)
            sp.dma_start(earlier[:], c["earlier"]).then_inc(loaded, 16)

        @block.scalar
        def _(act):
            act.wait_ge(vec, 2)
            nc.scalar.activation(shifted[:], shifted[:], ACT.Exp).then_inc(exp_done, 1)

        @block.vector
        def _(dve):
            steps = [0]

            def link(ins):
                steps[0] += 1
                ins.then_inc(vec, 1)
                dve.wait_ge(vec, steps[0])

            def ranks(x, n, out):
                a = better[:].rearrange("p t i j -> p t (i j)")[:, :, 0:n * n].rearrange("p t (i j) -> p t i j", i=n)
                q = equal[:].rearrange("p t i j -> p t (i j)")[:, :, 0:n * n].rearrange("p t (i j) -> p t i j", i=n)
                for i in range(n):
                    mine = x[:, :, i:i + 1].broadcast_to([128, NTILE, n])
                    nc.vector.tensor_tensor(a[:, :, i, :], x, mine, ALU.is_gt).then_inc(vec, 1)
                    nc.vector.tensor_tensor(q[:, :, i, :], x, mine, ALU.is_equal).then_inc(vec, 1)
                steps[0] += 2 * n
                dve.wait_ge(vec, steps[0])
                for i in range(n):
                    nc.vector.tensor_tensor(q[:, :, i, :], q[:, :, i, :],
                                            earlier[:, i:i + 1, 0:n].broadcast_to([128, NTILE, n]), ALU.mult
                                            ).then_inc(vec, 1)
                steps[0] += n
                dve.wait_ge(vec, steps[0])
                link(nc.vector.tensor_tensor(a, a, q, ALU.add))
                link(nc.vector.reduce_sum(out, a, AX))

            dve.wait_ge(loaded, 32)
            steps[0] = expert_softmax(nc, dve, vec, 0, exp_done, logits, shifted, stat, E)
            link(nc.vector.tensor_tensor(biased[:], logits[:], bias[:].unsqueeze(1).broadcast_to([128, NTILE, E]),
                                         ALU.add))
            link(nc.vector.tensor_tensor(group[:], biased[:, :, 0:E:2], biased[:, :, 1:E:2], ALU.add))
            ranks(group[:], GR, out_of_group[:])
            link(nc.vector.tensor_scalar(out_of_group[:], out_of_group[:], 2.0, -1e30, ALU.is_ge, ALU.mult))
            for i in range(2):
                link(nc.vector.tensor_tensor(biased[:, :, i:E:2], biased[:, :, i:E:2], out_of_group[:], ALU.add))
            ranks(biased[:], E, rank[:])
            link(nc.vector.tensor_scalar(rank[:], rank[:], 2.0, None, ALU.is_lt))
            link(nc.vector.tensor_tensor(gate[:, :, 0:E], logits[:], rank[:], ALU.mult))
            link(nc.vector.memset(gate[:, :, E:E1], 1.0))


@stage
def build_bias2(nc, pre, ne, b2_in, t):
    with ExitStack() as ctx:
        def sem(name):
            return nc.alloc_semaphore(name=pre + name)

        h, gate, ident = t["h"], t["gate"], t["ident"]
        b2 = ctx.enter_context(nc.sbuf_tensor(pre + "b2", [ne, D], F32))
        gate_s = [ctx.enter_context(nc.sbuf_tensor(f"{pre}gate_s{p}", [128, ne], F32)) for p in range(2)]
        gate_t = [ctx.enter_context(nc.sbuf_tensor(f"{pre}gate_t{p}", [ne, 128], F32)) for p in range(2)]
        p_g = ctx.enter_context(nc.psum_tensor(pre + "p_g", [128, 2, 512], F32))
        p_b = ctx.enter_context(nc.psum_tensor(pre + "p_b", [128, 2, 512], F32))
        loaded = sem("loaded")
        picked = sem("picked")
        turned = sem("turned")
        turned_copied = sem("turned_copied")
        bias_done = sem("bias_done")
        added = sem("added")
        block = ctx.enter_context(nc.Block())

        @block.sync
        def _(sp):
            sp.dma_start(b2[:], b2_in).then_inc(loaded, 16)

        @block.scalar
        def _(act):
            def step(i, p):
                wait_reuse(act, turned, i)
                nc.scalar.copy(gate_s[p][:], gate[:, bass.ds(i, 1), :].rearrange("p a e -> p (a e)")
                               ).then_inc(picked, 1)
                act.wait_ge(turned, i + 1)
                wait_reuse(act, bias_done, i)
                nc.scalar.copy(gate_t[p][:], p_g[0:ne, p, 0:128]).then_inc(turned_copied, 1)

            in_pairs(act, step)

        @block.tensor
        def _(pe):
            pe.wait_ge(loaded, 16)

            def step(i, p):
                pe.wait_ge(picked, i + 1)
                wait_reuse(pe, turned_copied, i)
                nc.tensor.transpose(p_g[0:ne, p, 0:128], gate_s[p][:], ident[:]).then_inc(turned, 1)
                pe.wait_ge(turned_copied, i + 1)
                wait_reuse(pe, added, i)
                nc.tensor.matmul(p_b[:, p, 0:D], gate_t[p][:], b2[:], start=True, stop=True).then_inc(bias_done, 1)

            in_pairs(pe, step)

        @block.vector
        def _(dve):
            def step(i, p):
                dve.wait_ge(bias_done, i + 1)
                at = h[:, bass.ds(i, 1), :].rearrange("p a f -> p (a f)")
                nc.vector.tensor_tensor(at, at, p_b[:, p, 0:D], ALU.add).then_inc(added, 1)

            in_pairs(dve, step)


@stage
def build_dispatch(nc, pre, w2_rows, c, t, h_out, rows):
    with ExitStack() as ctx:
        def sb(name, shape, dt=F32):
            return ctx.enter_context(nc.sbuf_tensor(pre + name, shape, dt))

        def sem(name):
            return nc.alloc_semaphore(name=pre + name)

        E, ET = 8, 8 * NTILE
        gate, table, chosen = t["gate"], t["table"], t["chosen"]
        lower = sb("lower", [128, 128])
        iota = sb("iota", [128, 128])
        part = sb("part", [128, 2])
        dummy = sb("dummy", [128, SLOTS])
        starts = sb("starts", [128, MAX_CH])
        ones = sb("ones", [128, 128])
        zeros = sb("zeros", [128, 2, D + 9])
        sel = sb("sel", [128, E, NTILE])
        tot = sb("tot", [128, ET])
        before = sb("before", [128, E, NTILE])
        cnt = sb("cnt", [128, E])
        above = sb("above", [128, E, MAX_CH])
        n_ch = sb("n_ch", [128, E])
        end_ch = sb("end_ch", [128, E])
        base = sb("base", [128, E])
        pos = sb("pos", [128, E, NTILE])
        near = sb("near", [128, E, NTILE])
        lo = sb("lo", [128, NTILE, E])
        hi = sb("hi", [128, NTILE, E])
        over = sb("over", [128, NCHK, E - 1])
        ch_expert = sb("ch_expert", [128, NCHK])
        lo_hot = [sb(f"lo_hot{p}", [128, E, 128], BF16) for p in range(2)]
        hi_hot = [sb(f"hi_hot{p}", [128, E, SLOTS], BF16) for p in range(2)]
        hi_val = [sb(f"hi_val{p}", [128, E, 2, SLOTS], BF16) for p in range(2)]
        listed_s = sb("listed_s", [128, 2, SLOTS])
        token = sb("token", [128, SLOTS])
        p_r = ctx.enter_context(nc.psum_tensor(pre + "p_r", [128, 512], F32))
        p_t = ctx.enter_context(nc.psum_tensor(pre + "p_t", [128, 512], F32))
        p_s = ctx.enter_context(nc.psum_tensor(pre + "p_s", [128, 512], F32))

        loaded = sem("loaded")
        cleared = sem("cleared")
        stored = sem("stored")
        vec = sem("vec")
        sel_ready = sem("sel_ready")
        counted = sem("counted")
        lo_ready = sem("lo_ready")
        hi_ready = sem("hi_ready")
        val_ready = sem("val_ready")
        listed = sem("listed")
        consts = [(lower[:], c["lower"]), (iota[:], c["iota"]), (part[:], c["part"]), (dummy[:], c["dummy"]),
                  (starts[:], c["starts"])]
        block = ctx.enter_context(nc.Block())

        @block.sync
        def _(sp):
            for dst, src in consts:
                sp.dma_start(dst, src).then_inc(loaded, 16)
            sp.dma_start(rows[0:S, :].rearrange("(t p) f -> p t f", p=128), t["rows"][:]).then_inc(stored, 16)
            sp.dma_start(h_out[0:S, :].rearrange("(t p) f -> p t f", p=128), t["h"][:]).then_inc(stored, 16)
            sp.wait_ge(cleared, 2)
            sp.dma_start(rows[S:S + 256, :].rearrange("(t p) f -> p t f", p=128), zeros[:, :, 0:rows.shape[1]]
                         ).then_inc(stored, 16)
            sp.dma_start(h_out[S:S + 256, :].rearrange("(t p) f -> p t f", p=128), zeros[:, :, 0:D]
                         ).then_inc(stored, 16)
            sp.wait_ge(stored, 64)

        @block.gpsimd
        def _(pool):
            nc.gpsimd.memset(ones[:], 1.0).then_inc(cleared, 1)
            nc.gpsimd.memset(zeros[:], 0.0).then_inc(cleared, 1)

        @block.vector
        def _(dve):
            steps = [0]

            def link(ins):
                steps[0] += 1
                ins.then_inc(vec, 1)
                dve.wait_ge(vec, steps[0])

            nc.vector.tensor_scalar(sel[:], gate[:, :, 0:E].rearrange("p t e -> p e t"), 0.0, None, ALU.is_gt
                                    ).then_inc(sel_ready, 1)
            dve.wait_ge(loaded, 16 * len(consts))
            dve.wait_ge(cleared, 2)
            dve.wait_ge(counted, 1)
            link(nc.vector.tensor_copy(tot[:], p_t[:, 0:ET]))
            flat = before[:].rearrange("p e t -> p (e t)")
            link(nc.vector.tensor_tensor_scan(flat, ones[:, 0:1].broadcast_to([128, ET]), tot[:], 0.0,
                                              ALU.mult, ALU.add))
            link(nc.vector.tensor_tensor(flat, flat, tot[:], ALU.subtract))
            link(nc.vector.reduce_sum(cnt[:], tot[:].rearrange("p (e t) -> p e t", e=E), AX))
            link(nc.vector.tensor_tensor(above[:], cnt[:].unsqueeze(2).broadcast_to([128, E, MAX_CH]),
                                         starts[:].unsqueeze(1).broadcast_to([128, E, MAX_CH]), ALU.is_gt))
            link(nc.vector.reduce_sum(n_ch[:], above[:], AX))
            link(nc.vector.tensor_tensor_scan(end_ch[:], ones[:, 0:E], n_ch[:], 0.0, ALU.mult, ALU.add))
            link(nc.vector.tensor_tensor(base[:], end_ch[:], n_ch[:], ALU.subtract))
            link(nc.vector.scalar_tensor_tensor(base[:], base[:], float(PC), before[:, :, 0], ALU.mult, ALU.subtract))
            link(nc.vector.tensor_tensor(pos[:], p_r[:, 0:ET].rearrange("p (e t) -> p e t", e=E), before[:], ALU.add))
            link(nc.vector.tensor_tensor(pos[:], pos[:], base[:].unsqueeze(2).broadcast_to([128, E, NTILE]), ALU.add))
            link(nc.vector.tensor_scalar(near[:], pos[:], 1.0 / 128, -63.5 / 128, ALU.mult, ALU.add))
            link(nc.vector.tensor_scalar(near[:], near[:], ROUND, None, ALU.add))
            link(nc.vector.tensor_scalar(near[:], near[:], -ROUND, None, ALU.add))
            link(nc.vector.scalar_tensor_tensor(lo[:].rearrange("p t e -> p e t"), near[:], -128.0, pos[:],
                                                ALU.mult, ALU.add))
            link(nc.vector.scalar_tensor_tensor(near[:], sel[:], -1000.0, near[:], ALU.mult, ALU.add))
            link(nc.vector.tensor_scalar(hi[:].rearrange("p t e -> p e t"), near[:], 1000.0, None, ALU.add))
            link(nc.vector.tensor_tensor(over[:], iota[:, 0:NCHK].unsqueeze(2).broadcast_to([128, NCHK, E - 1]),
                                         end_ch[:, 0:E - 1].unsqueeze(1).broadcast_to([128, NCHK, E - 1]), ALU.is_ge))
            link(nc.vector.reduce_sum(ch_expert[:], over[:], AX))
            for at, n in ((2, GF), (3, w2_rows)):
                link(nc.vector.tensor_scalar(table[:, :, at], ch_expert[:], float(n), part[:, 0:1], ALU.mult, ALU.add))
            link(nc.vector.tensor_tensor(chosen[:], ch_expert[:].unsqueeze(2).broadcast_to([128, NCHK, E]),
                                         iota[:, 0:E].unsqueeze(1).broadcast_to([128, NCHK, E]), ALU.is_equal))

            def step(i, p):
                wait_reuse(dve, listed, i - 1)
                for hot, x, n, ready in ((hi_hot, hi, SLOTS, hi_ready), (lo_hot, lo, 128, lo_ready)):
                    nc.vector.tensor_tensor(
                        hot[p][:], iota[:, 0:n].unsqueeze(1).broadcast_to([128, E, n]),
                        x[:, bass.ds(i, 1), :].rearrange("p a e -> p (a e)").unsqueeze(2).broadcast_to([128, E, n]),
                        ALU.is_equal).then_inc(ready, 1)

            in_pairs(dve, step)
            dve.wait_ge(listed, NTILE)
            link(nc.vector.tensor_copy(listed_s[:], p_s[:, 0:2 * SLOTS].rearrange("p (v s) -> p v s", v=2)))
            link(nc.vector.scalar_tensor_tensor(token[:], listed_s[:, 1, :], 128.0, listed_s[:, 0, :],
                                                ALU.mult, ALU.add))
            link(nc.vector.scalar_tensor_tensor(token[:], token[:], -1.0, dummy[:], ALU.add, ALU.subtract))
            link(nc.vector.scalar_tensor_tensor(token[:], listed_s[:, 0, :], 0.0, token[:], ALU.is_gt, ALU.mult))
            link(nc.vector.tensor_tensor(table[:, :, 0:2], token[:].rearrange("p (c a) -> p c a", a=2),
                                         dummy[:].rearrange("p (c a) -> p c a", a=2), ALU.add))

        @block.scalar
        def _(act):
            act.wait_ge(loaded, 16 * len(consts))

            def step(i, p):
                act.wait_ge(hi_ready, i + 1)
                wait_reuse(act, listed, i - 1)
                nc.scalar.activation(hi_val[p][:, :, 0, :], hi_hot[p][:], ACT.Copy, scale=part[:, 1:2]
                                     ).then_inc(val_ready, 1)
                nc.scalar.activation(hi_val[p][:, :, 1, :], hi_hot[p][:], ACT.Copy, scale=iota[:, bass.ds(i, 1)]
                                     ).then_inc(val_ready, 1)

            in_pairs(act, step)

        @block.tensor
        def _(pe):
            pe.wait_ge(loaded, 16 * len(consts))
            pe.wait_ge(cleared, 2)
            pe.wait_ge(sel_ready, 1)
            flat = sel[:].rearrange("p e t -> p (e t)")
            nc.tensor.matmul(p_r[:, 0:ET], lower[:], flat, start=True, stop=True)
            nc.tensor.matmul(p_t[:, 0:ET], ones[:], flat, start=True, stop=True).then_inc(counted, 1)

            def step(i, p):
                pe.wait_ge(lo_ready, i + 1)
                pe.wait_ge(val_ready, 2 * i + 2)
                for e in range(E):
                    mm = nc.tensor.matmul(p_s[:, 0:2 * SLOTS], lo_hot[p][:, e, :],
                                          hi_val[p][:, e, :, :].rearrange("p v s -> p (v s)"),
                                          start=(isinstance(i, int) and i == 0 and e == 0),
                                          stop=(isinstance(i, int) and i == NTILE - 1 and e == E - 1))
                mm.then_inc(listed, 1)

            in_pairs(pe, step)


def ahead(i, s, n):
    i, s = i + (s + n) // 4, (s + n) % 4
    return None if isinstance(i, int) and 4 * i + s >= NCHK else (i, s)


def in_fours(eng, step):
    for s in range(4):
        step(0, s)
    with eng.Fori(1, NCHK // 4 - 1) as i:
        for s in range(4):
            step(i, s)
    for s in range(4):
        step(NCHK // 4 - 1, s)


@stage
def build_sparse0(nc, c, t, rows, h_out):
    with ExitStack() as ctx:
        def sb(name, shape, dt=F32):
            return ctx.enter_context(nc.sbuf_tensor("s0_" + name, shape, dt))

        def sem(name):
            return nc.alloc_semaphore(name="s0_" + name)

        NR = 3
        RW = rows.shape[1]
        table, chosen = t["table"], t["chosen"]
        w1_rows, w2_rows = c["w1"], c["w2"]
        at = [sb(f"at{s}", [128, 4], I32) for s in range(4)]
        x = [[sb(f"x{s}{a}", [128, RW]) for a in range(2)] for s in range(4)]
        w1 = [sb(f"w1{s}", [GF, G * H0]) for s in range(4)]
        w2 = [sb(f"w2{s}", [128, M0 * D + M0]) for s in range(4)]
        xt = [sb(f"xt{s}", [GF, G, PC]) for s in range(2)]
        hid = [sb(f"hid{k}", [128, PC]) for k in range(NR)]
        one = sb("one", [128, 1])
        carrier = sb("carrier", [128, 2])
        picked = sb("picked", [128, 2, E0])
        gate_s = [sb(f"gate_s{s}", [128, 2]) for s in range(4)]
        y = [[sb(f"y{s}{a}", [128, D]) for a in range(2)] for s in range(4)]
        p_x = ctx.enter_context(nc.psum_tensor("s0_p_x", [128, 512], F32))
        p_h = ctx.enter_context(nc.psum_tensor("s0_p_h", [128, 2, 512], F32))
        p_y = ctx.enter_context(nc.psum_tensor("s0_p_y", [128, 2, 512], F32))
        p_xt = p_x[0:GF, 0:G * PC].rearrange("p (g t) -> p g t", g=G)

        one_ready = sem("one_ready")
        at_ready = sem("at_ready")
        carried = [sem("gather_carried"), sem("scatter_carried")]
        x_in = [sem(f"x_in{s}") for s in range(4)]
        w1_in = [sem(f"w1_in{s}") for s in range(4)]
        w2_in = [sem(f"w2_in{s}") for s in range(4)]
        turned = sem("turned")
        xt_copied = sem("xt_copied")
        picked_ready = sem("picked_ready")
        gate_ready = sem("gate_ready")
        first_done = sem("first_done")
        gelu_done = sem("gelu_done")
        second_done = sem("second_done")
        y_ready = sem("y_ready")
        scattered = sem("scattered")
        block = ctx.enter_context(nc.Block())

        @block.gpsimd
        def _(pool):
            nc.gpsimd.memset(one[:], 1.0).then_inc(one_ready, 1)
            pool.wait_ge(one_ready, 1)

            def carry(k, ch):
                wait_reuse(pool, carried[k], ch)
                nc.gpsimd.tensor_tensor(carrier[:, k:k + 1], one[:], one[:], ALU.mult).then_inc(carried[k], 1)

            def gather(i, s):
                ch = 4 * i + s
                pool.wait_ge(at_ready, ch + 1)
                carry(0, ch)
                for a in range(2):
                    nc.gpsimd.indirect_dma_start(x[s][a][:], None, rows[:, :],
                                                 bass.IndirectOffsetOnAxis(ap=at[s][:, a:a + 1], axis=0)
                                                 ).then_inc(x_in[s], 16)
                nc.gpsimd.indirect_dma_start(w1[s][:], None, w1_rows[:, :],
                                             bass.IndirectOffsetOnAxis(ap=at[s][0:GF, 2:3], axis=0)
                                             ).then_inc(w1_in[s], 16)
                nc.gpsimd.indirect_dma_start(w2[s][:], None, w2_rows[:, :],
                                             bass.IndirectOffsetOnAxis(ap=at[s][:, 3:4], axis=0)
                                             ).then_inc(w2_in[s], 16)

            def step(i, s):
                ch = 4 * i + s
                pool.wait_ge(y_ready, ch + 1)
                wait_reuse(pool, scattered, 32 * ch)
                carry(1, ch)
                for a in range(2):
                    nc.gpsimd.indirect_dma_start(h_out[:, :],
                                                 bass.IndirectOffsetOnAxis(ap=at[s][:, a:a + 1], axis=0),
                                                 y[s][a][:], None, compute_op=ALU.add).then_inc(scattered, 16)
                nxt = ahead(i, s, 3)
                if nxt:
                    gather(*nxt)

            for s in range(3):
                gather(0, s)
            in_fours(pool, step)
            pool.wait_ge(scattered, 32 * NCHK)

        @block.vector
        def _(dve):
            def indices(i, s):
                wait_reuse(dve, scattered, 32 * (4 * i + s - 3))
                nc.vector.tensor_copy(at[s][:], table[:, bass.ds(4 * i + s, 1), :].rearrange("p a k -> p (a k)")
                                      ).then_inc(at_ready, 1)

            def copy_xt(i, s):
                dve.wait_ge(turned, 4 * i + s + 1)
                nc.vector.tensor_copy(xt[s % 2][:], p_xt).then_inc(xt_copied, 1)

            def step(i, s):
                ch = 4 * i + s
                nxt = ahead(i, s, 3)
                if nxt:
                    indices(*nxt)
                dve.wait_ge(x_in[s], 32 * i + 32)
                for a in range(2):
                    nc.vector.tensor_tensor(picked[:, a, :], x[s][a][:, D:D + E0],
                                            chosen[:, bass.ds(ch, 1), :].rearrange("p a e -> p (a e)"), ALU.mult
                                            ).then_inc(picked_ready, 1)
                dve.wait_ge(picked_ready, 2 * ch + 2)
                nc.vector.reduce_sum(gate_s[s][:], picked[:], AX).then_inc(gate_ready, 1)
                nxt = ahead(i, s, 1)
                if nxt:
                    copy_xt(*nxt)
                dve.wait_ge(gate_ready, ch + 1)
                dve.wait_ge(second_done, M0 * ch + M0)
                for a in range(2):
                    v = nc.vector.tensor_scalar(y[s][a][:], p_y[:, s % 2, a * D:(a + 1) * D], gate_s[s][:, a:a + 1], None,
                                                ALU.mult)
                v.then_inc(y_ready, 1)

            for s in range(3):
                indices(0, s)
            copy_xt(0, 0)
            in_fours(dve, step)

        @block.scalar
        def _(act):
            def step(i, s):
                ch = 4 * i + s
                act.wait_ge(w2_in[s], 16 * i + 16)
                for k in range(M0):
                    act.wait_ge(first_done, M0 * ch + k + 1)
                    wait_reuse(act, second_done, M0 * ch + k - NR + 1)
                    nc.scalar.activation(hid[k % NR][:], p_h[:, k % 2, 0:PC], ACT.Gelu_apprx_tanh,
                                         bias=w2[s][:, M0 * D + k:M0 * D + k + 1]).then_inc(gelu_done, 1)

            in_fours(act, step)

        @block.tensor
        def _(pe):
            def turn(i, s):
                pe.wait_ge(x_in[s], 32 * i + 32)
                wait_reuse(pe, xt_copied, 4 * i + s)
                for a in range(2):
                    for g in range(G):
                        mm = nc.tensor.transpose(p_xt[:, g, a * 128:(a + 1) * 128], x[s][a][:, g * GF:(g + 1) * GF],
                                                 t["ident"][:])
                mm.then_inc(turned, 1)

            def first(i, s, k):
                ch = 4 * i + s
                if k == 0:
                    pe.wait_ge(xt_copied, ch + 1)
                    pe.wait_ge(w1_in[s], 16 * i + 16)
                wait_reuse(pe, gelu_done, M0 * ch + k - 1)
                for g in range(G):
                    mm = nc.tensor.matmul(p_h[:, k % 2, 0:PC], w1[s][:, g * H0 + k * 128:g * H0 + (k + 1) * 128],
                                          xt[s % 2][:, g, :], start=(g == 0), stop=(g == G - 1))
                mm.then_inc(first_done, 1)

            def second(i, s, k):
                ch = 4 * i + s
                if k == 0:
                    pe.wait_ge(w2_in[s], 16 * i + 16)
                    wait_reuse(pe, y_ready, ch - 1)
                pe.wait_ge(gelu_done, M0 * ch + k + 1)
                for a in range(2):
                    mm = nc.tensor.matmul(p_y[:, s % 2, a * D:(a + 1) * D], hid[k % NR][:, a * 128:(a + 1) * 128],
                                          w2[s][:, k * D:(k + 1) * D], start=(k == 0 and a == 0), stop=(k == M0 - 1),
                                          skip_group_check=True)
                mm.then_inc(second_done, 1)

            def step(i, s):
                nxt = ahead(i, s, 1)
                for k in range(M0):
                    if k + 1 < M0:
                        first(i, s, k + 1)
                    elif nxt:
                        first(*nxt, 0)
                    second(i, s, k)
                    if k == 2 and nxt:
                        turn(*nxt)

            turn(0, 0)
            first(0, 0, 0)
            in_fours(pe, step)


@stage
def build_sparse1(nc, c, t, rows, h_out):
    with ExitStack() as ctx:
        def sb(name, shape, dt=F32):
            return ctx.enter_context(nc.sbuf_tensor("s1_" + name, shape, dt))

        def sem(name):
            return nc.alloc_semaphore(name="s1_" + name)

        E = E1 - 1
        W2, B13 = G * 4 * I1, G * 4 * I1 + D
        ALPHA, LIMIT = 1.702, 7.0
        RW = rows.shape[1]
        table, chosen = t["table"], t["chosen"]
        w_rows = c["w"]
        at = [sb(f"at{s}", [128, 4], I32) for s in range(4)]
        x = [[sb(f"x{s}{a}", [128, RW]) for a in range(2)] for s in range(4)]
        w = [sb(f"w{s}", [GF, B13 + 4]) for s in range(4)]
        xt = [sb(f"xt{s}", [GF, G, PC]) for s in range(2)]
        h3 = sb("h3", [I1, 2, PC])
        prod = sb("prod", [I1, 2, PC])
        lin = sb("lin", [I1, PC])
        xg = sb("xg", [I1, PC])
        xl = sb("xl", [I1, PC])
        sg = sb("sg", [I1, PC])
        act_t = [sb(f"act_t{p}", [I1, PC]) for p in range(2)]
        one = sb("one", [128, 1])
        carrier = sb("carrier", [128, 2])
        picked = sb("picked", [128, 2, E])
        gate_s = [sb(f"gate_s{s}", [128, 2]) for s in range(4)]
        y = [[sb(f"y{s}{a}", [128, D]) for a in range(2)] for s in range(4)]
        p_x = ctx.enter_context(nc.psum_tensor("s1_p_x", [128, 512], F32))
        p_h = ctx.enter_context(nc.psum_tensor("s1_p_h", [128, 2, 4, PC], F32))
        p_y = ctx.enter_context(nc.psum_tensor("s1_p_y", [128, 2, 512], F32))
        p_xt = p_x[0:GF, 0:G * PC].rearrange("p (g t) -> p g t", g=G)

        one_ready = sem("one_ready")
        at_ready = sem("at_ready")
        carried = [sem("gather_carried"), sem("scatter_carried")]
        x_in = [sem(f"x_in{s}") for s in range(4)]
        w_in = [sem(f"w_in{s}") for s in range(4)]
        turned = sem("turned")
        xt_copied = sem("xt_copied")
        picked_ready = sem("picked_ready")
        gate_ready = sem("gate_ready")
        h3_done = sem("h3_done")
        h1_done = sem("h1_done")
        h3_copied = sem("h3_copied")
        prod_ready = sem("prod_ready")
        xg_ready = sem("xg_ready")
        xl_ready = sem("xl_ready")
        sg_ready = sem("sg_ready")
        lin_ready = sem("lin_ready")
        act_ready = sem("act_ready")
        second_done = sem("second_done")
        y_ready = sem("y_ready")
        scattered = sem("scattered")
        block = ctx.enter_context(nc.Block())

        @block.gpsimd
        def _(pool):
            nc.gpsimd.memset(one[:], 1.0).then_inc(one_ready, 1)
            pool.wait_ge(one_ready, 1)

            def carry(k, ch):
                wait_reuse(pool, carried[k], ch)
                nc.gpsimd.tensor_tensor(carrier[:, k:k + 1], one[:], one[:], ALU.mult).then_inc(carried[k], 1)

            def gather(i, s):
                ch = 4 * i + s
                pool.wait_ge(at_ready, ch + 1)
                carry(0, ch)
                for a in range(2):
                    nc.gpsimd.indirect_dma_start(x[s][a][:], None, rows[:, :],
                                                 bass.IndirectOffsetOnAxis(ap=at[s][:, a:a + 1], axis=0)
                                                 ).then_inc(x_in[s], 16)
                nc.gpsimd.indirect_dma_start(w[s][:], None, w_rows[:, :],
                                             bass.IndirectOffsetOnAxis(ap=at[s][0:GF, 2:3], axis=0)
                                             ).then_inc(w_in[s], 16)

            def step(i, s):
                ch = 4 * i + s
                pool.wait_ge(y_ready, ch + 1)
                wait_reuse(pool, scattered, 32 * ch)
                carry(1, ch)
                for a in range(2):
                    nc.gpsimd.indirect_dma_start(h_out[:, :],
                                                 bass.IndirectOffsetOnAxis(ap=at[s][:, a:a + 1], axis=0),
                                                 y[s][a][:], None, compute_op=ALU.add).then_inc(scattered, 16)
                nxt = ahead(i, s, 3)
                if nxt:
                    gather(*nxt)

            for s in range(3):
                gather(0, s)
            in_fours(pool, step)
            pool.wait_ge(scattered, 32 * NCHK)

        @block.vector
        def _(dve):
            def indices(i, s):
                wait_reuse(dve, scattered, 32 * (4 * i + s - 3))
                nc.vector.tensor_copy(at[s][:], table[:, bass.ds(4 * i + s, 1), :].rearrange("p a k -> p (a k)")
                                      ).then_inc(at_ready, 1)

            def swiglu(i, s):
                ch = 4 * i + s
                dve.wait_ge(w_in[s], 16 * i + 16)
                dve.wait_ge(h1_done, ch + 1)
                dve.wait_ge(h3_copied, 2 * ch + 2)
                for o in range(2):
                    nc.vector.scalar_tensor_tensor(prod[:, o, :], p_h[0:I1, s % 2, o, :], w[s][:, B13 + o:B13 + o + 1],
                                                   h3[:, o, :], ALU.add, ALU.mult).then_inc(prod_ready, 1)
                dve.wait_ge(prod_ready, 2 * ch + 2)
                wait_reuse(dve, sg_ready, ch)
                nc.vector.tensor_scalar(xg[:], prod[:, 0, :], LIMIT, None, ALU.min).then_inc(xg_ready, 1)
                nc.vector.tensor_scalar(xl[:], prod[:, 1, :], -LIMIT, LIMIT, ALU.max, ALU.min).then_inc(xl_ready, 1)
                dve.wait_ge(xg_ready, ch + 1)
                dve.wait_ge(xl_ready, ch + 1)
                nc.vector.scalar_tensor_tensor(lin[:], xl[:], 1.0, xg[:], ALU.add, ALU.mult).then_inc(lin_ready, 1)
                dve.wait_ge(lin_ready, ch + 1)
                dve.wait_ge(sg_ready, ch + 1)
                wait_reuse(dve, second_done, ch - 1)
                nc.vector.tensor_tensor(act_t[s % 2][:], lin[:], sg[:], ALU.mult).then_inc(act_ready, 1)

            def step(i, s):
                ch = 4 * i + s
                nxt = ahead(i, s, 3)
                if nxt:
                    indices(*nxt)
                dve.wait_ge(x_in[s], 32 * i + 32)
                for a in range(2):
                    nc.vector.tensor_tensor(picked[:, a, :], x[s][a][:, D:D + E],
                                            chosen[:, bass.ds(ch, 1), :].rearrange("p a e -> p (a e)"), ALU.mult
                                            ).then_inc(picked_ready, 1)
                dve.wait_ge(picked_ready, 2 * ch + 2)
                nc.vector.reduce_sum(gate_s[s][:], picked[:], AX).then_inc(gate_ready, 1)
                nxt = ahead(i, s, 1)
                if nxt:
                    swiglu(*nxt)
                dve.wait_ge(gate_ready, ch + 1)
                dve.wait_ge(second_done, ch + 1)
                for a in range(2):
                    v = nc.vector.tensor_scalar(y[s][a][:], p_y[:, s % 2, a * D:(a + 1) * D], gate_s[s][:, a:a + 1], None,
                                                ALU.mult)
                v.then_inc(y_ready, 1)

            for s in range(3):
                indices(0, s)
            swiglu(0, 0)
            in_fours(dve, step)

        @block.scalar
        def _(act):
            def copy_xt(i, s):
                act.wait_ge(turned, 4 * i + s + 1)
                nc.scalar.copy(xt[s % 2][:], p_xt).then_inc(xt_copied, 1)

            def step(i, s):
                ch = 4 * i + s
                act.wait_ge(w_in[s], 16 * i + 16)
                act.wait_ge(h3_done, ch + 1)
                wait_reuse(act, prod_ready, 2 * ch)
                for o in range(2):
                    nc.scalar.activation(h3[:, o, :], p_h[0:I1, s % 2, 2 + o, :], ACT.Identity,
                                         bias=w[s][:, B13 + 2 + o:B13 + 3 + o]).then_inc(h3_copied, 1)
                nxt = ahead(i, s, 1)
                if nxt:
                    copy_xt(*nxt)
                act.wait_ge(xg_ready, ch + 1)
                wait_reuse(act, act_ready, ch)
                nc.scalar.activation(sg[:], xg[:], ACT.Sigmoid, scale=ALPHA).then_inc(sg_ready, 1)

            copy_xt(0, 0)
            in_fours(act, step)

        @block.tensor
        def _(pe):
            def turn(i, s):
                pe.wait_ge(x_in[s], 32 * i + 32)
                wait_reuse(pe, xt_copied, 4 * i + s)
                for a in range(2):
                    for g in range(G):
                        mm = nc.tensor.transpose(p_xt[:, g, a * 128:(a + 1) * 128], x[s][a][:, g * GF:(g + 1) * GF],
                                                 t["ident"][:])
                mm.then_inc(turned, 1)

            def first(i, s):
                ch = 4 * i + s
                pe.wait_ge(xt_copied, ch + 1)
                pe.wait_ge(w_in[s], 16 * i + 16)
                for half, done in ((2, h3_done), (0, h1_done)):
                    if half == 2:
                        wait_reuse(pe, h3_copied, 2 * (ch - 1))
                    else:
                        wait_reuse(pe, prod_ready, 2 * (ch - 1))
                    for o in range(half, half + 2):
                        for g in range(G):
                            mm = nc.tensor.matmul(p_h[0:I1, s % 2, o, :], w[s][:, (g * 4 + o) * I1:(g * 4 + o + 1) * I1],
                                                  xt[s % 2][:, g, :], start=(g == 0), stop=(g == G - 1),
                                                  skip_group_check=True)
                    mm.then_inc(done, 1)

            def second(i, s):
                ch = 4 * i + s
                wait_reuse(pe, y_ready, ch - 1)
                pe.wait_ge(act_ready, ch + 1)
                for a in range(2):
                    mm = nc.tensor.matmul(p_y[:, s % 2, a * D:(a + 1) * D], act_t[s % 2][:, a * 128:(a + 1) * 128],
                                          w[s][:, W2:W2 + D], start=True, stop=True)
                mm.then_inc(second_done, 1)

            def step(i, s):
                nxt = ahead(i, s, 1)
                if nxt:
                    first(*nxt)
                nxt = ahead(i, s, 2)
                if nxt:
                    turn(*nxt)
                second(i, s)

            turn(0, 0)
            first(0, 0)
            turn(0, 1)
            in_fours(pe, step)


@stage
def build_shared(nc, c, t, h_acc, h_out):
    with ExitStack() as ctx:
        def sb(name, shape):
            return ctx.enter_context(nc.sbuf_tensor("sh_" + name, shape, F32))

        def sem(name):
            return nc.alloc_semaphore(name="sh_" + name)

        ALPHA, LIMIT = 1.702, 7.0
        N = CH * 128
        xt = t["xt"]
        h = sb("h", [128, NTILE, D])
        w13 = sb("w13", [GF, G, 4, I1])
        w2 = sb("w2", [I1, D])
        b13 = sb("b13", [I1, 4])
        h3 = sb("h3", [I1, 2, N])
        prod = sb("prod", [I1, 2, N])
        lin = sb("lin", [I1, N])
        xg = sb("xg", [I1, N])
        sg = sb("sg", [I1, N])
        xl = sb("xl", [I1, N])
        act_t = sb("act_t", [I1, N])
        p_h = ctx.enter_context(nc.psum_tensor("sh_p_h", [128, 4, 512], F32))
        p_y = ctx.enter_context(nc.psum_tensor("sh_p_y", [128, 2, 512], F32))

        w_in = sem("w_in")
        h_in = sem("h_in")
        h3_done = sem("h3_done")
        h1_done = sem("h1_done")
        h3_copied = sem("h3_copied")
        prod_ready = sem("prod_ready")
        xg_ready = sem("xg_ready")
        sg_ready = sem("sg_ready")
        xl_ready = sem("xl_ready")
        lin_ready = sem("lin_ready")
        act_ready = sem("act_ready")
        second_done = sem("second_done")
        added = sem("added")
        stored = sem("stored")
        block = ctx.enter_context(nc.Block())

        @block.sync
        def _(sp):
            for dst, src in ((w13[:], c["shared_w13"]), (w2[:], c["shared_w2"]), (b13[:], c["shared_b13"])):
                sp.dma_start(dst, src).then_inc(w_in, 16)

            def load(i, n):
                wait_reuse(sp, h_in, 16 * i)
                sp.dma_start(h[:, bass.ds(i * CH, n), :],
                             h_acc[0:S, :].rearrange("(t p) f -> p t f", p=128)[:, bass.ds(i * CH, n), :]
                             ).then_inc(h_in, 16)

            def store(i, n):
                sp.wait_ge(added, i + 1)
                sp.dma_start(h_out.rearrange("(t p) f -> p t f", p=128)[:, bass.ds(i * CH, n), :],
                             h[:, bass.ds(i * CH, n), :]).then_inc(stored, 16)

            over_chunks(sp, load)
            over_chunks(sp, store)
            sp.wait_ge(stored, 16 * (NCH + 1))

        @block.scalar
        def _(act):
            act.wait_ge(w_in, 48)

            def step(i, n):
                w = n * 128
                act.wait_ge(h3_done, i + 1)
                wait_reuse(act, prod_ready, 2 * i)
                for o in range(2):
                    nc.scalar.activation(h3[:, o, 0:w], p_h[0:I1, 2 + o, 0:w], ACT.Identity,
                                         bias=b13[:, 2 + o:3 + o]).then_inc(h3_copied, 1)
                act.wait_ge(xg_ready, i + 1)
                wait_reuse(act, act_ready, i)
                nc.scalar.activation(sg[:, 0:w], xg[:, 0:w], ACT.Sigmoid, scale=ALPHA).then_inc(sg_ready, 1)

            over_chunks(act, step)

        @block.vector
        def _(dve):
            dve.wait_ge(w_in, 48)

            def step(i, n):
                w = n * 128
                dve.wait_ge(h1_done, i + 1)
                dve.wait_ge(h3_copied, 2 * i + 2)
                for o in range(2):
                    nc.vector.scalar_tensor_tensor(prod[:, o, 0:w], p_h[0:I1, o, 0:w], b13[:, o:o + 1],
                                                   h3[:, o, 0:w], ALU.add, ALU.mult).then_inc(prod_ready, 1)
                dve.wait_ge(prod_ready, 2 * i + 2)
                wait_reuse(dve, sg_ready, i)
                nc.vector.tensor_scalar(xg[:, 0:w], prod[:, 0, 0:w], LIMIT, None, ALU.min).then_inc(xg_ready, 1)
                nc.vector.tensor_scalar(xl[:, 0:w], prod[:, 1, 0:w], -LIMIT, LIMIT, ALU.max, ALU.min
                                        ).then_inc(xl_ready, 1)
                dve.wait_ge(xl_ready, i + 1)
                dve.wait_ge(xg_ready, i + 1)
                nc.vector.scalar_tensor_tensor(lin[:, 0:w], xl[:, 0:w], 1.0, xg[:, 0:w], ALU.add, ALU.mult
                                               ).then_inc(lin_ready, 1)
                dve.wait_ge(lin_ready, i + 1)
                dve.wait_ge(sg_ready, i + 1)
                wait_reuse(dve, second_done, i)
                nc.vector.tensor_tensor(act_t[:, 0:w], lin[:, 0:w], sg[:, 0:w], ALU.mult).then_inc(act_ready, 1)
                dve.wait_ge(h_in, 16 * i + 16)
                dve.wait_ge(second_done, i + 1)
                for a in range(n):
                    at = h[:, bass.ds(i * CH + a, 1), :].rearrange("p a f -> p (a f)")
                    v = nc.vector.tensor_tensor(at, at, p_y[:, a // 2, (a % 2) * D:(a % 2 + 1) * D], ALU.add)
                v.then_inc(added, 1)

            over_chunks(dve, step)

        @block.tensor
        def _(pe):
            pe.wait_ge(w_in, 48)

            def first(i, n):
                w = n * 128
                for half, done in ((2, h3_done), (0, h1_done)):
                    if half == 2:
                        wait_reuse(pe, h3_copied, 2 * i)
                    else:
                        wait_reuse(pe, prod_ready, 2 * i)
                    for o in range(half, half + 2):
                        for g in range(G):
                            mm = nc.tensor.matmul(p_h[0:I1, o, 0:w], w13[:, g, o, :], xt[:, g, bass.ds(i * N, w)],
                                                  start=(g == 0), stop=(g == G - 1))
                    mm.then_inc(done, 1)

            def second(i, n):
                pe.wait_ge(act_ready, i + 1)
                wait_reuse(pe, added, i)
                for a in range(n):
                    mm = nc.tensor.matmul(p_y[:, a // 2, (a % 2) * D:(a % 2 + 1) * D], act_t[:, a * 128:(a + 1) * 128],
                                          w2[:], start=True, stop=True)
                mm.then_inc(second_done, 1)

            first(0, CH)
            first(1, CH)
            second(0, CH)
            with pe.Fori(1, NCH - 1) as i:
                first(i + 1, CH)
                second(i, CH)
            first(NCH, NTILE - NCH * CH)
            second(NCH - 1, CH)
            second(NCH, NTILE - NCH * CH)


def build_moe(nc, layer, h_in, h_out, c):
    ne = (E0, E1)[layer]
    n_gate = 8
    rows = nc.dram_tensor(f"rows{layer}", (S + 256, D + ne), F32, kind="Internal").ap()
    h_acc = h_out if layer == 0 else nc.dram_tensor("h_acc1", (S + 256, D), F32, kind="Internal").ap()
    with ExitStack() as ctx:
        def sb(name, shape, dt=F32):
            return ctx.enter_context(nc.sbuf_tensor(f"f{layer}_{name}", shape, dt))

        t = {"ident": sb("ident", [128, 128]), "table": sb("table", [128, NCHK, 4], I32),
             "chosen": sb("chosen", [128, NCHK, 8])}
        if layer == 1:
            t["xt"] = sb("xt", [GF, G, S])
        with ExitStack() as routing:
            def sb(name, shape):
                return routing.enter_context(nc.sbuf_tensor(f"f{layer}_{name}", shape, F32))

            t.update(h=sb("h", [128, NTILE, D]), logits=sb("logits", [128, NTILE, n_gate]),
                     rows=sb("rows", [128, NTILE, D + ne]))
            t["gate"] = t["rows"][:, :, D:D + ne]
            build_norm(nc, f"n{layer}_", h_in, c["ident"], c["gate_w"], t, n_gate)
            (build_gate0, build_gate1)[layer](nc, c, t)
            build_bias2(nc, f"b{layer}_", ne, c["b2"], t)
            build_dispatch(nc, f"d{layer}_", (128, I1)[layer], c, t, h_acc, rows)
        (build_sparse0, build_sparse1)[layer](nc, c, t, rows, h_acc)
        if layer == 1:
            build_shared(nc, c, t, h_acc, h_out)



CIN = 3
PP = 256
R = 5
VOCAB = 8000
NSEG = 3
KI = CIN * PP // 128
BI = 3
IT = [(3 * i, min(BI, B - 3 * i)) for i in range(-(-B // BI))]
TB = 4


@stage
def build_embed(nc, h_out, c, token_table, segm_table):
    with ExitStack() as ctx:
        def sb(name, shape, dt=F32):
            return ctx.enter_context(nc.sbuf_tensor("em_" + name, shape, dt))

        def sem(name):
            return nc.alloc_semaphore(name="em_" + name)

        pix = sb("pix", [128, KI, B * NI])
        wp = sb("wp", [128, 2, R, D])
        w_repr = sb("w_repr", [128, CIN * R])
        b_repr = sb("b_repr", [128, R])
        b_proj = sb("b_proj", [R, D])
        ones = sb("ones", [128, 128])
        mixed = sb("mixed", [128, CIN + 1, 2, D])
        pos = sb("pos", [NT, D])
        ids = [sb(f"ids{k}", [NT, B], I32) for k in range(2)]
        below = [sb(f"below{k}", [NT, B]) for k in range(2)]
        row = [sb(f"row{k}", [NT, B], I32) for k in range(2)]
        tok = sb("tok", [NT, B, D])
        seg = sb("seg", [NT, B, D])
        img = [sb(f"img{i}", [128, D]) for i in range(2)]
        p_i = ctx.enter_context(nc.psum_tensor("em_p_i", [128, 2, 512], F32))

        pix_in = [sem(f"pix_in{k}") for k in range(KI)]
        w_in = sem("w_in")
        ids_in = sem("ids_in")
        pos_in = sem("pos_in")
        ones_ready = sem("ones_ready")
        mixing = sem("mixing")
        below_ready = sem("below_ready")
        wrapped = sem("wrapped")
        rows_ready = sem("rows_ready")
        gathered = [sem(f"gathered{i}") for i in range(B // TB)]
        with_pos = sem("with_pos")
        text_ready = sem("text_ready")
        image_done = sem("image_done")
        image_copied = sem("image_copied")
        image_stored = [sem(f"image_stored{i}") for i in range(2)]
        text_stored = sem("text_stored")
        h3 = h_out.rearrange("(b t) f -> b t f", t=T)
        block = ctx.enter_context(nc.Block())

        @block.sync
        def _(sp):
            for k in range(2):
                sp.dma_start(ids[k][:], c["ids"][k]).then_inc(ids_in, 16)
            for dst, src in ((wp[:], c["wp"]), (w_repr[:], c["w_repr"].broadcast_to([128, CIN * R])),
                             (b_repr[:], c["b_repr"].broadcast_to([128, R])), (b_proj[:], c["b_proj"])):
                sp.dma_start(dst, src).then_inc(w_in, 16)
            for k in range(KI):
                sp.dma_start(pix[:, k, :], c["pix"][k]).then_inc(pix_in[k], 16)
            sp.dma_start(pos[:], c["pos"]).then_inc(pos_in, 16)
            for i, (b0, nb) in enumerate(IT):
                sp.wait_ge(image_copied, i + 1)
                for b in range(nb):
                    sp.dma_start(h3[b0 + b, 0:NI, :], img[i % 2][b * NI:(b + 1) * NI, :]
                                 ).then_inc(image_stored[i % 2], 16)
            for i in range(B // TB):
                sp.wait_ge(text_ready, i + 1)
                sp.dma_start(h3[i * TB:(i + 1) * TB, NI:T, :].rearrange("b t f -> t b f"),
                             tok[:, i * TB:(i + 1) * TB, :]).then_inc(text_stored, 16)
            for i in range(2):
                sp.wait_ge(image_stored[i], 16 * sum(n for _, n in IT[i::2]))
            sp.wait_ge(text_stored, 16 * (B // TB))

        @block.gpsimd
        def _(pool):
            nc.gpsimd.memset(ones[:], 1.0).then_inc(ones_ready, 1)
            pool.wait_ge(rows_ready, 2)
            for b in range(B):
                for dst, at, table in ((tok, row[0], token_table), (seg, row[1], segm_table)):
                    nc.gpsimd.indirect_dma_start(
                        dst[:, b, :], None, table[:, :], bass.IndirectOffsetOnAxis(ap=at[:, b:b + 1], axis=0)
                    ).then_inc(gathered[b // TB], 16)

        @block.vector
        def _(dve):
            dve.wait_ge(ids_in, 32)
            for k, n in enumerate((VOCAB, NSEG)):
                nc.vector.tensor_scalar(below[k][:], ids[k][:], 0.0, float(n), ALU.is_lt, ALU.mult
                                        ).then_inc(below_ready, 1)
            dve.wait_ge(below_ready, 2)
            for k in range(2):
                nc.vector.tensor_tensor(below[k][:], below[k][:], ids[k][:], ALU.add).then_inc(wrapped, 1)
            dve.wait_ge(wrapped, 2)
            for k, n in enumerate((VOCAB, NSEG)):
                nc.vector.tensor_scalar(row[k][:], below[k][:], 0.0, float(n - 1), ALU.max, ALU.min
                                        ).then_inc(rows_ready, 1)
            dve.wait_ge(w_in, 64)
            for r in range(R):
                if r > 0:
                    dve.wait_ge(mixing, (CIN + 1) * r)
                for ch in range(CIN + 1):
                    by = w_repr[:, ch * R + r:ch * R + r + 1] if ch < CIN else b_repr[:, r:r + 1]
                    if r == 0:
                        nc.vector.tensor_scalar(mixed[:, ch, :, :], wp[:, :, r, :], by, None, ALU.mult
                                                ).then_inc(mixing, 1)
                    else:
                        nc.vector.scalar_tensor_tensor(mixed[:, ch, :, :], wp[:, :, r, :], by, mixed[:, ch, :, :],
                                                       ALU.mult, ALU.add).then_inc(mixing, 1)
            dve.wait_ge(pos_in, 16)
            for i in range(B // TB):
                dve.wait_ge(gathered[i], 32 * TB)
                part = slice(i * TB, (i + 1) * TB)
                nc.vector.tensor_tensor(seg[:, part, :], seg[:, part, :],
                                        pos[:].unsqueeze(1).broadcast_to([NT, TB, D]), ALU.add).then_inc(with_pos, 1)
                dve.wait_ge(with_pos, i + 1)
                nc.vector.tensor_tensor(tok[:, part, :], seg[:, part, :], tok[:, part, :], ALU.add
                                        ).then_inc(text_ready, 1)

        @block.tensor
        def _(pe):
            pe.wait_ge(mixing, (CIN + 1) * R)
            pe.wait_ge(ones_ready, 1)
            for k in range(KI):
                pe.wait_ge(pix_in[k], 16)
            for i, (b0, nb) in enumerate(IT):
                if i >= 2:
                    wait_reuse(pe, image_copied, i - 1)
                out = p_i[0:nb * NI, i % 2, 0:D]
                for k in range(KI):
                    nc.tensor.matmul(out, pix[:, k, b0 * NI:(b0 + nb) * NI], mixed[:, k // 2, k % 2, :],
                                     start=(k == 0), stop=False)
                for k in range(2):
                    nc.tensor.matmul(out, ones[:, 0:nb * NI], mixed[:, CIN, k, :], start=False, stop=False)
                nc.tensor.matmul(out, ones[0:R, 0:nb * NI], b_proj[:], start=False, stop=True
                                 ).then_inc(image_done, 1)

        @block.scalar
        def _(act):
            for i, (b0, nb) in enumerate(IT):
                act.wait_ge(image_done, i + 1)
                if i >= 2:
                    act.wait_ge(image_stored[i % 2], 16 * sum(n for _, n in IT[i % 2:i:2]))
                nc.scalar.copy(img[i % 2][0:nb * NI, :], p_i[0:nb * NI, i % 2, 0:D]).then_inc(image_copied, 1)


def build(nc, a, out):
    def of(stage):
        return {k[3:]: v for k, v in a.items() if k[:3] == stage}

    h = [nc.dram_tensor(f"h{i}", (S + 256 * (i == 2), D), F32, kind="Internal").ap() for i in range(4)]
    build_embed(nc, h[0], of("em_"), a["em_token_table"], a["em_segm_table"])
    build_attention0(nc, h[0], h[1], of("a0_"))
    build_moe(nc, 0, h[1], h[2], of("f0_"))
    build_attention1(nc, h[2], h[3], of("a1_"))
    build_moe(nc, 1, h[3], out, of("f1_"))



def by_groups(w):
    return np.ascontiguousarray(w.reshape(G, GF, -1).transpose(1, 0, 2))


def layout(x):
    c = {}
    f32 = np.float32
    ident = np.eye(128, dtype=f32)
    f = np.arange(GF)
    head_mask = (f[:, None] // HS == np.arange(HG)).astype(f32)

    side = x["x"].shape[-1] // 16
    pix = x["x"].reshape(B, CIN, side, 16, side, 16).transpose(1, 3, 5, 0, 2, 4)
    c["em_pix"] = pix.reshape(KI, 128, B * NI)
    c["em_wp"] = x["L0_tok_W_proj"].reshape(R, D, 2, 128).transpose(3, 2, 0, 1)
    c["em_w_repr"] = x["L0_tok_W_repr"].T.reshape(1, CIN * R)
    c["em_b_repr"] = x["L0_tok_b_repr"][None]
    c["em_b_proj"] = x["L0_tok_b_proj"]
    c["em_ids"] = np.stack([x["x_txt"].T, x["mask_BS_i2_0"].T])
    c["em_token_table"] = x["L0_txt_token_table"]
    c["em_segm_table"] = x["L0_txt_segm_table"]
    even = (np.arange(D) // 2 * 2).astype(f32) / f32(D)
    angle = np.arange(NT, dtype=f32)[:, None] / np.power(f32(10000.0), even)[None, :]
    c["em_pos"] = np.where(np.arange(D) % 2 == 0, np.sin(angle), np.cos(angle)).astype(f32)

    c["a0_ident"] = ident
    c["a0_wqkv"] = by_groups(x["L0_attn_Wqkv"].T)
    c["a0_wproj"] = by_groups(x["L0_attn_Wproj"].T)
    c["a0_wv"] = np.ascontiguousarray(x["L0_attn_Wv"].T.reshape(2, 128, HS).transpose(1, 0, 2))
    c["a0_bv"] = np.tile(x["L0_attn_bv"], HG)[:, None]
    col = np.arange(128)
    spread = np.zeros((GF, HG, 3, 128), f32)
    for h in range(HG):
        for a in range(2):
            spread[h * HS + a * 8 + col // HS, h, a, col] = 1
        spread[h * HS + col % HS, h, 2, col] = 1
    c["a0_spread"] = spread
    c["a0_reset"] = np.broadcast_to((np.arange(T) % LMIN != 0).astype(f32), (GF, T))
    c["a0_head_mask"] = head_mask
    tail_rows = np.zeros((HG, NC, GF), f32)
    tail_rows[:, NS, :] = head_mask.T
    c["a0_tail_rows"] = tail_rows.reshape(NG, GF)
    tok = np.arange(TR)[:, None, None] + np.array(T0)[None, :, None]
    last = np.array([r for _, r in SETS] + [-1])
    c["a0_set_mask"] = np.where(tok >= last, 0, -1e30).astype(f32)

    c["a1_ident"] = ident
    c["a1_wqk"] = by_groups(np.concatenate([x["L1_attn_Wq"], x["L1_attn_Wk"]], axis=1))
    c["a1_wv"] = by_groups(x["L1_attn_Wv"])
    c["a1_wo"] = by_groups(x["L1_attn_Wo"])
    c["a1_bqk"] = np.concatenate([x["L1_attn_bq"].reshape(G, GF), x["L1_attn_bk"].reshape(G, GF)]).T
    c["a1_bv"] = x["L1_attn_bv"][None]
    c["a1_bo"] = x["L1_attn_bo"][None]
    c["a1_spread"] = spread[:, :, 2, :]
    c["a1_query_mask"] = (col[:, None] // HS == np.arange(TP) % QB).astype(f32)
    c["a1_head_mask"] = head_mask
    far = x["L1_attn_rel_emb"].shape[0] // 2
    offset = np.arange(QB)[:, None] - (np.arange(REL_W) - (REL_W - T))
    c["a1_rel"] = x["L1_attn_rel_emb"][np.clip(offset, -far, far) + far].transpose(0, 2, 1).reshape(128, REL_W)

    c["f0_ident"] = ident
    c["f0_gate_w"] = by_groups(x["L0_ffn_gate_weight"].T)
    power = 2 ** np.arange(29, -1, -1)
    c["f0_bits"] = np.broadcast_to(power.astype(np.int32), (128, 30))
    c["f0_bits_f"] = np.broadcast_to(power.astype(f32), (128, 30))
    c["f0_ones"] = np.ones((128, 128), f32)
    c["f0_w1"] = x["L0_ffn_w1"].reshape(E0, G, GF, H0).transpose(0, 2, 1, 3).reshape(E0 * GF, G * H0)
    w2 = x["L0_ffn_w2"].reshape(E0, M0, 128, D).transpose(0, 2, 1, 3).reshape(E0 * 128, M0 * D)
    b1 = x["L0_ffn_b1"].reshape(E0, M0, 128).transpose(0, 2, 1).reshape(E0 * 128, M0)
    c["f0_w2"] = np.concatenate([w2, b1], axis=1)
    c["f0_b2"] = x["L0_ffn_b2"]

    slot_tile = np.arange(SLOTS)
    for f in ("f0_", "f1_"):
        c[f + "lower"] = np.triu(np.ones((128, 128), f32), 1)
        c[f + "iota"] = np.broadcast_to(np.arange(128, dtype=f32), (128, 128))
        c[f + "part"] = (col[:, None] + np.arange(2)).astype(f32)
        c[f + "dummy"] = (S + slot_tile % 2 * 128 + col[:, None]).astype(f32)
        c[f + "starts"] = np.broadcast_to(np.arange(MAX_CH, dtype=f32) * PC, (128, MAX_CH))

    w1, w3, w2, b1, b3, b2 = (np.concatenate([x["L1_ffn_" + a], x["L1_ffn_" + s][None]])
                              for a, s in (("W1", "Ws1"), ("W3", "Ws3"), ("W2", "Ws2"),
                                           ("B1", "Bs1"), ("B3", "Bs3"), ("B2", "Bs2")))
    c["f1_ident"] = ident
    c["f1_gate_w"] = by_groups(x["L1_ffn_gate_w"].T)
    c["f1_gate_b"] = x["L1_ffn_gate_b"][None]
    n = E1 - 1
    c["f1_earlier"] = np.broadcast_to(np.tril(np.ones((n, n), f32), -1), (128, n, n))
    w = np.stack([w1, w3]).reshape(2, E1, G, GF, I1, 2)
    w13 = w.transpose(1, 3, 2, 0, 5, 4).reshape(E1, GF, G * 4 * I1)
    b13 = np.stack([b1, b3]).reshape(2, E1, I1, 2).transpose(1, 2, 0, 3).reshape(E1, I1, 4)
    c["f1_w"] = np.concatenate([w13, w2, b13], axis=2)[:n].reshape(n * GF, -1)
    c["f1_shared_w13"] = w13[n].reshape(GF, G, 4, I1)
    c["f1_shared_w2"] = w2[n]
    c["f1_shared_b13"] = b13[n]
    c["f1_b2"] = b2
    return c


def kernel(**inputs):
    from concourse import bacc
    from concourse.bass_utils import run_bass_kernel_spmd

    nc = bacc.Bacc("TRN2", target_bir_lowering=False, num_devices=1)
    arrays, a = {}, {}
    for name, array in layout({k: np.asarray(v) for k, v in inputs.items()}).items():
        arrays["in_" + name] = np.ascontiguousarray(array)
        a[name] = nc.dram_tensor("in_" + name, array.shape, mybir.dt.from_np(array.dtype), kind="ExternalInput").ap()
    out = nc.dram_tensor("out", (S, D), F32, kind="ExternalOutput").ap()
    build(nc, a, out)
    r = run_bass_kernel_spmd(nc, [arrays], core_ids=[0])
    return r.results[0]["out"].reshape(B, T, D)
```

```python
from contextlib import ExitStack

import numpy as np

import concourse.bass as bass
from concourse import mybir

F32 = mybir.dt.float32
I32 = mybir.dt.int32
BF16 = mybir.dt.bfloat16
ALU = mybir.AluOpType
ACT = mybir.ActivationFunctionType
AX = mybir.AxisListType.X

B = 32
NI = 36
NT = 128
T = NI + NT
S = B * T
D = 192
G = 2
GF = D // G
NH = 12
HG = NH // G
HS = D // NH
EPS = 1e-5
SCALE = 0.25

TR = 84
T0 = (0, 80)
TOWN = (80, 84)

LMIN = 16
SETS = [(i * L, (i + 1) * L - 1) for L in (16, 32, 64, 128) for i in range(T // L)]
NS = len(SETS)
NC = NS + 1
NG = HG * NC


def pipelined(eng, first, second, third, beside):
    def around(b, p, with_third, with_first):
        def place(at):
            for kind, part in beside.get(at, ()):
                if kind == "third" and with_third:
                    third[part](b, p)
                if kind == "first" and with_first:
                    first[part](b + 2, p)
        second(b + 1, 1 - p, place)

    for part in first:
        part(0, 0)
    around(-1, 1, False, True)
    for p in range(2):
        around(p, p, True, True)
    with eng.Fori(1, B // 2 - 1) as pair:
        for p in range(2):
            around(pair * 2 + p, p, True, True)
    around(B - 2, 0, True, False)
    for part in third:
        part(B - 1, 1)


def stage(build):
    def run(nc, *args):
        with nc.cleanup_on_exit():
            build(nc, *args)
    return run


def wait_reuse(eng, sem, value):
    if not (isinstance(value, int) and value <= 0):
        eng.wait_ge(sem, value)


def rows_of(h, b, j, n):
    return h[bass.ds(b * T + T0[j], n), :]


@stage
def build_attention0(nc, h_in, h_out, c):
    with ExitStack() as ctx:
        def sb(name, shape):
            return ctx.enter_context(nc.sbuf_tensor("a0_" + name, shape, F32))

        def ps(name, shape):
            return ctx.enter_context(nc.psum_tensor("a0_" + name, shape, F32))

        def sem(name):
            return nc.alloc_semaphore(name="a0_" + name)

        ident = sb("ident", [128, 128])
        wqkv = sb("wqkv", [GF, G, 3 * D])
        wproj = sb("wproj", [GF, G, D])
        spread = sb("spread", [GF, HG, 3, 128])
        wv_pad = sb("wv_pad", [128, 2, 5 * HS + HS + 5 * HS])
        bv = sb("bv", [GF, 1])
        reset = sb("reset", [GF, T])
        head_mask = sb("head_mask", [GF, HG])
        tail_rows = sb("tail_rows", [NG, GF])
        set_mask = sb("set_mask", [TR, 2, NC])
        half = sb("half", [TR, 2])
        eps = sb("eps", [TR, 2])
        carrier = sb("carrier", [TR, 1])

        hb = sb("hb", [TR, 2, D])
        stats = sb("stats", [TR, 2, 6])
        mean_var = sb("mean_var", [TR, 2, 2])
        var_eps = sb("var_eps", [TR, 2])
        rstd = sb("rstd", [TR, 2])
        xn = sb("xn", [TR, 2, D])
        xt = sb("xt", [GF, G, T])
        qkv = [sb(f"qkv{p}", [GF, 3 * G, T]) for p in range(2)]
        v0x = [sb(f"v0x{i}", [128, T]) for i in range(3)]
        outer = [sb(f"outer{i}", [128, 2, T]) for i in range(3)]
        vt = sb("vt", [GF, G, T])
        ktail = sb("ktail", [GF, G, T])
        vtail = [sb(f"vtail{p}", [GF, G, T]) for p in range(2)]
        ksets = sb("ksets", [GF, G, NS])
        vsets = sb("vsets", [GF, G, NS])
        kdiag = sb("kdiag", [GF, G, HG, NC])
        vdiag = [sb(f"vdiag{p}", [GF, G, HG, NC]) for p in range(2)]
        qk_tail = sb("qk_tail", [GF, G, T])
        lg = sb("lg", [TR, 2 * NH, NC])
        lmax = sb("lmax", [TR, 2 * NH])
        lsum = sb("lsum", [TR, 2 * NH])
        rsum = sb("rsum", [TR, 2 * NH])
        ex = sb("ex", [TR, 2 * NH, NC])
        att = [sb(f"att{p}", [TR, 2 * NH, NC]) for p in range(2)]
        att_t = sb("att_t", [NG, G, T])
        vd_t = sb("vd_t", [NG, G, GF])
        tail_part = sb("tail_part", [GF, G, T])
        ct = sb("ct", [GF, G, T])
        hres = sb("hres", [TR, 2, D])
        hnew = sb("hnew", [TR, 2, D])

        p_x = ps("p_x", [128, 512])
        p_q = ps("p_q", [128, 2, 512])
        p_e = ps("p_e", [128, 3, 512])
        p_v = ps("p_v", [128, 512])
        p_a = ps("p_a", [128, 512])
        p_xt = p_x[0:GF, 0:G * T].rearrange("p (g t) -> p g t", g=G)
        p_vd = p_x[0:NG, 0:G * GF].rearrange("p (g f) -> p g f", g=G)
        p_vt = p_v[0:GF, 0:G * T].rearrange("p (g t) -> p g t", g=G)
        p_at = p_a[0:NG, 0:G * T].rearrange("p (g t) -> p g t", g=G)
        p_o = p_a[0:TR, 0:2 * D].rearrange("p (j f) -> p j f", j=2)
        p_c = p_q[0:GF, 0, 0:G * T].rearrange("p (g t) -> p g t", g=G)
        p_w = p_q[0:GF, 1, 0:G * T].rearrange("p (g t) -> p g t", g=G)

        const_in = sem("const_in")
        cleared = sem("cleared")
        h_in_sem = sem("h_in")
        hres_in = sem("hres_in")
        h_stored = sem("h_stored")
        aggr_in = sem("aggr_in")
        aggr = sem("aggr")
        rstd_ready = sem("rstd_ready")
        pool0 = sem("pool0")
        xn_ready = sem("xn_ready")
        xt_done = sem("xt_done")
        xt_copied = sem("xt_copied")
        qkv_done = sem("qkv_done")
        qkv_copied = sem("qkv_copied")
        spread_done = sem("spread_done")
        v0_copied = sem("v0_copied")
        outer_ready = sem("outer_ready")
        bilin_done = sem("bilin_done")
        vt_copied = sem("vt_copied")
        k_summed = sem("k_summed")
        v_summed = sem("v_summed")
        soft = sem("soft")
        ktail_ready = sem("ktail_ready")
        vtail_ready = sem("vtail_ready")
        kdiag_ready = sem("kdiag_ready")
        qk_ready = sem("qk_ready")
        logits_done = sem("logits_done")
        lg_shifted = sem("lg_shifted")
        exp_done = sem("exp_done")
        att_ready = sem("att_ready")
        vdiag_ready = sem("vdiag_ready")
        turned = sem("turned")
        turned_copied = sem("turned_copied")
        ctx_done = sem("ctx_done")
        vec2 = sem("vec2")
        ct_ready = sem("ct_ready")
        proj_done = sem("proj_done")
        hnew_ready = sem("hnew_ready")

        consts = [(ident[:], c["ident"]), (wqkv[:], c["wqkv"]), (wproj[:], c["wproj"]),
                  (spread[:], c["spread"]), (bv[:], c["bv"]), (reset[:], c["reset"]),
                  (head_mask[:], c["head_mask"]), (tail_rows[:], c["tail_rows"]), (set_mask[:], c["set_mask"]),
                  (wv_pad[:, :, 5 * HS:6 * HS], c["wv"])]
        block = ctx.enter_context(nc.Block())

        @block.sync
        def _(sp):
            sp.wait_ge(cleared, 4)
            for dst, src in consts:
                sp.dma_start(dst, src).then_inc(const_in, 16)

            def first(b, p):
                wait_reuse(sp, xn_ready, b)
                for j in range(2):
                    sp.dma_start(hb[:, j, :], rows_of(h_in, b, j, TR)).then_inc(h_in_sem, 16)

            def second(b, p, place):
                place(0)

            def residual(b, p):
                wait_reuse(sp, hnew_ready, b)
                for j in range(2):
                    sp.dma_start(hres[:, j, :], rows_of(h_in, b, j, TR)).then_inc(hres_in, 16)

            def store(b, p):
                sp.wait_ge(hnew_ready, b + 1)
                for j in range(2):
                    sp.dma_start(rows_of(h_out, b, j, TOWN[j]), hnew[0:TOWN[j], j, :]).then_inc(h_stored, 16)

            pipelined(sp, [first], second, [residual, store],
                      {0: [("third", 0), ("first", 0), ("third", 1)]})
            sp.wait_ge(h_stored, 32 * B)

        @block.gpsimd
        def _(pool):
            nc.gpsimd.memset(wv_pad[:], 0.0).then_inc(cleared, 1)
            nc.gpsimd.memset(kdiag[:], 0.0).then_inc(cleared, 1)
            nc.gpsimd.memset(vdiag[0][:], 0.0).then_inc(cleared, 1)
            nc.gpsimd.memset(vdiag[1][:], 0.0).then_inc(cleared, 1)
            nc.gpsimd.memset(half[:], -0.5).then_inc(cleared, 1)
            nc.gpsimd.memset(eps[:], EPS).then_inc(cleared, 1)
            pool.wait_ge(cleared, 6)

            def first(b, p):
                pool.wait_ge(aggr, 2 * b + 2)
                nc.gpsimd.tensor_tensor(var_eps[:], mean_var[:, :, 1], eps[:], ALU.add).then_inc(pool0, 1)
                pool.wait_ge(pool0, b + 1)
                nc.gpsimd.tensor_tensor(rstd[:], var_eps[:], half[:], ALU.pow).then_inc(rstd_ready, 1)

            def second(b, p, place):
                pool.wait_ge(ktail_ready, 2 * b + 2)
                wait_reuse(pool, logits_done, b)
                nc.gpsimd.tensor_tensor(qk_tail[:], qkv[p][:, 0:2, :], ktail[:], ALU.mult).then_inc(qk_ready, 1)
                place(0)

            pipelined(pool, [first], second, [], {0: [("first", 0)]})

        @block.vector
        def _(dve):
            dve.wait_ge(const_in, 16 * len(consts))
            dve.wait_ge(cleared, 6)

            def first(b, p):
                dve.wait_ge(h_in_sem, 32 * b + 32)
                for j in range(2):
                    nc.vector.bn_stats(stats[:, j, :], hb[:, j, :]).then_inc(aggr_in, 1)
                dve.wait_ge(aggr_in, 2 * b + 2)
                nc.vector.tensor_copy(carrier[:], half[:, 0:1])
                for j in range(2):
                    nc.vector.bn_aggr(mean_var[:, j, :], stats[:, j, :]).then_inc(aggr, 1)

            def normalise(b, p):
                dve.wait_ge(rstd_ready, b + 1)
                wait_reuse(dve, xt_done, b)
                for j in range(2):
                    i = nc.vector.tensor_scalar(xn[:, j, :], hb[:, j, :], mean_var[:, j, 0:1], rstd[:, j:j + 1],
                                                ALU.subtract, ALU.mult)
                i.then_inc(xn_ready, 1)

            def sums(b, src, tail, scanned, sets, summed, diag):
                for g in range(G):
                    nc.vector.tensor_tensor_scan(tail[:, g, :], reset[:], src[:, g, :], 0.0, ALU.mult, ALU.add
                                                 ).then_inc(scanned, 1)
                dve.wait_ge(scanned, 2 * b + 2)
                nc.vector.tensor_copy(sets[:, :, 0:10], tail[:, :, 15:160:16]).then_inc(summed, 1)
                dve.wait_ge(summed, 4 * b + 1)
                nc.vector.tensor_tensor(sets[:, :, 10:15], sets[:, :, 0:10:2], sets[:, :, 1:10:2], ALU.add
                                        ).then_inc(summed, 1)
                dve.wait_ge(summed, 4 * b + 2)
                nc.vector.tensor_tensor(sets[:, :, 15:17], sets[:, :, 10:14:2], sets[:, :, 11:14:2], ALU.add
                                        ).then_inc(summed, 1)
                dve.wait_ge(summed, 4 * b + 3)
                nc.vector.tensor_tensor(sets[:, :, 17:18], sets[:, :, 15:16], sets[:, :, 16:17], ALU.add
                                        ).then_inc(summed, 1)
                dve.wait_ge(summed, 4 * b + 4)
                return [nc.vector.tensor_tensor(diag[:, g, :, 0:NS],
                                                sets[:, g:g + 1, :].broadcast_to([GF, HG, NS]),
                                                head_mask[:].unsqueeze(2).broadcast_to([GF, HG, NS]), ALU.mult)
                        for g in range(G)][-1]

            def k_sums(b, p):
                dve.wait_ge(qkv_copied, 2 * b + 2)
                wait_reuse(dve, logits_done, b)
                wait_reuse(dve, qk_ready, b)
                sums(b, qkv[p][:, 2:4, :], ktail, ktail_ready, ksets, k_summed, kdiag).then_inc(kdiag_ready, 1)

            def v_sums(b, p):
                dve.wait_ge(vt_copied, b + 1)
                sums(b, vt, vtail[p], vtail_ready, vsets, v_summed, vdiag[p]).then_inc(vdiag_ready, 1)

            def products(b, p, h):
                dve.wait_ge(v0_copied, NH * b + h + 1)
                wait_reuse(dve, bilin_done, NH * b + h - 2)
                nc.vector.tensor_tensor(outer[h % 3][:], p_e[:, h % 3, 0:2 * T].rearrange("p (a t) -> p a t", a=2),
                                        v0x[h % 3][:].unsqueeze(1).broadcast_to([128, 2, T]), ALU.mult
                                        ).then_inc(outer_ready, 1)

            def second(b, p, place):
                for h in range(6):
                    products(b, p, h)
                    place(h)
                dve.wait_ge(logits_done, b + 1)
                for j in range(2):
                    nc.vector.scalar_tensor_tensor(
                        lg[:, j * NH:(j + 1) * NH, :],
                        p_a[0:TR, j * 228:(j + 1) * 228].rearrange("p (h s) -> p h s", h=NH), SCALE,
                        set_mask[:, j:j + 1, :].broadcast_to([TR, NH, NC]), ALU.mult, ALU.add).then_inc(soft, 1)
                dve.wait_ge(soft, 5 * b + 2)
                nc.vector.tensor_reduce(lmax[:], lg[:], AX, ALU.max).then_inc(soft, 1)
                dve.wait_ge(soft, 5 * b + 3)
                nc.vector.tensor_tensor(lg[:], lg[:], lmax[:].unsqueeze(2).broadcast_to([TR, 2 * NH, NC]),
                                        ALU.subtract).then_inc(lg_shifted, 1)
                for h in range(6, 8):
                    products(b, p, h)
                    place(h)
                dve.wait_ge(exp_done, b + 1)
                nc.vector.reduce_sum(lsum[:], ex[:], AX).then_inc(soft, 1)
                products(b, p, 8)
                place(8)
                dve.wait_ge(soft, 5 * b + 4)
                nc.vector.reciprocal(rsum[:], lsum[:]).then_inc(soft, 1)
                products(b, p, 9)
                dve.wait_ge(soft, 5 * b + 5)
                nc.vector.tensor_tensor(att[p][:], ex[:], rsum[:].unsqueeze(2).broadcast_to([TR, 2 * NH, NC]),
                                        ALU.mult).then_inc(att_ready, 1)
                place(9)
                for h in range(10, NH):
                    products(b, p, h)
                    place(h)

            def context(b, p):
                dve.wait_ge(ctx_done, b + 1)
                nc.vector.tensor_tensor(tail_part[:], p_w, vtail[p][:], ALU.mult).then_inc(vec2, 1)
                dve.wait_ge(vec2, b + 1)
                nc.vector.tensor_tensor(ct[:], tail_part[:], p_c, ALU.add).then_inc(ct_ready, 1)

            def residual(b, p):
                dve.wait_ge(proj_done, b + 1)
                dve.wait_ge(hres_in, 32 * b + 32)
                wait_reuse(dve, h_stored, 32 * b)
                nc.vector.tensor_tensor(hnew[:], p_o, hres[:], ALU.add).then_inc(hnew_ready, 1)

            pipelined(dve, [first, normalise, k_sums], second, [v_sums, context, residual],
                      {0: [("third", 0)], 1: [("first", 0)], 4: [("first", 1)], 6: [("third", 1)],
                       10: [("first", 2)], 11: [("third", 2)]})

        @block.scalar
        def _(act):
            act.wait_ge(const_in, 16 * len(consts))

            def copy_xt(b, p):
                act.wait_ge(xt_done, b + 1)
                nc.scalar.copy(xt[:], p_xt).then_inc(xt_copied, 1)

            def copy_qkv(i):
                def part(b, p):
                    act.wait_ge(qkv_done, 2 * b + i + 1)
                    nc.scalar.copy(qkv[p][:, 3 * i:3 * i + 3, :],
                                   p_q[0:GF, i, 0:3 * T].rearrange("p (o t) -> p o t", o=3)).then_inc(qkv_copied, 1)
                return part

            def spread_v(b, h):
                act.wait_ge(spread_done, NH * b + h + 1)
                wait_reuse(act, outer_ready, NH * b + h - 2)
                nc.scalar.copy(v0x[h % 3][:], p_e[:, h % 3, 2 * T:3 * T]).then_inc(v0_copied, 1)

            def second(b, p, place):
                for h in range(7):
                    spread_v(b, h)
                    place(h)
                act.wait_ge(lg_shifted, b + 1)
                wait_reuse(act, att_ready, b)
                nc.scalar.activation(ex[:], lg[:], ACT.Exp).then_inc(exp_done, 1)
                for h in range(7, NH):
                    spread_v(b, h)
                    place(h)
                act.wait_ge(bilin_done, NH * b + NH)
                wait_reuse(act, vdiag_ready, b)
                nc.scalar.activation(vt[:], p_vt, ACT.Identity, bias=bv[:]).then_inc(vt_copied, 1)

            def copy_turned(b, p):
                act.wait_ge(turned, b + 1)
                nc.scalar.copy(vd_t[:], p_vd).then_inc(turned_copied, 1)
                nc.scalar.copy(att_t[:], p_at).then_inc(turned_copied, 1)

            pipelined(act, [copy_xt, copy_qkv(0), copy_qkv(1)], second, [copy_turned],
                      {3: [("third", 0)], 7: [("first", 0)], 9: [("first", 1), ("first", 2)]})

        @block.tensor
        def _(pe):
            pe.wait_ge(const_in, 16 * len(consts))
            pe.wait_ge(cleared, 6)

            def first(b, p):
                pe.wait_ge(xn_ready, b + 1)
                wait_reuse(pe, turned_copied, 2 * b - 2)
                wait_reuse(pe, xt_copied, b)
                for g in range(G):
                    for j in range(2):
                        mm = nc.tensor.transpose(p_xt[:, g, T0[j]:T0[j] + TR], xn[:, j, g * GF:(g + 1) * GF],
                                                 ident[0:TR, 0:TR])
                mm.then_inc(xt_done, 1)

            def project_in(b, p):
                pe.wait_ge(xt_copied, b + 1)
                wait_reuse(pe, ct_ready, b - 1)
                wait_reuse(pe, qkv_copied, 2 * b)
                for i in range(2):
                    for o in range(3):
                        for k in range(G):
                            mm = nc.tensor.matmul(p_q[0:GF, i, o * T:(o + 1) * T],
                                                  wqkv[:, k, (3 * i + o) * GF:(3 * i + o + 1) * GF], xt[:, k, :],
                                                  start=(k == 0), stop=(k == G - 1))
                    mm.then_inc(qkv_done, 1)

            def heads_out(b, p, h):
                g, hh = h // HG, h % HG
                wait_reuse(pe, outer_ready, NH * b + h - 2)
                for a in range(3):
                    src = qkv[p][:, 2 + g, :] if a < 2 else qkv[p][:, 4 + g, :]
                    mm = nc.tensor.matmul(p_e[:, h % 3, a * T:(a + 1) * T], spread[:, hh, a, :], src,
                                          start=True, stop=True)
                mm.then_inc(spread_done, 1)

            def contract(b, h):
                g, hh = h // HG, h % HG
                pe.wait_ge(outer_ready, NH * b + h + 1)
                if h == 0:
                    wait_reuse(pe, vt_copied, b)
                for a in range(2):
                    mm = nc.tensor.matmul(p_vt[:, g, :], wv_pad[:, a, (5 - hh) * HS:(11 - hh) * HS],
                                          outer[h % 3][:, a, :], start=(hh == 0 and a == 0),
                                          stop=(hh == HG - 1 and a == 1))
                mm.then_inc(bilin_done, 1)

            def logits(b, p):
                pe.wait_ge(kdiag_ready, b + 1)
                pe.wait_ge(qk_ready, b + 1)
                wait_reuse(pe, turned_copied, 2 * b)
                wait_reuse(pe, hnew_ready, b - 1)
                for j in range(2):
                    for g in range(G):
                        at = j * 228 + g * NG
                        nc.tensor.matmul(p_a[0:TR, at:at + NG], qkv[p][:, g, T0[j]:T0[j] + TR],
                                         kdiag[:, g, :, :].rearrange("p h s -> p (h s)"), start=True, stop=False)
                        mm = nc.tensor.matmul(p_a[0:TR, at + NS:at + NG:NC], qk_tail[:, g, T0[j]:T0[j] + TR],
                                              head_mask[:], start=False, stop=True)
                mm.then_inc(logits_done, 1)

            def second(b, p, place):
                pe.wait_ge(qkv_copied, 2 * b + 2)
                heads_out(b, p, 0)
                heads_out(b, p, 1)
                place(0)
                for h in range(2, NH):
                    heads_out(b, p, h)
                    if h == 4:
                        logits(b, p)
                    contract(b, h - 2)
                    place(h)
                contract(b, NH - 2)
                contract(b, NH - 1)

            def turn(b, p):
                pe.wait_ge(att_ready, b + 1)
                pe.wait_ge(vdiag_ready, b + 1)
                pe.wait_ge(xt_copied, b + 2 if not isinstance(b, int) else min(b + 2, B))
                wait_reuse(pe, hnew_ready, b)
                for g in range(G):
                    nc.tensor.transpose(p_vd[:, g, :], vdiag[p][:, g, :, :].rearrange("p h s -> p (h s)"),
                                        ident[0:GF, 0:GF])
                    for j in range(2):
                        mm = nc.tensor.transpose(
                            p_at[:, g, T0[j]:T0[j] + TR],
                            att[p][:, j * NH + g * HG:j * NH + (g + 1) * HG, :].rearrange("p h s -> p (h s)"),
                            ident[0:TR, 0:TR])
                mm.then_inc(turned, 1)

            def context(b, p):
                pe.wait_ge(turned_copied, 2 * b + 2)
                pe.wait_ge(qkv_copied, 2 * b + 4 if not isinstance(b, int) else min(2 * b + 4, 2 * B))
                for g in range(G):
                    nc.tensor.matmul(p_c[:, g, :], vd_t[:, g, :], att_t[:, g, :], start=True, stop=True)
                    mm = nc.tensor.matmul(p_w[:, g, :], tail_rows[:], att_t[:, g, :], start=True, stop=True)
                mm.then_inc(ctx_done, 1)

            def project_out(b, p):
                pe.wait_ge(ct_ready, b + 1)
                pe.wait_ge(lg_shifted, b + 2 if not isinstance(b, int) else min(b + 2, B))
                for j in range(2):
                    for g in range(G):
                        mm = nc.tensor.matmul(p_o[:, j, :], ct[:, g, T0[j]:T0[j] + TR], wproj[:, g, :],
                                              start=(g == 0), stop=(g == G - 1))
                mm.then_inc(proj_done, 1)

            pipelined(pe, [first, project_in], second, [turn, context, project_out],
                      {3: [("third", 0)], 5: [("third", 1)], 7: [("first", 0)], 9: [("first", 1)], 10: [("third", 2)]})


QB = 8
NQ = -(-T // QB)
TP = NQ * QB
QR = NH * QB
QG = 3
REL_W = T + (NQ - 1) * QB
V0 = (HG - 1) * HS
VW = V0 + HS + V0


@stage
def build_attention1(nc, h_in, h_out, c):
    with ExitStack() as ctx:
        def sb(name, shape):
            return ctx.enter_context(nc.sbuf_tensor("a1_" + name, shape, F32))

        def ps(name, shape):
            return ctx.enter_context(nc.psum_tensor("a1_" + name, shape, F32))

        def sem(name):
            return nc.alloc_semaphore(name="a1_" + name)

        ident = sb("ident", [128, 128])
        wqk = sb("wqk", [GF, G, 2 * D])
        wv = sb("wv", [GF, G, D])
        wo = sb("wo", [GF, G, D])
        bqk = sb("bqk", [GF, 2 * G])
        bv = sb("bv", [TR, D])
        bo = sb("bo", [TR, D])
        spread = sb("spread", [GF, HG, 128])
        query_mask = sb("query_mask", [128, TP])
        head_mask = sb("head_mask", [GF, HG])
        rel = sb("rel", [128, REL_W])
        half = sb("half", [TR, 2])
        eps = sb("eps", [TR, 2])
        carrier = sb("carrier", [TR, 1])

        hb = sb("hb", [TR, 2, D])
        stats = sb("stats", [TR, 2, 6])
        mean_var = sb("mean_var", [TR, 2, 2])
        var_eps = sb("var_eps", [TR, 2])
        rstd = sb("rstd", [TR, 2])
        xn = sb("xn", [TR, 2, D])
        xt = [sb(f"xt{p}", [GF, G, T]) for p in range(2)]
        qk = [sb(f"qk{p}", [GF, 2 * G, TP]) for p in range(2)]
        q_heads = [sb(f"q_heads{p}", [GF, G, NQ, NH, QB]) for p in range(2)]
        q_block = [sb(f"q_block{p}", [128, NQ, NH, QB]) for p in range(2)]
        v_pad = [sb(f"v_pad{p}", [TR, 2, NH, VW]) for p in range(2)]
        ntop = sb("ntop", [QR, NQ])
        ex = [sb(f"ex{i}", [QR, QG, T]) for i in range(3)]
        esum = sb("esum", [QR, NQ])
        rsum = sb("rsum", [QR, NQ])
        ex_t = [sb(f"ex_t{p}", [TR, 2, NH, TP]) for p in range(2)]
        ct = sb("ct", [GF, G, T])
        hres = sb("hres", [TR, 2, D])
        hbias = sb("hbias", [TR, 2, D])
        hnew = sb("hnew", [TR, 2, D])

        p_x = ps("p_x", [128, 512])
        p_q = ps("p_q", [128, 2, 512])
        p_s = ps("p_s", [128, 2, 512])
        p_t = ps("p_t", [128, 2, 512])
        p_c = ps("p_c", [128, 512])
        p_xt = p_x[0:GF, 0:G * T].rearrange("p (g t) -> p g t", g=G)
        p_o = p_x[0:TR, 0:2 * D].rearrange("p (j f) -> p j f", j=2)
        p_ct = p_c[0:GF, 0:G * TP].rearrange("p (g t) -> p g t", g=G)

        const_in = sem("const_in")
        cleared = sem("cleared")
        h_in_sem = sem("h_in")
        hres_in = sem("hres_in")
        h_stored = sem("h_stored")
        stats_ready = sem("stats_ready")
        aggr = sem("aggr")
        pool0 = sem("pool0")
        rstd_ready = sem("rstd_ready")
        xn_ready = sem("xn_ready")
        xt_done = sem("xt_done")
        xt_copied = sem("xt_copied")
        qk_done = sem("qk_done")
        qk_copied = sem("qk_copied")
        q_heads_ready0 = sem("q_heads_ready0")
        q_heads_ready1 = sem("q_heads_ready1")
        spread_done = sem("spread_done")
        q_block_ready = sem("q_block_ready")
        v_done = sem("v_done")
        v_ready = sem("v_ready")
        scores_done = sem("scores_done")
        ntop_ready = sem("ntop_ready")
        exp_done = sem("exp_done")
        turned = sem("turned")
        turned_copied0 = sem("turned_copied0")
        turned_copied1 = sem("turned_copied1")
        context_done = sem("context_done")
        scaled = sem("scaled")
        rsum_ready = sem("rsum_ready")
        weights_ready = sem("weights_ready")
        ct_copied = sem("ct_copied")
        hbias_ready = sem("hbias_ready")
        proj_done = sem("proj_done")
        hnew_ready = sem("hnew_ready")

        consts = [(ident[:], c["ident"]), (wqk[:], c["wqk"]), (wv[:], c["wv"]), (wo[:], c["wo"]),
                  (bqk[:], c["bqk"]), (bv[:], c["bv"].broadcast_to([TR, D])), (bo[:], c["bo"].broadcast_to([TR, D])),
                  (spread[:], c["spread"]), (query_mask[:], c["query_mask"]), (head_mask[:], c["head_mask"]),
                  (rel[:], c["rel"])]
        NG3 = NQ // QG
        POOL_HEADS = HG
        block = ctx.enter_context(nc.Block())

        @block.sync
        def _(sp):
            for dst, src in consts:
                sp.dma_start(dst, src).then_inc(const_in, 16)

            def first(b, p):
                wait_reuse(sp, xn_ready, b)
                for j in range(2):
                    sp.dma_start(hb[:, j, :], rows_of(h_in, b, j, TR)).then_inc(h_in_sem, 16)

            def second(b, p, place):
                place(0)

            def residual(b, p):
                wait_reuse(sp, hbias_ready, b)
                for j in range(2):
                    sp.dma_start(hres[:, j, :], rows_of(h_in, b, j, TR)).then_inc(hres_in, 16)

            def store(b, p):
                sp.wait_ge(hnew_ready, b + 1)
                for j in range(2):
                    sp.dma_start(rows_of(h_out, b, j, TOWN[j]), hnew[0:TOWN[j], j, :]).then_inc(h_stored, 16)

            pipelined(sp, [first], second, [residual, store],
                      {0: [("third", 0), ("first", 0), ("third", 1)]})
            sp.wait_ge(h_stored, 32 * B)

        @block.gpsimd
        def _(pool):
            nc.gpsimd.memset(half[:], -0.5).then_inc(cleared, 1)
            nc.gpsimd.memset(eps[:], EPS).then_inc(cleared, 1)
            for p in range(2):
                nc.gpsimd.memset(q_heads[p][:], 0.0).then_inc(cleared, 1)
                nc.gpsimd.memset(qk[p][:, :, T:TP], 0.0).then_inc(cleared, 1)
                nc.gpsimd.memset(v_pad[p][:], 0.0).then_inc(cleared, 1)
            pool.wait_ge(cleared, 8)
            pool.wait_ge(const_in, 16 * len(consts))

            def first(b, p):
                pool.wait_ge(aggr, 2 * b + 2)
                nc.gpsimd.tensor_tensor(var_eps[:], mean_var[:, :, 1], eps[:], ALU.add).then_inc(pool0, 1)
                pool.wait_ge(pool0, b + 1)
                nc.gpsimd.tensor_tensor(rstd[:], var_eps[:], half[:], ALU.pow).then_inc(rstd_ready, 1)

            def split_heads(b, p):
                pool.wait_ge(qk_copied, 4 * b + 2)
                wait_reuse(pool, scores_done, NG3 * (b - 1))
                for h in range(POOL_HEADS):
                    dst = q_heads[p][:, 0, :, h, :]
                    src = qk[p][:, 0, :].rearrange("p (n q) -> p n q", q=QB)
                    if h == 0:
                        i = nc.gpsimd.tensor_tensor(dst, src, head_mask[:, 0:1].unsqueeze(2).broadcast_to(
                            [GF, NQ, QB]), ALU.mult)
                    else:
                        i = nc.gpsimd.tensor_scalar(dst, src, head_mask[:, h:h + 1], None, ALU.mult)
                i.then_inc(q_heads_ready0, 1)

            def second(b, p, place):
                place(0)

            def add_bias(b, p):
                pool.wait_ge(hres_in, 32 * b + 32)
                wait_reuse(pool, hnew_ready, b)
                nc.gpsimd.tensor_tensor(hbias[:], hres[:], bo[:].unsqueeze(1).broadcast_to([TR, 2, D]), ALU.add
                                        ).then_inc(hbias_ready, 1)

            pipelined(pool, [first, split_heads], second, [add_bias],
                      {0: [("third", 0), ("first", 0), ("first", 1)]})

        @block.vector
        def _(dve):
            dve.wait_ge(const_in, 16 * len(consts))
            dve.wait_ge(cleared, 8)
            nc.vector.tensor_scalar(bqk[:, 0:G], bqk[:, 0:G], SCALE, None, ALU.mult).then_inc(scaled, 1)

            def first(b, p):
                dve.wait_ge(h_in_sem, 32 * b + 32)
                for j in range(2):
                    nc.vector.bn_stats(stats[:, j, :], hb[:, j, :]).then_inc(stats_ready, 1)
                dve.wait_ge(stats_ready, 2 * b + 2)
                nc.vector.tensor_copy(carrier[:], half[:, 0:1])
                for j in range(2):
                    nc.vector.bn_aggr(mean_var[:, j, :], stats[:, j, :]).then_inc(aggr, 1)

            def normalise(b, p):
                dve.wait_ge(rstd_ready, b + 1)
                wait_reuse(dve, xt_done, b)
                for j in range(2):
                    i = nc.vector.tensor_scalar(xn[:, j, :], hb[:, j, :], mean_var[:, j, 0:1], rstd[:, j:j + 1],
                                                ALU.subtract, ALU.mult)
                i.then_inc(xn_ready, 1)

            def block_queries(i):
                def part(b, p):
                    dve.wait_ge(spread_done, 4 * b + i + 1)
                    if i == 0:
                        wait_reuse(dve, scores_done, NG3 * (b - 1))
                    nc.vector.tensor_tensor(q_block[p][:, :, 3 * i:3 * i + 3, :].rearrange("p n h q -> p h n q"),
                                            p_q[:, i % 2, 0:3 * TP].rearrange("p (h n q) -> p h n q", h=3, q=QB),
                                            query_mask[:].rearrange("p (n q) -> p n q", q=QB).unsqueeze(1)
                                            .broadcast_to([128, 3, NQ, QB]), ALU.mult).then_inc(q_block_ready, 1)
                return part

            def second(b, p, place):
                dve.wait_ge(v_done, b + 1)
                wait_reuse(dve, context_done, b - 1)
                for j in range(2):
                    i = nc.vector.tensor_tensor(v_pad[p][:, j, :, V0:V0 + HS],
                                                p_o[:, j, :].rearrange("p (h e) -> p h e", h=NH),
                                                bv[:].rearrange("p (h e) -> p h e", h=NH), ALU.add)
                i.then_inc(v_ready, 1)

                def divide(k):
                    dve.wait_ge(exp_done, NG3 * b + k + 1)
                    cols = slice(QG * k, QG * k + QG)
                    nc.vector.reciprocal(rsum[:, cols], esum[:, cols]).then_inc(rsum_ready, 1)
                    dve.wait_ge(rsum_ready, NG3 * b + k + 1)
                    for i in range(QG):
                        a = nc.vector.tensor_scalar(ex[k % 3][:, i, :], ex[k % 3][:, i, :],
                                                    rsum[:, QG * k + i:QG * k + i + 1], None, ALU.mult)
                    a.then_inc(weights_ready, 1)

                def copy_turned(k):
                    dve.wait_ge(turned, NG3 * b + k + 1)
                    nc.vector.tensor_copy(ex_t[p][:, 1, :, QB * QG * k:QB * QG * (k + 1)]
                                          .rearrange("p h (i q) -> p i h q", q=QB),
                                          p_t[0:TR, 1, 0:QG * QR].rearrange("p (i h q) -> p i h q", i=QG, q=QB)
                                          ).then_inc(turned_copied1, 1)

                for k in range(NG3 + 2):
                    if k < NG3:
                        dve.wait_ge(scores_done, NG3 * b + k + 1)
                        if k == 0:
                            wait_reuse(dve, exp_done, NG3 * b)
                        nc.vector.tensor_reduce(ntop[:, QG * k:QG * k + QG],
                                                p_s[0:QR, k % 2, 0:QG * T].rearrange("p (i t) -> p i t", i=QG),
                                                AX, ALU.max, negate=True).then_inc(ntop_ready, 1)
                    if 1 <= k <= NG3:
                        divide(k - 1)
                    if k >= 2:
                        copy_turned(k - 2)
                    place(k)

            def residual(b, p):
                dve.wait_ge(proj_done, b + 1)
                dve.wait_ge(hbias_ready, b + 1)
                wait_reuse(dve, h_stored, 32 * b)
                nc.vector.tensor_tensor(hnew[:], p_o, hbias[:], ALU.add).then_inc(hnew_ready, 1)

            pipelined(dve, [first, normalise] + [block_queries(i) for i in range(4)], second, [residual],
                      {0: [("first", 0)], 2: [("first", 1)], 3: [("third", 0)], 6: [("first", 2), ("first", 3)],
                       7: [("first", 4), ("first", 5)]})

        @block.scalar
        def _(act):
            act.wait_ge(const_in, 16 * len(consts))
            act.wait_ge(cleared, 8)
            act.wait_ge(scaled, 1)

            def copy_xt(b, p):
                act.wait_ge(xt_done, b + 1)
                nc.scalar.copy(xt[p][:], p_xt).then_inc(xt_copied, 1)

            def copy_qk(b, p):
                act.wait_ge(qk_done, b + 1)
                for o in range(2 * G):
                    nc.scalar.activation(qk[p][:, o, 0:T], p_q[0:GF, o // 3, (o % 3) * T:(o % 3 + 1) * T], ACT.Identity,
                                         bias=bqk[:, o:o + 1], scale=SCALE if o < G else 1.0).then_inc(qk_copied, 1)

            def split_heads(b, p):
                act.wait_ge(qk_copied, 4 * b + 2)
                wait_reuse(act, scores_done, NG3 * (b - 1))
                for h in range(POOL_HEADS, NH):
                    g = h // HG
                    i = nc.scalar.activation(q_heads[p][:, g, :, h, :],
                                             qk[p][:, g, :].rearrange("p (n q) -> p n q", q=QB), ACT.Copy,
                                             scale=head_mask[:, h - g * HG:h - g * HG + 1])
                i.then_inc(q_heads_ready1, 1)

            def second(b, p, place):
                def copy_turned(k):
                    act.wait_ge(turned, NG3 * b + k + 1)
                    nc.scalar.copy(ex_t[p][:, 0, :, QB * QG * k:QB * QG * (k + 1)]
                                   .rearrange("p h (i q) -> p i h q", q=QB),
                                   p_t[0:TR, 0, 0:QG * QR].rearrange("p (i h q) -> p i h q", i=QG, q=QB)
                                   ).then_inc(turned_copied0, 1)

                wait_reuse(act, context_done, b - 1)
                for k in range(NG3 + 2):
                    if k < NG3:
                        act.wait_ge(ntop_ready, NG3 * b + k + 1)
                        wait_reuse(act, turned, NG3 * b + max(k - 2, 0))
                        for i in range(QG):
                            at = QG * k + i
                            a = nc.scalar.activation(ex[k % 3][:, i, :], p_s[0:QR, k % 2, i * T:(i + 1) * T],
                                                     ACT.Exp, bias=ntop[:, at:at + 1], accum_out=esum[:, at:at + 1])
                        a.then_inc(exp_done, 1)
                    if k >= 2:
                        copy_turned(k - 2)
                    place(k)

            def copy_ct(b, p):
                act.wait_ge(context_done, b + 1)
                wait_reuse(act, proj_done, b)
                nc.scalar.copy(ct[:], p_ct[:, :, 0:T]).then_inc(ct_copied, 1)

            pipelined(act, [copy_xt, copy_qk, split_heads], second, [copy_ct],
                      {1: [("third", 0)], 4: [("first", 0)], 5: [("first", 1)], 7: [("first", 2)]})

        @block.tensor
        def _(pe):
            pe.wait_ge(const_in, 16 * len(consts))
            pe.wait_ge(cleared, 8)

            def first(b, p):
                pe.wait_ge(xn_ready, b + 1)
                wait_reuse(pe, hnew_ready, b - 1)
                wait_reuse(pe, v_ready, b)
                for g in range(G):
                    for j in range(2):
                        mm = nc.tensor.transpose(p_xt[:, g, T0[j]:T0[j] + TR], xn[:, j, g * GF:(g + 1) * GF],
                                                 ident[0:TR, 0:TR])
                mm.then_inc(xt_done, 1)

            def project_in(b, p):
                pe.wait_ge(xt_copied, b + 1)
                wait_reuse(pe, q_block_ready, 4 * b)
                for o in range(2 * G):
                    for k in range(G):
                        mm = nc.tensor.matmul(p_q[0:GF, o // 3, (o % 3) * T:(o % 3 + 1) * T],
                                              wqk[:, k, o * GF:(o + 1) * GF], xt[p][:, k, :],
                                              start=(k == 0), stop=(k == G - 1))
                mm.then_inc(qk_done, 1)

            def spread_queries(i):
                def part(b, p):
                    pe.wait_ge(qk_copied, 4 * b + 4)
                    if i >= 2:
                        wait_reuse(pe, q_block_ready, 4 * b + i - 1)
                    for h in range(3 * i, 3 * i + 3):
                        mm = nc.tensor.matmul(p_q[:, i % 2, (h - 3 * i) * TP:(h - 3 * i + 1) * TP],
                                              spread[:, h % HG, :], qk[p][:, h // HG, :], start=True, stop=True)
                    mm.then_inc(spread_done, 1)
                return part

            def second(b, p, place):
                wait_reuse(pe, hnew_ready, b - 1)
                pe.wait_ge(xt_copied, b + 1)
                for j in range(2):
                    for g in range(G):
                        mm = nc.tensor.matmul(p_o[:, j, :], xt[p][:, g, T0[j]:T0[j] + TR], wv[:, g, :],
                                              start=(g == 0), stop=(g == G - 1))
                mm.then_inc(v_done, 1)
                pe.wait_ge(q_heads_ready0, b + 1)
                pe.wait_ge(q_heads_ready1, b + 1)
                pe.wait_ge(q_block_ready, 4 * b + 4)

                def scores(k):
                    wait_reuse(pe, exp_done, NG3 * b + max(k - 1, 0))
                    for i in range(QG):
                        n = QG * k + i
                        out = p_s[0:QR, k % 2, i * T:(i + 1) * T]
                        nc.tensor.matmul(out, q_block[p][:, n, :, :].rearrange("p h q -> p (h q)"),
                                         rel[:, REL_W - T - QB * n:REL_W - QB * n], start=True, stop=False)
                        for g in range(G):
                            mm = nc.tensor.matmul(out, q_heads[p][:, g, n, :, :].rearrange("p h q -> p (h q)"),
                                                  qk[p][:, G + g, 0:T], start=False, stop=(g == G - 1))
                    mm.then_inc(scores_done, 1)

                def turn(k):
                    pe.wait_ge(weights_ready, NG3 * b + k + 1)
                    wait_reuse(pe, turned_copied0, NG3 * b + k)
                    wait_reuse(pe, turned_copied1, NG3 * b + k)
                    for j in range(2):
                        for i in range(QG):
                            mm = nc.tensor.transpose(p_t[0:TR, j, i * QR:(i + 1) * QR],
                                                     ex[k % 3][:, i, T0[j]:T0[j] + TR], ident[0:QR, 0:QR])
                    mm.then_inc(turned, 1)

                for k in range(NG3 + 2):
                    if k < NG3:
                        scores(k)
                    if k >= 2:
                        turn(k - 2)
                    place(k)

            def context(g):
                def part(b, p):
                    pe.wait_ge(v_ready, b + 1)
                    pe.wait_ge(turned_copied0, NG3 * b + NG3)
                    pe.wait_ge(turned_copied1, NG3 * b + NG3)
                    wait_reuse(pe, ct_copied, b)
                    for h in range(HG):
                        for j in range(2):
                            mm = nc.tensor.matmul(
                                p_ct[:, g, :], v_pad[p][0:TOWN[j], j, g * HG + h, V0 - h * HS:V0 - h * HS + GF],
                                ex_t[p][0:TOWN[j], j, g * HG + h, :], start=(h == 0 and j == 0),
                                stop=(h == HG - 1 and j == 1))
                    if g == G - 1:
                        mm.then_inc(context_done, 1)
                return part

            def project_out(b, p):
                pe.wait_ge(ct_copied, b + 1)
                pe.wait_ge(v_ready, b + 2 if not isinstance(b, int) else min(b + 2, B))
                for j in range(2):
                    for g in range(G):
                        mm = nc.tensor.matmul(p_o[:, j, :], ct[:, g, T0[j]:T0[j] + TR], wo[:, g, :],
                                              start=(g == 0), stop=(g == G - 1))
                mm.then_inc(proj_done, 1)

            pipelined(pe, [first, project_in] + [spread_queries(i) for i in range(4)], second,
                      [context(0), context(1), project_out],
                      {0: [("third", 0)], 1: [("third", 1)], 3: [("third", 2)], 4: [("first", 0)],
                       5: [("first", 1)], 6: [("first", 2), ("first", 3)], 7: [("first", 4), ("first", 5)]})



NTILE = S // 128
CH = 4
NCH = NTILE // CH
E0 = 8
H0 = 768
M0 = H0 // 128
KEPT = 2 * S
E1 = 9
I1 = 96

PC = 256
NCHK = -(-(KEPT + 8 * (PC - 1) - PC + 1) // PC)
MAX_CH = -(-S // PC)
SLOTS = NCHK * PC // 128
SL = 6
ROUND = 1.5 * 2 ** 23


def in_pairs(eng, step):
    for p in range(2):
        step(p, p)
    with eng.Fori(1, NTILE // 2) as pair:
        for p in range(2):
            step(pair * 2 + p, p)
    step(NTILE - 1, 0)


def over_chunks(eng, step):
    step(0, CH)
    with eng.Fori(1, NCH) as i:
        step(i, CH)
    step(NCH, NTILE - NCH * CH)


@stage
def build_norm(nc, pre, h_in, ident_in, gate_in, t, n_gate):
    with ExitStack() as ctx:
        def sb(name, shape):
            return ctx.enter_context(nc.sbuf_tensor(pre + name, shape, F32))

        def sem(name):
            return nc.alloc_semaphore(name=pre + name)

        h, xt, logits, ident = t["h"], t.get("xt"), t["logits"], t["ident"]
        wg = sb("wg", [GF, G, n_gate])
        stats = sb("stats", [128, NTILE, 6])
        mean = sb("mean", [128, NTILE])
        gap = sb("gap", [128, NTILE])
        sq = sb("sq", [128, NTILE])
        var = sb("var", [128, NTILE])
        half = sb("half", [128, NTILE])
        rstd = sb("rstd", [128, NTILE])
        xn = [sb(f"xn{p}", [128, D]) for p in range(2)]
        xs = [sb(f"xs{p}", [GF, G, 128]) for p in range(2)]
        p_x = ctx.enter_context(nc.psum_tensor(pre + "p_x", [128, 2, 512], F32))
        p_l = ctx.enter_context(nc.psum_tensor(pre + "p_l", [128, 512], F32))

        LOAD = 8
        loaded = sem("loaded")
        h_loaded = [sem(f"h_loaded{k}") for k in range(NTILE // LOAD + 1)]
        half_ready = sem("half_ready")
        stats_ready = sem("stats_ready")
        vec = sem("vec")
        var_ready = sem("var_ready")
        rstd_ready = sem("rstd_ready")
        xn_ready = sem("xn_ready")
        xt_done = sem("xt_done")
        xs_copied = sem("xs_copied")
        xt_copied = sem("xt_copied")
        logits_done = sem("logits_done")
        block = ctx.enter_context(nc.Block())

        @block.sync
        def _(sp):
            for k in range(NTILE // LOAD + 1):
                tiles = slice(k * LOAD, min((k + 1) * LOAD, NTILE))
                sp.dma_start(h[:, tiles, :], h_in.rearrange("(t p) f -> p t f", p=128)[:, tiles, :]
                             ).then_inc(h_loaded[k], 16)
            sp.dma_start(wg[:], gate_in).then_inc(loaded, 16)
            sp.dma_start(ident[:], ident_in).then_inc(loaded, 16)

        @block.gpsimd
        def _(pool):
            nc.gpsimd.memset(half[:], -0.5).then_inc(half_ready, 1)
            pool.wait_ge(half_ready, 1)
            pool.wait_ge(var_ready, 1)
            nc.gpsimd.tensor_tensor(rstd[:], var[:], half[:], ALU.pow).then_inc(rstd_ready, 1)

        @block.vector
        def _(dve):
            for i in range(NTILE):
                if i % LOAD == 0:
                    dve.wait_ge(h_loaded[i // LOAD], 16)
                nc.vector.bn_stats(stats[:, i, :], h[:, i, :]).then_inc(stats_ready, 1)
            dve.wait_ge(stats_ready, NTILE)
            nc.vector.tensor_tensor(mean[:], stats[:, :, 1], stats[:, :, 4], ALU.add).then_inc(vec, 1)
            nc.vector.tensor_tensor(gap[:], stats[:, :, 1], stats[:, :, 4], ALU.subtract).then_inc(vec, 1)
            nc.vector.tensor_tensor(var[:], stats[:, :, 2], stats[:, :, 5], ALU.add).then_inc(vec, 1)
            dve.wait_ge(vec, 3)
            nc.vector.tensor_scalar(mean[:], mean[:], 0.5, None, ALU.mult).then_inc(vec, 1)
            nc.vector.scalar_tensor_tensor(sq[:], gap[:], 0.25, gap[:], ALU.mult, ALU.mult).then_inc(vec, 1)
            nc.vector.tensor_scalar(var[:], var[:], 1.0 / D, EPS, ALU.mult, ALU.add).then_inc(vec, 1)
            dve.wait_ge(vec, 6)
            nc.vector.tensor_tensor(var[:], var[:], sq[:], ALU.add).then_inc(var_ready, 1)
            dve.wait_ge(rstd_ready, 1)

            def step(i, p):
                wait_reuse(dve, xt_done, i - 1)
                at = h[:, bass.ds(i, 1), :].rearrange("p a f -> p (a f)")
                nc.vector.tensor_scalar(xn[p][:], at, mean[:, bass.ds(i, 1)], rstd[:, bass.ds(i, 1)],
                                        ALU.subtract, ALU.mult).then_inc(xn_ready, 1)
                nc.vector.tensor_scalar(t["rows"][:, bass.ds(i, 1), 0:D].rearrange("p a f -> p (a f)"), at,
                                        mean[:, bass.ds(i, 1)], rstd[:, bass.ds(i, 1)], ALU.subtract, ALU.mult)
                if xt is not None and not (isinstance(i, int) and i == 0):
                    keep(i - 1, 1 - p)

            def keep(i, p):
                dve.wait_ge(xs_copied, i + 1)
                nc.vector.tensor_copy(xt[:, :, bass.ds(i * 128, 128)], xs[p][:]).then_inc(xt_copied, 1)

            in_pairs(dve, step)
            if xt is not None:
                keep(NTILE - 1, 0)
            dve.wait_ge(logits_done, NTILE)
            nc.vector.tensor_copy(logits[:], p_l[:, 0:NTILE * n_gate].rearrange("p (t e) -> p t e", e=n_gate)
                                  ).then_inc(vec, 1)

        @block.scalar
        def _(act):
            def step(i, p):
                act.wait_ge(xt_done, i + 1)
                wait_reuse(act, logits_done, i - 1)
                if xt is not None:
                    wait_reuse(act, xt_copied, i - 1)
                nc.scalar.copy(xs[p][:], p_x[0:GF, p, 0:G * 128].rearrange("p (g t) -> p g t", g=G)
                               ).then_inc(xs_copied, 1)

            in_pairs(act, step)

        @block.tensor
        def _(pe):
            pe.wait_ge(loaded, 32)

            def step(i, p):
                pe.wait_ge(xn_ready, i + 1)
                wait_reuse(pe, xs_copied, i - 1)
                for g in range(G):
                    mm = nc.tensor.transpose(p_x[0:GF, p, g * 128:(g + 1) * 128], xn[p][:, g * GF:(g + 1) * GF],
                                             ident[:])
                mm.then_inc(xt_done, 1)
                if not (isinstance(i, int) and i == 0):
                    gate_logits(i - 1, 1 - p)

            def gate_logits(i, p):
                pe.wait_ge(xs_copied, i + 1)
                for g in range(G):
                    mm = nc.tensor.matmul(p_l[:, bass.ds(i * n_gate, n_gate)], xs[p][:, g, :], wg[:, g, :],
                                          start=(g == 0), stop=(g == G - 1))
                mm.then_inc(logits_done, 1)

            in_pairs(pe, step)
            gate_logits(NTILE - 1, 0)


def expert_softmax(nc, dve, vec, at, exp_done, logits, shifted, stat, n):
    wide = [128, NTILE, n]
    nc.vector.tensor_reduce(stat[:], logits[:], AX, ALU.max).then_inc(vec, 1)
    dve.wait_ge(vec, at + 1)
    nc.vector.tensor_tensor(shifted[:], logits[:], stat[:].unsqueeze(2).broadcast_to(wide), ALU.subtract
                            ).then_inc(vec, 1)
    dve.wait_ge(exp_done, 1)
    nc.vector.reduce_sum(stat[:], shifted[:], AX).then_inc(vec, 1)
    dve.wait_ge(vec, at + 3)
    nc.vector.reciprocal(stat[:], stat[:]).then_inc(vec, 1)
    dve.wait_ge(vec, at + 4)
    nc.vector.tensor_tensor(logits[:], shifted[:], stat[:].unsqueeze(2).broadcast_to(wide), ALU.mult
                            ).then_inc(vec, 1)
    dve.wait_ge(vec, at + 5)
    return at + 5


@stage
def build_gate0(nc, c, t):
    with ExitStack() as ctx:
        def sb(name, shape, dt=F32):
            return ctx.enter_context(nc.sbuf_tensor("g0_" + name, shape, dt))

        def sem(name):
            return nc.alloc_semaphore(name="g0_" + name)

        NP = 15
        logits, gate = t["logits"], t["gate"]
        shifted = sb("shifted", [128, NTILE, E0])
        stat = sb("stat", [128, NTILE])
        score = sb("score", [128, E0, NTILE])
        above = sb("above", [128, E0, NTILE])
        tested = [sb(f"tested{v}", [128, E0, NTILE]) for v in range(3)]
        ties = sb("ties", [128, E0, NTILE])
        tie_rank = sb("tie_rank", [128, E0 * NTILE])
        before = sb("before", [128, E0 * NTILE])
        room = sb("room", [128, 1])
        count = sb("count", [128, 3])
        bits = sb("bits", [128, 3 * NP], I32)
        bits_f = sb("bits_f", [128, 3 * NP])
        fits = sb("fits", [128, 3])
        found = sb("found", [128, 1], I32)
        tried = sb("tried", [128, 3], I32)
        kept = sb("kept", [128, 1], I32)
        ones = sb("ones", [128, 128])
        lower = sb("lower", [128, 128])
        p_c = ctx.enter_context(nc.psum_tensor("g0_p_c", [128, 512], F32))
        p_r = ctx.enter_context(nc.psum_tensor("g0_p_r", [128, 512], F32))
        p_t = ctx.enter_context(nc.psum_tensor("g0_p_t", [128, 512], F32))

        loaded = sem("loaded")
        cleared = sem("cleared")
        vec = sem("vec")
        shift_done = sem("shift_done")
        exp_done = sem("exp_done")
        tried_ready = sem("tried_ready")
        counted = sem("counted")
        summed = sem("summed")
        fits_ready = sem("fits_ready")
        kept_ready = sem("kept_ready")
        found_ready = sem("found_ready")
        masks_ready = sem("masks_ready")
        ranks_done = sem("ranks_done")
        block = ctx.enter_context(nc.Block())

        @block.sync
        def _(sp):
            for dst, src in ((bits[:], c["bits"]), (bits_f[:], c["bits_f"]), (ones[:], c["ones"]),
                             (lower[:], c["lower"])):
                sp.dma_start(dst, src).then_inc(loaded, 16)

        @block.scalar
        def _(act):
            act.wait_ge(vec, 2)
            nc.scalar.activation(shifted[:], shifted[:], ACT.Exp).then_inc(exp_done, 1)

        @block.vector
        def _(dve):
            dve.wait_ge(loaded, 64)
            at = expert_softmax(nc, dve, vec, 0, exp_done, logits, shifted, stat, E0)
            nc.vector.tensor_copy(score[:], logits[:].rearrange("p t e -> p e t")).then_inc(vec, 1)
            nc.vector.memset(found[:], 0).then_inc(vec, 1)
            dve.wait_ge(vec, at + 2)
            with dve.Fori(0, NP) as i:
                nc.vector.tensor_tensor(tried[:], found[:].broadcast_to([128, 3]), bits[:, bass.ds(i * 3, 3)],
                                        ALU.bitwise_or).then_inc(tried_ready, 1)
                dve.wait_ge(tried_ready, i + 1)
                for v in range(3):
                    n = nc.vector.tensor_scalar(tested[v][:], score[:], tried[:, v:v + 1].bitcast(F32), 0.0, ALU.is_ge,
                                                ALU.add, accum_out=count[:, v:v + 1])
                n.then_inc(counted, 1)
                dve.wait_ge(summed, i + 1)
                nc.vector.scalar_tensor_tensor(fits[:], p_c[:, 0:3], float(KEPT), bits_f[:, bass.ds(i * 3, 3)],
                                               ALU.is_ge, ALU.mult).then_inc(fits_ready, 1)
                dve.wait_ge(fits_ready, i + 1)
                nc.vector.tensor_reduce(kept[:], fits[:], AX, ALU.max).then_inc(kept_ready, 1)
                dve.wait_ge(kept_ready, i + 1)
                nc.vector.tensor_tensor(found[:], found[:], kept[:], ALU.bitwise_or).then_inc(found_ready, 1)
                dve.wait_ge(found_ready, i + 1)
            nc.vector.tensor_scalar(above[:], score[:], found[:].bitcast(F32), 0.0, ALU.is_gt, ALU.add,
                                    accum_out=count[:, 0:1]).then_inc(masks_ready, 1)
            nc.vector.tensor_scalar(ties[:], score[:], found[:].bitcast(F32), None, ALU.is_equal
                                    ).then_inc(masks_ready, 1)
            dve.wait_ge(ranks_done, 1)
            nc.vector.tensor_scalar(room[:], p_c[:, 3:4], -1.0, float(KEPT), ALU.mult, ALU.add).then_inc(vec, 1)
            nc.vector.tensor_copy(tie_rank[:], p_t[:, 0:E0 * NTILE]).then_inc(vec, 1)
            dve.wait_ge(vec, at + 4)
            nc.vector.tensor_tensor_scan(before[:], ones[:, 0:1].broadcast_to([128, E0 * NTILE]), tie_rank[:], 0.0,
                                         ALU.mult, ALU.add).then_inc(vec, 1)
            dve.wait_ge(vec, at + 5)
            nc.vector.tensor_tensor(before[:], before[:], tie_rank[:], ALU.subtract).then_inc(vec, 1)
            dve.wait_ge(vec, at + 6)
            nc.vector.tensor_tensor(tie_rank[:], p_r[:, 0:E0 * NTILE], before[:], ALU.add).then_inc(vec, 1)
            dve.wait_ge(vec, at + 7)
            nc.vector.scalar_tensor_tensor(before[:], tie_rank[:], room[:], ties[:].rearrange("p e t -> p (e t)"),
                                           ALU.is_lt, ALU.mult).then_inc(vec, 1)
            dve.wait_ge(vec, at + 8)
            nc.vector.tensor_tensor(above[:], above[:], before[:].rearrange("p (e t) -> p e t", e=E0), ALU.add
                                    ).then_inc(vec, 1)
            dve.wait_ge(vec, at + 9)
            nc.vector.tensor_tensor(gate[:], score[:].rearrange("p e t -> p t e"),
                                    above[:].rearrange("p e t -> p t e"), ALU.mult).then_inc(vec, 1)

        @block.tensor
        def _(pe):
            pe.wait_ge(loaded, 64)
            with pe.Fori(0, NP) as i:
                pe.wait_ge(counted, i + 1)
                nc.tensor.matmul(p_c[:, 0:3], ones[:], count[:], start=True, stop=True).then_inc(summed, 1)
            pe.wait_ge(masks_ready, 2)
            nc.tensor.matmul(p_c[:, 3:4], ones[:], count[:, 0:1], start=True, stop=True)
            flat = ties[:].rearrange("p e t -> p (e t)")
            nc.tensor.matmul(p_r[:, 0:E0 * NTILE], lower[:], flat, start=True, stop=True)
            nc.tensor.matmul(p_t[:, 0:E0 * NTILE], ones[:], flat, start=True, stop=True).then_inc(ranks_done, 1)


@stage
def build_gate1(nc, c, t):
    with ExitStack() as ctx:
        def sb(name, shape, dt=F32):
            return ctx.enter_context(nc.sbuf_tensor("g1_" + name, shape, dt))

        def sem(name):
            return nc.alloc_semaphore(name="g1_" + name)

        E, GR = E1 - 1, (E1 - 1) // 2
        logits, gate = t["logits"], t["gate"]
        shifted = sb("shifted", [128, NTILE, E])
        stat = sb("stat", [128, NTILE])
        bias = sb("bias", [128, E])
        biased = sb("biased", [128, NTILE, E])
        group = sb("group", [128, NTILE, GR])
        out_of_group = sb("out_of_group", [128, NTILE, GR])
        earlier = sb("earlier", [128, E, E])
        better = sb("better", [128, NTILE, E, E])
        equal = sb("equal", [128, NTILE, E, E])
        rank = sb("rank", [128, NTILE, E])
        loaded = sem("loaded")
        vec = sem("vec")
        exp_done = sem("exp_done")
        block = ctx.enter_context(nc.Block())

        @block.sync
        def _(sp):
            sp.dma_start(bias[:], c["gate_b"].broadcast_to([128, E])).then_inc(loaded, 16)
            sp.dma_start(earlier[:], c["earlier"]).then_inc(loaded, 16)

        @block.scalar
        def _(act):
            act.wait_ge(vec, 2)
            nc.scalar.activation(shifted[:], shifted[:], ACT.Exp).then_inc(exp_done, 1)

        @block.vector
        def _(dve):
            steps = [0]

            def link(ins):
                steps[0] += 1
                ins.then_inc(vec, 1)
                dve.wait_ge(vec, steps[0])

            def ranks(x, n, out):
                a = better[:].rearrange("p t i j -> p t (i j)")[:, :, 0:n * n].rearrange("p t (i j) -> p t i j", i=n)
                q = equal[:].rearrange("p t i j -> p t (i j)")[:, :, 0:n * n].rearrange("p t (i j) -> p t i j", i=n)
                for i in range(n):
                    mine = x[:, :, i:i + 1].broadcast_to([128, NTILE, n])
                    nc.vector.tensor_tensor(a[:, :, i, :], x, mine, ALU.is_gt).then_inc(vec, 1)
                    nc.vector.tensor_tensor(q[:, :, i, :], x, mine, ALU.is_equal).then_inc(vec, 1)
                steps[0] += 2 * n
                dve.wait_ge(vec, steps[0])
                for i in range(n):
                    nc.vector.tensor_tensor(q[:, :, i, :], q[:, :, i, :],
                                            earlier[:, i:i + 1, 0:n].broadcast_to([128, NTILE, n]), ALU.mult
                                            ).then_inc(vec, 1)
                steps[0] += n
                dve.wait_ge(vec, steps[0])
                link(nc.vector.tensor_tensor(a, a, q, ALU.add))
                link(nc.vector.reduce_sum(out, a, AX))

            dve.wait_ge(loaded, 32)
            steps[0] = expert_softmax(nc, dve, vec, 0, exp_done, logits, shifted, stat, E)
            link(nc.vector.tensor_tensor(biased[:], logits[:], bias[:].unsqueeze(1).broadcast_to([128, NTILE, E]),
                                         ALU.add))
            link(nc.vector.tensor_tensor(group[:], biased[:, :, 0:E:2], biased[:, :, 1:E:2], ALU.add))
            ranks(group[:], GR, out_of_group[:])
            link(nc.vector.tensor_scalar(out_of_group[:], out_of_group[:], 2.0, -1e30, ALU.is_ge, ALU.mult))
            for i in range(2):
                link(nc.vector.tensor_tensor(biased[:, :, i:E:2], biased[:, :, i:E:2], out_of_group[:], ALU.add))
            ranks(biased[:], E, rank[:])
            link(nc.vector.tensor_scalar(rank[:], rank[:], 2.0, None, ALU.is_lt))
            link(nc.vector.tensor_tensor(gate[:, :, 0:E], logits[:], rank[:], ALU.mult))
            link(nc.vector.memset(gate[:, :, E:E1], 1.0))


@stage
def build_dispatch(nc, pre, w2_rows, picks, c, t, h_out, rows):
    with ExitStack() as ctx:
        def sb(name, shape, dt=F32):
            return ctx.enter_context(nc.sbuf_tensor(pre + name, shape, dt))

        def sem(name):
            return nc.alloc_semaphore(name=pre + name)

        E, ET = 8, 8 * NTILE
        gate, table, chosen = t["gate"], t["table"], t["chosen"]
        lower = sb("lower", [128, 128])
        iota = sb("iota", [128, 128])
        part = sb("part", [128, 2])
        dummy = sb("dummy", [128, SLOTS])
        starts = sb("starts", [128, MAX_CH])
        ones = sb("ones", [128, 128])
        zeros = sb("zeros", [128, 2, D + 9])
        sel = sb("sel", [128, E, NTILE])
        tot = sb("tot", [128, ET])
        before = sb("before", [128, E, NTILE])
        cnt = sb("cnt", [128, E])
        above = sb("above", [128, E, MAX_CH])
        n_ch = sb("n_ch", [128, E])
        end_ch = sb("end_ch", [128, E])
        base = sb("base", [128, E])
        pos = sb("pos", [128, E, NTILE])
        near = sb("near", [128, E, NTILE])
        lo = sb("lo", [128, NTILE, picks])
        hi = sb("hi", [128, NTILE, picks])
        lo_all = sb("lo_all", [128, E, NTILE])
        earlier = sb("earlier", [128, E, NTILE])
        this = sb("this", [128, E, NTILE])
        term = sb("term", [128, E, NTILE])
        kth_hi = sb("kth_hi", [128, NTILE])
        over = sb("over", [128, NCHK, E - 1])
        ch_expert = sb("ch_expert", [128, NCHK])
        lo_hot = [sb(f"lo_hot{p}", [128, picks, 128], BF16) for p in range(2)]
        hi_hot = [sb(f"hi_hot{p}", [128, picks, SLOTS], BF16) for p in range(2)]
        hi_val = [sb(f"hi_val{p}", [128, picks, 2, SLOTS], BF16) for p in range(2)]
        listed_s = sb("listed_s", [128, 2, SLOTS])
        token = sb("token", [128, SLOTS])
        p_r = ctx.enter_context(nc.psum_tensor(pre + "p_r", [128, 512], F32))
        p_t = ctx.enter_context(nc.psum_tensor(pre + "p_t", [128, 512], F32))
        p_s = ctx.enter_context(nc.psum_tensor(pre + "p_s", [128, 512], F32))

        loaded = sem("loaded")
        cleared = sem("cleared")
        stored = sem("stored")
        vec = sem("vec")
        sel_ready = sem("sel_ready")
        counted = sem("counted")
        lo_ready = sem("lo_ready")
        hi_ready = sem("hi_ready")
        val_ready = sem("val_ready")
        listed = sem("listed")
        consts = [(lower[:], c["lower"]), (iota[:], c["iota"]), (part[:], c["part"]), (dummy[:], c["dummy"]),
                  (starts[:], c["starts"])]
        block = ctx.enter_context(nc.Block())

        @block.sync
        def _(sp):
            for dst, src in consts:
                sp.dma_start(dst, src).then_inc(loaded, 16)
            sp.dma_start(rows[0:S, :].rearrange("(t p) f -> p t f", p=128), t["rows"][:]).then_inc(stored, 16)
            sp.dma_start(h_out[0:S, :].rearrange("(t p) f -> p t f", p=128), t["h"][:]).then_inc(stored, 16)
            sp.wait_ge(cleared, 2)
            sp.dma_start(rows[S:S + 256, :].rearrange("(t p) f -> p t f", p=128), zeros[:, :, 0:rows.shape[1]]
                         ).then_inc(stored, 16)
            sp.dma_start(h_out[S:S + 256, :].rearrange("(t p) f -> p t f", p=128), zeros[:, :, 0:D]
                         ).then_inc(stored, 16)
            sp.wait_ge(stored, 64)

        @block.gpsimd
        def _(pool):
            nc.gpsimd.memset(ones[:], 1.0).then_inc(cleared, 1)
            nc.gpsimd.memset(zeros[:], 0.0).then_inc(cleared, 1)

        @block.vector
        def _(dve):
            steps = [0]

            def link(ins):
                steps[0] += 1
                ins.then_inc(vec, 1)
                dve.wait_ge(vec, steps[0])

            nc.vector.tensor_scalar(sel[:], gate[:, :, 0:E].rearrange("p t e -> p e t"), 0.0, None, ALU.is_gt
                                    ).then_inc(sel_ready, 1)
            dve.wait_ge(loaded, 16 * len(consts))
            dve.wait_ge(cleared, 2)
            dve.wait_ge(counted, 1)
            link(nc.vector.tensor_copy(tot[:], p_t[:, 0:ET]))
            flat = before[:].rearrange("p e t -> p (e t)")
            link(nc.vector.tensor_tensor_scan(flat, ones[:, 0:1].broadcast_to([128, ET]), tot[:], 0.0,
                                              ALU.mult, ALU.add))
            link(nc.vector.tensor_tensor(flat, flat, tot[:], ALU.subtract))
            link(nc.vector.reduce_sum(cnt[:], tot[:].rearrange("p (e t) -> p e t", e=E), AX))
            link(nc.vector.tensor_tensor(above[:], cnt[:].unsqueeze(2).broadcast_to([128, E, MAX_CH]),
                                         starts[:].unsqueeze(1).broadcast_to([128, E, MAX_CH]), ALU.is_gt))
            link(nc.vector.reduce_sum(n_ch[:], above[:], AX))
            link(nc.vector.tensor_tensor_scan(end_ch[:], ones[:, 0:E], n_ch[:], 0.0, ALU.mult, ALU.add))
            link(nc.vector.tensor_tensor(base[:], end_ch[:], n_ch[:], ALU.subtract))
            link(nc.vector.scalar_tensor_tensor(base[:], base[:], float(PC), before[:, :, 0], ALU.mult, ALU.subtract))
            link(nc.vector.tensor_tensor(pos[:], p_r[:, 0:ET].rearrange("p (e t) -> p e t", e=E), before[:], ALU.add))
            link(nc.vector.tensor_tensor(pos[:], pos[:], base[:].unsqueeze(2).broadcast_to([128, E, NTILE]), ALU.add))
            link(nc.vector.tensor_scalar(near[:], pos[:], 1.0 / 128, -63.5 / 128, ALU.mult, ALU.add))
            link(nc.vector.tensor_scalar(near[:], near[:], ROUND, None, ALU.add))
            link(nc.vector.tensor_scalar(near[:], near[:], -ROUND, None, ALU.add))
            link(nc.vector.scalar_tensor_tensor(lo_all[:], near[:], -128.0, pos[:], ALU.mult, ALU.add))
            if picks == E:
                link(nc.vector.tensor_copy(lo[:].rearrange("p t e -> p e t"), lo_all[:]))
                link(nc.vector.scalar_tensor_tensor(near[:], sel[:], -1000.0, near[:], ALU.mult, ALU.add))
                link(nc.vector.tensor_scalar(hi[:].rearrange("p t e -> p e t"), near[:], 1000.0, None, ALU.add))
            else:
                link(nc.vector.memset(earlier[:, 0, :], 0.0))
                for e in range(1, E):
                    link(nc.vector.tensor_tensor(earlier[:, e, :], earlier[:, e - 1, :], sel[:, e - 1, :], ALU.add))
                link(nc.vector.tensor_scalar(near[:], near[:], -1000.0, None, ALU.add))
                for k in range(picks):
                    link(nc.vector.scalar_tensor_tensor(this[:], earlier[:], float(k), sel[:], ALU.is_equal, ALU.mult))
                    link(nc.vector.tensor_tensor(term[:], this[:], lo_all[:], ALU.mult))
                    link(nc.vector.reduce_sum(lo[:, :, k], term[:].rearrange("p e t -> p t e"), AX))
                    link(nc.vector.tensor_tensor(term[:], this[:], near[:], ALU.mult))
                    link(nc.vector.reduce_sum(kth_hi[:], term[:].rearrange("p e t -> p t e"), AX))
                    link(nc.vector.tensor_scalar(hi[:, :, k], kth_hi[:], 1000.0, None, ALU.add))
            link(nc.vector.tensor_tensor(over[:], iota[:, 0:NCHK].unsqueeze(2).broadcast_to([128, NCHK, E - 1]),
                                         end_ch[:, 0:E - 1].unsqueeze(1).broadcast_to([128, NCHK, E - 1]), ALU.is_ge))
            link(nc.vector.reduce_sum(ch_expert[:], over[:], AX))
            for at, n in ((2, GF), (3, w2_rows)):
                link(nc.vector.tensor_scalar(table[:, :, at], ch_expert[:], float(n), part[:, 0:1], ALU.mult, ALU.add))
            link(nc.vector.tensor_tensor(chosen[:], ch_expert[:].unsqueeze(2).broadcast_to([128, NCHK, E]),
                                         iota[:, 0:E].unsqueeze(1).broadcast_to([128, NCHK, E]), ALU.is_equal))

            def step(i, p):
                wait_reuse(dve, listed, i - 1)
                for hot, x, n, ready in ((hi_hot, hi, SLOTS, hi_ready), (lo_hot, lo, 128, lo_ready)):
                    nc.vector.tensor_tensor(
                        hot[p][:], iota[:, 0:n].unsqueeze(1).broadcast_to([128, picks, n]),
                        x[:, bass.ds(i, 1), :].rearrange("p a e -> p (a e)").unsqueeze(2).broadcast_to([128, picks, n]),
                        ALU.is_equal).then_inc(ready, 1)

            in_pairs(dve, step)
            dve.wait_ge(listed, NTILE)
            link(nc.vector.tensor_copy(listed_s[:], p_s[:, 0:2 * SLOTS].rearrange("p (v s) -> p v s", v=2)))
            link(nc.vector.scalar_tensor_tensor(token[:], listed_s[:, 1, :], 128.0, listed_s[:, 0, :],
                                                ALU.mult, ALU.add))
            link(nc.vector.scalar_tensor_tensor(token[:], token[:], -1.0, dummy[:], ALU.add, ALU.subtract))
            link(nc.vector.scalar_tensor_tensor(token[:], listed_s[:, 0, :], 0.0, token[:], ALU.is_gt, ALU.mult))
            link(nc.vector.tensor_tensor(table[:, :, 0:2], token[:].rearrange("p (c a) -> p c a", a=2),
                                         dummy[:].rearrange("p (c a) -> p c a", a=2), ALU.add))

        @block.scalar
        def _(act):
            act.wait_ge(loaded, 16 * len(consts))

            def step(i, p):
                act.wait_ge(hi_ready, i + 1)
                wait_reuse(act, listed, i - 1)
                nc.scalar.activation(hi_val[p][:, :, 0, :], hi_hot[p][:], ACT.Copy, scale=part[:, 1:2]
                                     ).then_inc(val_ready, 1)
                nc.scalar.activation(hi_val[p][:, :, 1, :], hi_hot[p][:], ACT.Copy, scale=iota[:, bass.ds(i, 1)]
                                     ).then_inc(val_ready, 1)

            in_pairs(act, step)

        @block.tensor
        def _(pe):
            pe.wait_ge(loaded, 16 * len(consts))
            pe.wait_ge(cleared, 2)
            pe.wait_ge(sel_ready, 1)
            flat = sel[:].rearrange("p e t -> p (e t)")
            nc.tensor.matmul(p_r[:, 0:ET], lower[:], flat, start=True, stop=True)
            nc.tensor.matmul(p_t[:, 0:ET], ones[:], flat, start=True, stop=True).then_inc(counted, 1)

            def step(i, p):
                pe.wait_ge(lo_ready, i + 1)
                pe.wait_ge(val_ready, 2 * i + 2)
                for k in range(picks):
                    mm = nc.tensor.matmul(p_s[:, 0:2 * SLOTS], lo_hot[p][:, k, :],
                                          hi_val[p][:, k, :, :].rearrange("p v s -> p (v s)"),
                                          start=(isinstance(i, int) and i == 0 and k == 0),
                                          stop=(isinstance(i, int) and i == NTILE - 1 and k == picks - 1))
                mm.then_inc(listed, 1)

            in_pairs(pe, step)


def ahead(i, s, n):
    i, s = i + (s + n) // SL, (s + n) % SL
    return None if isinstance(i, int) and SL * i + s >= NCHK else (i, s)


def in_rounds(eng, step):
    for s in range(SL):
        step(0, s)
    with eng.Fori(1, NCHK // SL - 1) as i:
        for s in range(SL):
            step(i, s)
    for s in range(SL):
        step(NCHK // SL - 1, s)


@stage
def build_sparse0(nc, c, t, rows, h_out):
    with ExitStack() as ctx:
        def sb(name, shape, dt=F32):
            return ctx.enter_context(nc.sbuf_tensor("s0_" + name, shape, dt))

        def sem(name):
            return nc.alloc_semaphore(name="s0_" + name)

        NR = 3
        B1, B2 = M0 * D, M0 * D + M0
        RW = rows.shape[1]
        table, chosen = t["table"], t["chosen"]
        w1_rows, w2_rows = c["w1"], c["w2"]
        at = [sb(f"at{s}", [128, 4], I32) for s in range(SL)]
        x = [[sb(f"x{s}{a}", [128, RW]) for a in range(2)] for s in range(SL)]
        w1 = [sb(f"w1{s}", [GF, G * H0]) for s in range(SL)]
        w2 = [sb(f"w2{s}", [128, B2 + D]) for s in range(SL)]
        xt = [sb(f"xt{s}", [GF, G, PC]) for s in range(2)]
        hid = [sb(f"hid{k}", [128, PC]) for k in range(NR)]
        one = sb("one", [128, 1])
        carrier = sb("carrier", [128, 2])
        picked = sb("picked", [128, 2, E0])
        gate_s = [sb(f"gate_s{s}", [128, 2]) for s in range(SL)]
        with_b2 = sb("with_b2", [128, 2, D])
        y = [[sb(f"y{s}{a}", [128, D]) for a in range(2)] for s in range(SL)]
        p_x = ctx.enter_context(nc.psum_tensor("s0_p_x", [128, 512], F32))
        p_h = ctx.enter_context(nc.psum_tensor("s0_p_h", [128, 2, 512], F32))
        p_y = ctx.enter_context(nc.psum_tensor("s0_p_y", [128, 2, 512], F32))
        p_xt = p_x[0:GF, 0:G * PC].rearrange("p (g t) -> p g t", g=G)

        one_ready = sem("one_ready")
        at_ready = sem("at_ready")
        carried = [sem("gather_carried"), sem("scatter_carried")]
        x_in = [sem(f"x_in{s}") for s in range(SL)]
        w1_in = [sem(f"w1_in{s}") for s in range(SL)]
        w2_in = [sem(f"w2_in{s}") for s in range(SL)]
        turned = sem("turned")
        xt_copied = sem("xt_copied")
        picked_ready = sem("picked_ready")
        gate_ready = sem("gate_ready")
        b2_added = sem("b2_added")
        first_done = sem("first_done")
        gelu_done = sem("gelu_done")
        second_done = sem("second_done")
        y_ready = sem("y_ready")
        scattered = sem("scattered")
        block = ctx.enter_context(nc.Block())

        @block.gpsimd
        def _(pool):
            nc.gpsimd.memset(one[:], 1.0).then_inc(one_ready, 1)
            pool.wait_ge(one_ready, 1)

            def carry(k, ch):
                wait_reuse(pool, carried[k], ch)
                nc.gpsimd.tensor_tensor(carrier[:, k:k + 1], one[:], one[:], ALU.mult).then_inc(carried[k], 1)

            def gather(i, s):
                ch = SL * i + s
                pool.wait_ge(at_ready, ch + 1)
                carry(0, ch)
                for a in range(2):
                    nc.gpsimd.indirect_dma_start(x[s][a][:], None, rows[:, :],
                                                 bass.IndirectOffsetOnAxis(ap=at[s][:, a:a + 1], axis=0)
                                                 ).then_inc(x_in[s], 16)
                nc.gpsimd.indirect_dma_start(w1[s][:], None, w1_rows[:, :],
                                             bass.IndirectOffsetOnAxis(ap=at[s][0:GF, 2:3], axis=0)
                                             ).then_inc(w1_in[s], 16)
                nc.gpsimd.indirect_dma_start(w2[s][:], None, w2_rows[:, :],
                                             bass.IndirectOffsetOnAxis(ap=at[s][:, 3:4], axis=0)
                                             ).then_inc(w2_in[s], 16)

            def step(i, s):
                ch = SL * i + s
                pool.wait_ge(y_ready, ch + 1)
                wait_reuse(pool, scattered, 32 * ch)
                carry(1, ch)
                for a in range(2):
                    nc.gpsimd.indirect_dma_start(h_out[:, :],
                                                 bass.IndirectOffsetOnAxis(ap=at[s][:, a:a + 1], axis=0),
                                                 y[s][a][:], None, compute_op=ALU.add).then_inc(scattered, 16)
                nxt = ahead(i, s, SL - 1)
                if nxt:
                    gather(*nxt)

            for s in range(SL - 1):
                gather(0, s)
            in_rounds(pool, step)
            pool.wait_ge(scattered, 32 * NCHK)

        @block.vector
        def _(dve):
            def indices(i, s):
                wait_reuse(dve, scattered, 32 * (SL * i + s - SL + 1))
                nc.vector.tensor_copy(at[s][:], table[:, bass.ds(SL * i + s, 1), :].rearrange("p a k -> p (a k)")
                                      ).then_inc(at_ready, 1)

            def copy_xt(i, s):
                dve.wait_ge(turned, SL * i + s + 1)
                nc.vector.tensor_copy(xt[s % 2][:], p_xt).then_inc(xt_copied, 1)

            def step(i, s):
                ch = SL * i + s
                dve.wait_ge(x_in[s], 32 * i + 32)
                for a in range(2):
                    nc.vector.tensor_tensor(picked[:, a, :], x[s][a][:, D:D + E0],
                                            chosen[:, bass.ds(ch, 1), :].rearrange("p a e -> p (a e)"), ALU.mult
                                            ).then_inc(picked_ready, 1)
                dve.wait_ge(picked_ready, 2 * ch + 2)
                nc.vector.reduce_sum(gate_s[s][:], picked[:], AX).then_inc(gate_ready, 1)
                nxt = ahead(i, s, 1)
                if nxt:
                    copy_xt(*nxt)
                dve.wait_ge(gate_ready, ch + 1)
                dve.wait_ge(second_done, M0 * ch + M0)
                wait_reuse(dve, y_ready, ch)
                nc.vector.tensor_tensor(with_b2[:], p_y[:, s % 2, 0:2 * D].rearrange("p (a f) -> p a f", a=2),
                                        w2[s][:, B2:B2 + D].unsqueeze(1).broadcast_to([128, 2, D]), ALU.add
                                        ).then_inc(b2_added, 1)
                dve.wait_ge(b2_added, ch + 1)
                for a in range(2):
                    v = nc.vector.tensor_scalar(y[s][a][:], with_b2[:, a, :], gate_s[s][:, a:a + 1], None,
                                                ALU.mult)
                v.then_inc(y_ready, 1)
                nxt = ahead(i, s, SL - 1)
                if nxt:
                    indices(*nxt)

            for s in range(SL - 1):
                indices(0, s)
            copy_xt(0, 0)
            in_rounds(dve, step)

        @block.scalar
        def _(act):
            def step(i, s):
                ch = SL * i + s
                act.wait_ge(w2_in[s], 16 * i + 16)
                for k in range(M0):
                    act.wait_ge(first_done, M0 * ch + k + 1)
                    wait_reuse(act, second_done, M0 * ch + k - NR + 1)
                    nc.scalar.activation(hid[k % NR][:], p_h[:, k % 2, 0:PC], ACT.Gelu_apprx_tanh,
                                         bias=w2[s][:, B1 + k:B1 + k + 1]).then_inc(gelu_done, 1)

            in_rounds(act, step)

        @block.tensor
        def _(pe):
            def turn(i, s):
                pe.wait_ge(x_in[s], 32 * i + 32)
                wait_reuse(pe, xt_copied, SL * i + s)
                for a in range(2):
                    for g in range(G):
                        mm = nc.tensor.transpose(p_xt[:, g, a * 128:(a + 1) * 128], x[s][a][:, g * GF:(g + 1) * GF],
                                                 t["ident"][:])
                mm.then_inc(turned, 1)

            def first(i, s, k):
                ch = SL * i + s
                if k == 0:
                    pe.wait_ge(xt_copied, ch + 1)
                    pe.wait_ge(w1_in[s], 16 * i + 16)
                wait_reuse(pe, gelu_done, M0 * ch + k - 1)
                for g in range(G):
                    mm = nc.tensor.matmul(p_h[:, k % 2, 0:PC], w1[s][:, g * H0 + k * 128:g * H0 + (k + 1) * 128],
                                          xt[s % 2][:, g, :], start=(g == 0), stop=(g == G - 1))
                mm.then_inc(first_done, 1)

            def second(i, s, k):
                ch = SL * i + s
                if k == 0:
                    pe.wait_ge(w2_in[s], 16 * i + 16)
                    wait_reuse(pe, y_ready, ch - 1)
                pe.wait_ge(gelu_done, M0 * ch + k + 1)
                for a in range(2):
                    mm = nc.tensor.matmul(p_y[:, s % 2, a * D:(a + 1) * D], hid[k % NR][:, a * 128:(a + 1) * 128],
                                          w2[s][:, k * D:(k + 1) * D], start=(k == 0 and a == 0), stop=(k == M0 - 1),
                                          skip_group_check=True)
                mm.then_inc(second_done, 1)

            def step(i, s):
                nxt = ahead(i, s, 1)
                for k in range(M0):
                    if k + 1 < M0:
                        first(i, s, k + 1)
                    elif nxt:
                        first(*nxt, 0)
                    second(i, s, k)
                    if k == 2 and nxt:
                        turn(*nxt)

            turn(0, 0)
            first(0, 0, 0)
            in_rounds(pe, step)


@stage
def build_sparse1(nc, c, t, rows, h_out):
    with ExitStack() as ctx:
        def sb(name, shape, dt=F32):
            return ctx.enter_context(nc.sbuf_tensor("s1_" + name, shape, dt))

        def sem(name):
            return nc.alloc_semaphore(name="s1_" + name)

        E = E1 - 1
        W2, B13 = G * 4 * I1, G * 4 * I1 + D
        ALPHA, LIMIT = 1.702, 7.0
        RW = rows.shape[1]
        table, chosen = t["table"], t["chosen"]
        w_rows = c["w"]
        at = [sb(f"at{s}", [128, 4], I32) for s in range(SL)]
        x = [[sb(f"x{s}{a}", [128, RW]) for a in range(2)] for s in range(SL)]
        w = [sb(f"w{s}", [I1 + 1, B13 + 4]) for s in range(SL)]
        xt = [sb(f"xt{s}", [GF, G, PC]) for s in range(2)]
        h3 = sb("h3", [I1, 2, PC])
        prod = sb("prod", [I1, 2, PC])
        lin = sb("lin", [I1, PC])
        xg = sb("xg", [I1, PC])
        xl = sb("xl", [I1, PC])
        sg = sb("sg", [I1, PC])
        act_t = [sb(f"act_t{p}", [I1 + 1, PC]) for p in range(2)]
        one = sb("one", [128, 1])
        carrier = sb("carrier", [128, 2])
        picked = sb("picked", [128, 2, E])
        gate_s = [sb(f"gate_s{s}", [128, 2]) for s in range(SL)]
        y = [[sb(f"y{s}{a}", [128, D]) for a in range(2)] for s in range(SL)]
        p_x = ctx.enter_context(nc.psum_tensor("s1_p_x", [128, 512], F32))
        p_h = ctx.enter_context(nc.psum_tensor("s1_p_h", [128, 2, 4, PC], F32))
        p_y = ctx.enter_context(nc.psum_tensor("s1_p_y", [128, 2, 512], F32))
        p_xt = p_x[0:GF, 0:G * PC].rearrange("p (g t) -> p g t", g=G)

        one_ready = sem("one_ready")
        at_ready = sem("at_ready")
        carried = [sem("gather_carried"), sem("scatter_carried")]
        x_in = [sem(f"x_in{s}") for s in range(SL)]
        w_in = [sem(f"w_in{s}") for s in range(SL)]
        turned = sem("turned")
        xt_copied = sem("xt_copied")
        picked_ready = sem("picked_ready")
        gate_ready = sem("gate_ready")
        h3_done = sem("h3_done")
        h1_done = sem("h1_done")
        h3_copied = sem("h3_copied")
        prod_ready = sem("prod_ready")
        xg_ready = sem("xg_ready")
        xl_ready = sem("xl_ready")
        sg_ready = sem("sg_ready")
        lin_ready = sem("lin_ready")
        act_ready = sem("act_ready")
        second_done = sem("second_done")
        y_ready = sem("y_ready")
        scattered = sem("scattered")
        block = ctx.enter_context(nc.Block())

        @block.gpsimd
        def _(pool):
            nc.gpsimd.memset(one[:], 1.0).then_inc(one_ready, 1)
            for p in range(2):
                pool.wait_ge(one_ready, p + 1)
                nc.gpsimd.memset(act_t[p][I1:I1 + 1, :], 1.0).then_inc(one_ready, 1)
            pool.wait_ge(one_ready, 3)

            def carry(k, ch):
                wait_reuse(pool, carried[k], ch)
                nc.gpsimd.tensor_tensor(carrier[:, k:k + 1], one[:], one[:], ALU.mult).then_inc(carried[k], 1)

            def gather(i, s):
                ch = SL * i + s
                pool.wait_ge(at_ready, ch + 1)
                carry(0, ch)
                for a in range(2):
                    nc.gpsimd.indirect_dma_start(x[s][a][:], None, rows[:, :],
                                                 bass.IndirectOffsetOnAxis(ap=at[s][:, a:a + 1], axis=0)
                                                 ).then_inc(x_in[s], 16)
                nc.gpsimd.indirect_dma_start(w[s][:], None, w_rows[:, :],
                                             bass.IndirectOffsetOnAxis(ap=at[s][0:I1 + 1, 3:4], axis=0)
                                             ).then_inc(w_in[s], 16)

            def step(i, s):
                ch = SL * i + s
                pool.wait_ge(y_ready, ch + 1)
                wait_reuse(pool, scattered, 32 * ch)
                carry(1, ch)
                for a in range(2):
                    nc.gpsimd.indirect_dma_start(h_out[:, :],
                                                 bass.IndirectOffsetOnAxis(ap=at[s][:, a:a + 1], axis=0),
                                                 y[s][a][:], None, compute_op=ALU.add).then_inc(scattered, 16)
                nxt = ahead(i, s, SL - 1)
                if nxt:
                    gather(*nxt)

            for s in range(SL - 1):
                gather(0, s)
            in_rounds(pool, step)
            pool.wait_ge(scattered, 32 * NCHK)

        @block.vector
        def _(dve):
            def indices(i, s):
                wait_reuse(dve, scattered, 32 * (SL * i + s - SL + 1))
                nc.vector.tensor_copy(at[s][:], table[:, bass.ds(SL * i + s, 1), :].rearrange("p a k -> p (a k)")
                                      ).then_inc(at_ready, 1)

            def swiglu(i, s):
                ch = SL * i + s
                dve.wait_ge(w_in[s], 16 * i + 16)
                dve.wait_ge(h1_done, ch + 1)
                dve.wait_ge(h3_copied, 2 * ch + 2)
                for o in range(2):
                    nc.vector.scalar_tensor_tensor(prod[:, o, :], p_h[0:I1, s % 2, o, :],
                                                   w[s][0:I1, B13 + o:B13 + o + 1], h3[:, o, :], ALU.add, ALU.mult
                                                   ).then_inc(prod_ready, 1)
                dve.wait_ge(prod_ready, 2 * ch + 2)
                wait_reuse(dve, sg_ready, ch)
                nc.vector.tensor_scalar(xg[:], prod[:, 0, :], LIMIT, None, ALU.min).then_inc(xg_ready, 1)
                nc.vector.tensor_scalar(xl[:], prod[:, 1, :], -LIMIT, LIMIT, ALU.max, ALU.min).then_inc(xl_ready, 1)
                dve.wait_ge(xg_ready, ch + 1)
                dve.wait_ge(xl_ready, ch + 1)
                nc.vector.scalar_tensor_tensor(lin[:], xl[:], 1.0, xg[:], ALU.add, ALU.mult).then_inc(lin_ready, 1)
                dve.wait_ge(lin_ready, ch + 1)
                dve.wait_ge(sg_ready, ch + 1)
                wait_reuse(dve, second_done, ch - 1)
                nc.vector.tensor_tensor(act_t[s % 2][0:I1, :], lin[:], sg[:], ALU.mult).then_inc(act_ready, 1)

            def step(i, s):
                ch = SL * i + s
                dve.wait_ge(x_in[s], 32 * i + 32)
                for a in range(2):
                    nc.vector.tensor_tensor(picked[:, a, :], x[s][a][:, D:D + E],
                                            chosen[:, bass.ds(ch, 1), :].rearrange("p a e -> p (a e)"), ALU.mult
                                            ).then_inc(picked_ready, 1)
                dve.wait_ge(picked_ready, 2 * ch + 2)
                nc.vector.reduce_sum(gate_s[s][:], picked[:], AX).then_inc(gate_ready, 1)
                nxt = ahead(i, s, 1)
                if nxt:
                    swiglu(*nxt)
                dve.wait_ge(gate_ready, ch + 1)
                dve.wait_ge(second_done, ch + 1)
                for a in range(2):
                    v = nc.vector.tensor_scalar(y[s][a][:], p_y[:, s % 2, a * D:(a + 1) * D], gate_s[s][:, a:a + 1],
                                                None,
                                                ALU.mult)
                v.then_inc(y_ready, 1)
                nxt = ahead(i, s, SL - 1)
                if nxt:
                    indices(*nxt)

            for s in range(SL - 1):
                indices(0, s)
            swiglu(0, 0)
            in_rounds(dve, step)

        @block.scalar
        def _(act):
            def copy_xt(i, s):
                act.wait_ge(turned, SL * i + s + 1)
                nc.scalar.copy(xt[s % 2][:], p_xt).then_inc(xt_copied, 1)

            def step(i, s):
                ch = SL * i + s
                act.wait_ge(w_in[s], 16 * i + 16)
                act.wait_ge(h3_done, ch + 1)
                wait_reuse(act, prod_ready, 2 * ch)
                for o in range(2):
                    nc.scalar.activation(h3[:, o, :], p_h[0:I1, s % 2, 2 + o, :], ACT.Identity,
                                         bias=w[s][0:I1, B13 + 2 + o:B13 + 3 + o]).then_inc(h3_copied, 1)
                nxt = ahead(i, s, 1)
                if nxt:
                    copy_xt(*nxt)
                act.wait_ge(xg_ready, ch + 1)
                wait_reuse(act, act_ready, ch)
                nc.scalar.activation(sg[:], xg[:], ACT.Sigmoid, scale=ALPHA).then_inc(sg_ready, 1)

            copy_xt(0, 0)
            in_rounds(act, step)

        @block.tensor
        def _(pe):
            def turn(i, s):
                pe.wait_ge(x_in[s], 32 * i + 32)
                wait_reuse(pe, xt_copied, SL * i + s)
                for a in range(2):
                    for g in range(G):
                        mm = nc.tensor.transpose(p_xt[:, g, a * 128:(a + 1) * 128], x[s][a][:, g * GF:(g + 1) * GF],
                                                 t["ident"][:])
                mm.then_inc(turned, 1)

            def first(i, s):
                ch = SL * i + s
                pe.wait_ge(xt_copied, ch + 1)
                pe.wait_ge(w_in[s], 16 * i + 16)
                for half, done in ((2, h3_done), (0, h1_done)):
                    if half == 2:
                        wait_reuse(pe, h3_copied, 2 * (ch - 1))
                    else:
                        wait_reuse(pe, prod_ready, 2 * (ch - 1))
                    for o in range(half, half + 2):
                        for g in range(G):
                            mm = nc.tensor.matmul(p_h[0:I1, s % 2, o, :],
                                                  w[s][0:GF, (g * 4 + o) * I1:(g * 4 + o + 1) * I1],
                                                  xt[s % 2][:, g, :], start=(g == 0), stop=(g == G - 1),
                                                  skip_group_check=True)
                    mm.then_inc(done, 1)

            def second(i, s):
                ch = SL * i + s
                wait_reuse(pe, y_ready, ch - 1)
                pe.wait_ge(act_ready, ch + 1)
                for a in range(2):
                    mm = nc.tensor.matmul(p_y[:, s % 2, a * D:(a + 1) * D], act_t[s % 2][:, a * 128:(a + 1) * 128],
                                          w[s][:, W2:W2 + D], start=True, stop=True)
                mm.then_inc(second_done, 1)

            def step(i, s):
                nxt = ahead(i, s, 1)
                if nxt:
                    first(*nxt)
                second(i, s)
                nxt = ahead(i, s, 2)
                if nxt:
                    turn(*nxt)

            pe.wait_ge(one_ready, 3)
            turn(0, 0)
            first(0, 0)
            turn(0, 1)
            in_rounds(pe, step)


@stage
def build_shared(nc, c, t, h_acc, h_out):
    with ExitStack() as ctx:
        def sb(name, shape):
            return ctx.enter_context(nc.sbuf_tensor("sh_" + name, shape, F32))

        def sem(name):
            return nc.alloc_semaphore(name="sh_" + name)

        ALPHA, LIMIT = 1.702, 7.0
        N = CH * 128
        xt = t["xt"]
        h = sb("h", [128, NTILE, D])
        w13 = sb("w13", [GF, G, 4, I1])
        w2 = sb("w2", [I1 + 1, D])
        b13 = sb("b13", [I1, 4])
        h3 = sb("h3", [I1, 2, N])
        prod = sb("prod", [I1, 2, N])
        lin = sb("lin", [I1, N])
        xg = sb("xg", [I1, N])
        sg = sb("sg", [I1, N])
        xl = sb("xl", [I1, N])
        act_t = sb("act_t", [I1 + 1, N])
        p_h = ctx.enter_context(nc.psum_tensor("sh_p_h", [128, 4, 512], F32))
        p_y = ctx.enter_context(nc.psum_tensor("sh_p_y", [128, 2, 512], F32))

        w_in = sem("w_in")
        one_ready = sem("one_ready")
        h_in = sem("h_in")
        h3_done = sem("h3_done")
        h1_done = sem("h1_done")
        h3_copied = sem("h3_copied")
        prod_ready = sem("prod_ready")
        xg_ready = sem("xg_ready")
        sg_ready = sem("sg_ready")
        xl_ready = sem("xl_ready")
        lin_ready = sem("lin_ready")
        act_ready = sem("act_ready")
        second_done = sem("second_done")
        added = sem("added")
        stored = sem("stored")
        block = ctx.enter_context(nc.Block())

        @block.sync
        def _(sp):
            for dst, src in ((w13[:], c["shared_w13"]), (w2[:], c["shared_w2"]), (b13[:], c["shared_b13"])):
                sp.dma_start(dst, src).then_inc(w_in, 16)

            def load(i, n):
                wait_reuse(sp, h_in, 16 * i)
                sp.dma_start(h[:, bass.ds(i * CH, n), :],
                             h_acc[0:S, :].rearrange("(t p) f -> p t f", p=128)[:, bass.ds(i * CH, n), :]
                             ).then_inc(h_in, 16)

            def store(i, n):
                sp.wait_ge(added, i + 1)
                sp.dma_start(h_out.rearrange("(t p) f -> p t f", p=128)[:, bass.ds(i * CH, n), :],
                             h[:, bass.ds(i * CH, n), :]).then_inc(stored, 16)

            over_chunks(sp, load)
            over_chunks(sp, store)
            sp.wait_ge(stored, 16 * (NCH + 1))

        @block.gpsimd
        def _(pool):
            nc.gpsimd.memset(act_t[I1:I1 + 1, :], 1.0).then_inc(one_ready, 1)

        @block.scalar
        def _(act):
            act.wait_ge(w_in, 48)

            def step(i, n):
                w = n * 128
                act.wait_ge(h3_done, i + 1)
                wait_reuse(act, prod_ready, 2 * i)
                for o in range(2):
                    nc.scalar.activation(h3[:, o, 0:w], p_h[0:I1, 2 + o, 0:w], ACT.Identity,
                                         bias=b13[:, 2 + o:3 + o]).then_inc(h3_copied, 1)
                act.wait_ge(xg_ready, i + 1)
                wait_reuse(act, act_ready, i)
                nc.scalar.activation(sg[:, 0:w], xg[:, 0:w], ACT.Sigmoid, scale=ALPHA).then_inc(sg_ready, 1)

            over_chunks(act, step)

        @block.vector
        def _(dve):
            dve.wait_ge(w_in, 48)

            def step(i, n):
                w = n * 128
                dve.wait_ge(h1_done, i + 1)
                dve.wait_ge(h3_copied, 2 * i + 2)
                for o in range(2):
                    nc.vector.scalar_tensor_tensor(prod[:, o, 0:w], p_h[0:I1, o, 0:w], b13[:, o:o + 1],
                                                   h3[:, o, 0:w], ALU.add, ALU.mult).then_inc(prod_ready, 1)
                dve.wait_ge(prod_ready, 2 * i + 2)
                wait_reuse(dve, sg_ready, i)
                nc.vector.tensor_scalar(xg[:, 0:w], prod[:, 0, 0:w], LIMIT, None, ALU.min).then_inc(xg_ready, 1)
                nc.vector.tensor_scalar(xl[:, 0:w], prod[:, 1, 0:w], -LIMIT, LIMIT, ALU.max, ALU.min
                                        ).then_inc(xl_ready, 1)
                dve.wait_ge(xl_ready, i + 1)
                dve.wait_ge(xg_ready, i + 1)
                nc.vector.scalar_tensor_tensor(lin[:, 0:w], xl[:, 0:w], 1.0, xg[:, 0:w], ALU.add, ALU.mult
                                               ).then_inc(lin_ready, 1)
                dve.wait_ge(lin_ready, i + 1)
                dve.wait_ge(sg_ready, i + 1)
                wait_reuse(dve, second_done, i)
                nc.vector.tensor_tensor(act_t[0:I1, 0:w], lin[:, 0:w], sg[:, 0:w], ALU.mult).then_inc(act_ready, 1)
                dve.wait_ge(h_in, 16 * i + 16)
                dve.wait_ge(second_done, i + 1)
                for a in range(n):
                    at = h[:, bass.ds(i * CH + a, 1), :].rearrange("p a f -> p (a f)")
                    v = nc.vector.tensor_tensor(at, at, p_y[:, a // 2, (a % 2) * D:(a % 2 + 1) * D], ALU.add)
                v.then_inc(added, 1)

            over_chunks(dve, step)

        @block.tensor
        def _(pe):
            pe.wait_ge(w_in, 48)
            pe.wait_ge(one_ready, 1)

            def first(i, n):
                w = n * 128
                for half, done in ((2, h3_done), (0, h1_done)):
                    if half == 2:
                        wait_reuse(pe, h3_copied, 2 * i)
                    else:
                        wait_reuse(pe, prod_ready, 2 * i)
                    for o in range(half, half + 2):
                        for g in range(G):
                            mm = nc.tensor.matmul(p_h[0:I1, o, 0:w], w13[:, g, o, :], xt[:, g, bass.ds(i * N, w)],
                                                  start=(g == 0), stop=(g == G - 1))
                    mm.then_inc(done, 1)

            def second(i, n):
                pe.wait_ge(act_ready, i + 1)
                wait_reuse(pe, added, i)
                for a in range(n):
                    mm = nc.tensor.matmul(p_y[:, a // 2, (a % 2) * D:(a % 2 + 1) * D], act_t[:, a * 128:(a + 1) * 128],
                                          w2[:], start=True, stop=True)
                mm.then_inc(second_done, 1)

            first(0, CH)
            first(1, CH)
            second(0, CH)
            with pe.Fori(1, NCH - 1) as i:
                first(i + 1, CH)
                second(i, CH)
            first(NCH, NTILE - NCH * CH)
            second(NCH - 1, CH)
            second(NCH, NTILE - NCH * CH)


def build_moe(nc, layer, h_in, h_out, c):
    ne = (E0, E1)[layer]
    n_gate = 8
    rows = nc.dram_tensor(f"rows{layer}", (S + 256, D + ne), F32, kind="Internal").ap()
    h_acc = h_out if layer == 0 else nc.dram_tensor("h_acc1", (S + 256, D), F32, kind="Internal").ap()
    with ExitStack() as ctx:
        def sb(name, shape, dt=F32):
            return ctx.enter_context(nc.sbuf_tensor(f"f{layer}_{name}", shape, dt))

        t = {"ident": sb("ident", [128, 128]), "table": sb("table", [128, NCHK, 4], I32),
             "chosen": sb("chosen", [128, NCHK, 8])}
        if layer == 1:
            t["xt"] = sb("xt", [GF, G, S])
        with ExitStack() as routing:
            def sb(name, shape):
                return routing.enter_context(nc.sbuf_tensor(f"f{layer}_{name}", shape, F32))

            t.update(h=sb("h", [128, NTILE, D]), logits=sb("logits", [128, NTILE, n_gate]),
                     rows=sb("rows", [128, NTILE, D + ne]))
            t["gate"] = t["rows"][:, :, D:D + ne]
            build_norm(nc, f"n{layer}_", h_in, c["ident"], c["gate_w"], t, n_gate)
            (build_gate0, build_gate1)[layer](nc, c, t)
            build_dispatch(nc, f"d{layer}_", (128, I1 + 1)[layer], (E0, 2)[layer], c, t, h_acc, rows)
        (build_sparse0, build_sparse1)[layer](nc, c, t, rows, h_acc)
        if layer == 1:
            build_shared(nc, c, t, h_acc, h_out)



CIN = 3
PP = 256
R = 5
VOCAB = 8000
NSEG = 3
KI = CIN * PP // 128
BI = 3
IT = [(3 * i, min(BI, B - 3 * i)) for i in range(-(-B // BI))]
TB = 4


@stage
def build_embed(nc, h_out, c, token_table):
    with ExitStack() as ctx:
        def sb(name, shape, dt=F32):
            return ctx.enter_context(nc.sbuf_tensor("em_" + name, shape, dt))

        def sem(name):
            return nc.alloc_semaphore(name="em_" + name)

        pix = sb("pix", [128, KI, B * NI])
        wp = sb("wp", [128, 2, R, D])
        w_repr = sb("w_repr", [128, CIN * R])
        b_repr = sb("b_repr", [128, R])
        b_proj = sb("b_proj", [R, D])
        ones = sb("ones", [128, 128])
        mixed = sb("mixed", [128, CIN + 1, 2, D])
        pos = sb("pos", [NT, D])
        ids = [sb(f"ids{k}", [NT, B], I32) for k in range(2)]
        below = [sb(f"below{k}", [NT, B]) for k in range(2)]
        row = [sb(f"row{k}", [NT, B], I32) for k in range(2)]
        tok = sb("tok", [NT, B, D])
        seg_pos = sb("seg_pos", [NT, NSEG, D])
        is_seg = sb("is_seg", [NT, NSEG, B])
        img = [sb(f"img{i}", [128, D]) for i in range(2)]
        p_i = ctx.enter_context(nc.psum_tensor("em_p_i", [128, 2, 512], F32))

        pix_in = [sem(f"pix_in{k}") for k in range(KI)]
        w_in = sem("w_in")
        ids_in = sem("ids_in")
        pos_in = sem("pos_in")
        ones_ready = sem("ones_ready")
        mixing = sem("mixing")
        below_ready = sem("below_ready")
        wrapped = sem("wrapped")
        rows_ready = sem("rows_ready")
        gathered = [sem(f"gathered{i}") for i in range(B // TB)]
        masks_ready = sem("masks_ready")
        with_pos = sem("with_pos")
        seg_added = sem("seg_added")
        text_ready = sem("text_ready")
        image_done = sem("image_done")
        image_copied = sem("image_copied")
        image_stored = [sem(f"image_stored{i}") for i in range(2)]
        text_stored = sem("text_stored")
        h3 = h_out.rearrange("(b t) f -> b t f", t=T)
        block = ctx.enter_context(nc.Block())

        @block.sync
        def _(sp):
            for k in range(2):
                sp.dma_start(ids[k][:], c["ids"][k]).then_inc(ids_in, 16)
            for dst, src in ((wp[:], c["wp"]), (w_repr[:], c["w_repr"].broadcast_to([128, CIN * R])),
                             (b_repr[:], c["b_repr"].broadcast_to([128, R])), (b_proj[:], c["b_proj"])):
                sp.dma_start(dst, src).then_inc(w_in, 16)
            for k in range(KI):
                sp.dma_start(pix[:, k, :], c["pix"][k]).then_inc(pix_in[k], 16)
            sp.dma_start(pos[:], c["pos"]).then_inc(pos_in, 16)
            sp.dma_start(seg_pos[:].rearrange("p k f -> p (k f)"), c["segm_table"].broadcast_to([NT, NSEG * D])
                         ).then_inc(pos_in, 16)
            for i in range(B // TB):
                sp.wait_ge(text_ready, i + 1)
                sp.dma_start(h3[i * TB:(i + 1) * TB, NI:T, :].rearrange("b t f -> t b f"),
                             tok[:, i * TB:(i + 1) * TB, :]).then_inc(text_stored, 16)
            sp.wait_ge(text_stored, 16 * (B // TB))

        @block.gpsimd
        def _(pool):
            nc.gpsimd.memset(ones[:], 1.0).then_inc(ones_ready, 1)
            pool.wait_ge(rows_ready, 2)
            for b in range(B):
                nc.gpsimd.indirect_dma_start(
                    tok[:, b, :], None, token_table[:, :], bass.IndirectOffsetOnAxis(ap=row[0][:, b:b + 1], axis=0)
                ).then_inc(gathered[b // TB], 16)

        @block.vector
        def _(dve):
            dve.wait_ge(ids_in, 32)
            for k, n in enumerate((VOCAB, NSEG)):
                nc.vector.tensor_scalar(below[k][:], ids[k][:], 0.0, float(n), ALU.is_lt, ALU.mult
                                        ).then_inc(below_ready, 1)
            dve.wait_ge(below_ready, 2)
            for k in range(2):
                nc.vector.tensor_tensor(below[k][:], below[k][:], ids[k][:], ALU.add).then_inc(wrapped, 1)
            dve.wait_ge(wrapped, 2)
            for k, n in enumerate((VOCAB, NSEG)):
                nc.vector.tensor_scalar(row[k][:], below[k][:], 0.0, float(n - 1), ALU.max, ALU.min
                                        ).then_inc(rows_ready, 1)
            dve.wait_ge(w_in, 64)
            for r in range(R):
                if r > 0:
                    dve.wait_ge(mixing, (CIN + 1) * r)
                for ch in range(CIN + 1):
                    by = w_repr[:, ch * R + r:ch * R + r + 1] if ch < CIN else b_repr[:, r:r + 1]
                    if r == 0:
                        nc.vector.tensor_scalar(mixed[:, ch, :, :], wp[:, :, r, :], by, None, ALU.mult
                                                ).then_inc(mixing, 1)
                    else:
                        nc.vector.scalar_tensor_tensor(mixed[:, ch, :, :], wp[:, :, r, :], by, mixed[:, ch, :, :],
                                                       ALU.mult, ALU.add).then_inc(mixing, 1)
            dve.wait_ge(pos_in, 32)
            dve.wait_ge(rows_ready, 2)
            nc.vector.tensor_tensor(seg_pos[:], seg_pos[:], pos[:].unsqueeze(1).broadcast_to([NT, NSEG, D]), ALU.add
                                    ).then_inc(with_pos, 1)
            for k in range(NSEG):
                nc.vector.tensor_scalar(is_seg[:, k, :], row[1][:], float(k), None, ALU.is_equal
                                        ).then_inc(masks_ready, 1)
            dve.wait_ge(with_pos, 1)
            dve.wait_ge(masks_ready, NSEG)
            for i in range(B // TB):
                dve.wait_ge(gathered[i], 16 * TB)
                for k in range(NSEG):
                    if k > 0:
                        dve.wait_ge(seg_added, (NSEG - 1) * i + k)
                    for b in range(i * TB, (i + 1) * TB):
                        v = nc.vector.scalar_tensor_tensor(tok[:, b, :], seg_pos[:, k, :], is_seg[:, k, b:b + 1],
                                                           tok[:, b, :], ALU.mult, ALU.add)
                    v.then_inc(seg_added if k < NSEG - 1 else text_ready, 1)

        @block.tensor
        def _(pe):
            pe.wait_ge(mixing, (CIN + 1) * R)
            pe.wait_ge(ones_ready, 1)
            for k in range(KI):
                pe.wait_ge(pix_in[k], 16)
            for i, (b0, nb) in enumerate(IT):
                if i >= 2:
                    wait_reuse(pe, image_copied, i - 1)
                out = p_i[0:nb * NI, i % 2, 0:D]
                for k in range(KI):
                    nc.tensor.matmul(out, pix[:, k, b0 * NI:(b0 + nb) * NI], mixed[:, k // 2, k % 2, :],
                                     start=(k == 0), stop=False)
                for k in range(2):
                    nc.tensor.matmul(out, ones[:, 0:nb * NI], mixed[:, CIN, k, :], start=False, stop=False)
                nc.tensor.matmul(out, ones[0:R, 0:nb * NI], b_proj[:], start=False, stop=True
                                 ).then_inc(image_done, 1)

        @block.scalar
        def _(act):
            for i, (b0, nb) in enumerate(IT):
                act.wait_ge(image_done, i + 1)
                if i >= 2:
                    act.wait_ge(image_stored[i % 2], 16 * sum(n for _, n in IT[i % 2:i:2]))
                nc.scalar.copy(img[i % 2][0:nb * NI, :], p_i[0:nb * NI, i % 2, 0:D]).then_inc(image_copied, 1)
                act.wait_ge(image_copied, i + 1)
                for b in range(nb):
                    act.dma_start(h3[b0 + b, 0:NI, :], img[i % 2][b * NI:(b + 1) * NI, :]
                                  ).then_inc(image_stored[i % 2], 16)
            for i in range(2):
                act.wait_ge(image_stored[i], 16 * sum(n for _, n in IT[i::2]))


def build(nc, a, out):
    def of(stage):
        return {k[3:]: v for k, v in a.items() if k[:3] == stage}

    h = [nc.dram_tensor(f"h{i}", (S + 256 * (i == 2), D), F32, kind="Internal").ap() for i in range(4)]
    build_embed(nc, h[0], of("em_"), a["em_token_table"])
    build_attention0(nc, h[0], h[1], of("a0_"))
    build_moe(nc, 0, h[1], h[2], of("f0_"))
    build_attention1(nc, h[2], h[3], of("a1_"))
    build_moe(nc, 1, h[3], out, of("f1_"))



def by_groups(w):
    return np.ascontiguousarray(w.reshape(G, GF, -1).transpose(1, 0, 2))


def layout(x):
    c = {}
    f32 = np.float32
    ident = np.eye(128, dtype=f32)
    f = np.arange(GF)
    head_mask = (f[:, None] // HS == np.arange(HG)).astype(f32)

    side = x["x"].shape[-1] // 16
    pix = x["x"].reshape(B, CIN, side, 16, side, 16).transpose(1, 3, 5, 0, 2, 4)
    c["em_pix"] = pix.reshape(KI, 128, B * NI)
    c["em_wp"] = x["L0_tok_W_proj"].reshape(R, D, 2, 128).transpose(3, 2, 0, 1)
    c["em_w_repr"] = x["L0_tok_W_repr"].T.reshape(1, CIN * R)
    c["em_b_repr"] = x["L0_tok_b_repr"][None]
    c["em_b_proj"] = x["L0_tok_b_proj"]
    c["em_ids"] = np.stack([x["x_txt"].T, x["mask_BS_i2_0"].T])
    c["em_token_table"] = x["L0_txt_token_table"]
    c["em_segm_table"] = x["L0_txt_segm_table"].reshape(1, NSEG * D)
    even = (np.arange(D) // 2 * 2).astype(f32) / f32(D)
    angle = np.arange(NT, dtype=f32)[:, None] / np.power(f32(10000.0), even)[None, :]
    c["em_pos"] = np.where(np.arange(D) % 2 == 0, np.sin(angle), np.cos(angle)).astype(f32)

    c["a0_ident"] = ident
    c["a0_wqkv"] = by_groups(x["L0_attn_Wqkv"].T)
    c["a0_wproj"] = by_groups(x["L0_attn_Wproj"].T)
    c["a0_wv"] = np.ascontiguousarray(x["L0_attn_Wv"].T.reshape(2, 128, HS).transpose(1, 0, 2))
    c["a0_bv"] = np.tile(x["L0_attn_bv"], HG)[:, None]
    col = np.arange(128)
    spread = np.zeros((GF, HG, 3, 128), f32)
    for h in range(HG):
        for a in range(2):
            spread[h * HS + a * 8 + col // HS, h, a, col] = 1
        spread[h * HS + col % HS, h, 2, col] = 1
    c["a0_spread"] = spread
    c["a0_reset"] = np.broadcast_to((np.arange(T) % LMIN != 0).astype(f32), (GF, T))
    c["a0_head_mask"] = head_mask
    tail_rows = np.zeros((HG, NC, GF), f32)
    tail_rows[:, NS, :] = head_mask.T
    c["a0_tail_rows"] = tail_rows.reshape(NG, GF)
    tok = np.arange(TR)[:, None, None] + np.array(T0)[None, :, None]
    last = np.array([r for _, r in SETS] + [-1])
    c["a0_set_mask"] = np.where(tok >= last, 0, -1e30).astype(f32)

    c["a1_ident"] = ident
    c["a1_wqk"] = by_groups(np.concatenate([x["L1_attn_Wq"], x["L1_attn_Wk"]], axis=1))
    c["a1_wv"] = by_groups(x["L1_attn_Wv"])
    c["a1_wo"] = by_groups(x["L1_attn_Wo"])
    c["a1_bqk"] = np.concatenate([x["L1_attn_bq"].reshape(G, GF), x["L1_attn_bk"].reshape(G, GF)]).T
    c["a1_bv"] = x["L1_attn_bv"][None]
    c["a1_bo"] = x["L1_attn_bo"][None]
    c["a1_spread"] = spread[:, :, 2, :]
    c["a1_query_mask"] = (col[:, None] // HS == np.arange(TP) % QB).astype(f32)
    c["a1_head_mask"] = head_mask
    far = x["L1_attn_rel_emb"].shape[0] // 2
    offset = np.arange(QB)[:, None] - (np.arange(REL_W) - (REL_W - T))
    c["a1_rel"] = x["L1_attn_rel_emb"][np.clip(offset, -far, far) + far].transpose(0, 2, 1).reshape(128, REL_W)

    c["f0_ident"] = ident
    c["f0_gate_w"] = by_groups(x["L0_ffn_gate_weight"].T)
    pairs = (4 ** np.arange(14, -1, -1)[:, None] * np.arange(1, 4)).reshape(-1)
    c["f0_bits"] = np.broadcast_to(pairs.astype(np.int32), (128, len(pairs)))
    c["f0_bits_f"] = np.broadcast_to(pairs.astype(f32), (128, len(pairs)))
    c["f0_ones"] = np.ones((128, 128), f32)
    c["f0_w1"] = x["L0_ffn_w1"].reshape(E0, G, GF, H0).transpose(0, 2, 1, 3).reshape(E0 * GF, G * H0)
    w2 = x["L0_ffn_w2"].reshape(E0, M0, 128, D).transpose(0, 2, 1, 3).reshape(E0 * 128, M0 * D)
    b1 = x["L0_ffn_b1"].reshape(E0, M0, 128).transpose(0, 2, 1).reshape(E0 * 128, M0)
    c["f0_w2"] = np.concatenate([w2, b1, np.repeat(x["L0_ffn_b2"], 128, axis=0)], axis=1)

    slot_tile = np.arange(SLOTS)
    for f in ("f0_", "f1_"):
        c[f + "lower"] = np.triu(np.ones((128, 128), f32), 1)
        c[f + "iota"] = np.broadcast_to(np.arange(128, dtype=f32), (128, 128))
        c[f + "part"] = (col[:, None] + np.arange(2)).astype(f32)
        c[f + "dummy"] = (S + slot_tile % 2 * 128 + col[:, None]).astype(f32)
        c[f + "starts"] = np.broadcast_to(np.arange(MAX_CH, dtype=f32) * PC, (128, MAX_CH))

    w1, w3, w2, b1, b3, b2 = (np.concatenate([x["L1_ffn_" + a], x["L1_ffn_" + s][None]])
                              for a, s in (("W1", "Ws1"), ("W3", "Ws3"), ("W2", "Ws2"),
                                           ("B1", "Bs1"), ("B3", "Bs3"), ("B2", "Bs2")))
    c["f1_ident"] = ident
    c["f1_gate_w"] = by_groups(x["L1_ffn_gate_w"].T)
    c["f1_gate_b"] = x["L1_ffn_gate_b"][None]
    n = E1 - 1
    c["f1_earlier"] = np.broadcast_to(np.tril(np.ones((n, n), f32), -1), (128, n, n))
    w = np.stack([w1, w3]).reshape(2, E1, G, GF, I1, 2)
    w13 = w.transpose(1, 3, 2, 0, 5, 4).reshape(E1, GF, G * 4 * I1)
    b13 = np.stack([b1, b3]).reshape(2, E1, I1, 2).transpose(1, 2, 0, 3).reshape(E1, I1, 4)
    w2 = np.concatenate([w2, b2[:, None, :]], axis=1)
    packed = np.zeros((n, I1 + 1, G * 4 * I1 + D + 4), f32)
    packed[:, 0:GF, 0:G * 4 * I1] = w13[:n]
    packed[:, :, G * 4 * I1:-4] = w2[:n]
    packed[:, 0:I1, -4:] = b13[:n]
    c["f1_w"] = packed.reshape(n * (I1 + 1), -1)
    c["f1_shared_w13"] = w13[n].reshape(GF, G, 4, I1)
    c["f1_shared_w2"] = w2[n]
    c["f1_shared_b13"] = b13[n]
    return c


def kernel(**inputs):
    from concourse import bacc
    from concourse.bass_utils import run_bass_kernel_spmd

    nc = bacc.Bacc("TRN2", target_bir_lowering=False, num_devices=1)
    arrays, a = {}, {}
    for name, array in layout({k: np.asarray(v) for k, v in inputs.items()}).items():
        arrays["in_" + name] = np.ascontiguousarray(array)
        a[name] = nc.dram_tensor("in_" + name, array.shape, mybir.dt.from_np(array.dtype), kind="ExternalInput").ap()
    out = nc.dram_tensor("out", (S, D), F32, kind="ExternalOutput").ap()
    build(nc, a, out)
    r = run_bass_kernel_spmd(nc, [arrays], core_ids=[0])
    return r.results[0]["out"].reshape(B, T, D)
```
